# Optimizing a Trainium2 kernel written in Bass

```python
import numpy as np
import jax
import jax.numpy as jnp

def _softmax(x, axis=-1):
    return jax.nn.softmax(x, axis=axis)

def _gelu(x):
    return jax.nn.gelu(x, approximate=True)

def _silu(x):
    return jax.nn.silu(x)

def _sigmoid(x):
    return jax.nn.sigmoid(x)

def _layernorm(x, axis=-1, eps=1e-05):
    m = jnp.mean(x, axis=axis, keepdims=True)
    v = jnp.var(x, axis=axis, keepdims=True)
    return (x - m) / jnp.sqrt(v + eps)

def _scatter_add(tgt, idx, src, axis=0):
    return tgt.at[idx].add(src)

def _segment_sum(src, seg, n):
    return jax.ops.segment_sum(src, seg, n)
kernel_name = 'mk_seq_postln_d2_jaxref_r8_107ed4'

def setup_inputs(seed: int=0):
    np.random.seed(seed)
    _w = jnp.asarray

    def _L0_attn_setup():
        import jax, jax.numpy as jnp
        import numpy as np
        D_MODEL = 128
        N_HEADS = 16
        B, T = (4, 256)
        key = jax.random.key(seed)
        ks = jax.random.split(key, 5)
        s_in = 1.0 / np.sqrt(D_MODEL)
        x = jax.random.normal(ks[0], (B, T, D_MODEL), dtype=jnp.float32)
        W_qkv = jax.random.uniform(ks[1], (D_MODEL, 3 * D_MODEL), jnp.float32, -s_in, s_in)
        b_qkv = jax.random.uniform(ks[2], (3 * D_MODEL,), jnp.float32, -s_in, s_in)
        W_proj = jax.random.uniform(ks[3], (D_MODEL, D_MODEL), jnp.float32, -s_in, s_in)
        b_proj = jax.random.uniform(ks[4], (D_MODEL,), jnp.float32, -s_in, s_in)
        return {'x': x, 'W_qkv': W_qkv, 'b_qkv': b_qkv, 'W_proj': W_proj, 'b_proj': b_proj}
    _L0_attn_in = _L0_attn_setup()

    def _L0_ffn_setup():
        import jax, jax.numpy as jnp
        import numpy as np
        D = 128
        LW = 16
        DEPTH = 8
        NN = 2 ** DEPTH - 1
        NL = 2 ** DEPTH
        B, S = (2, 128)

        def _fff(x, nw, nb, w1, b1, w2, b2, act):
            node = jnp.zeros(x.shape[:2], dtype=jnp.int32)
            for _ in range(DEPTH):
                logit = jnp.einsum('bsd,bsd->bs', x, nw[node]) + nb[node]
                node = 2 * node + 1 + (logit > 0).astype(jnp.int32)
            leaf = node - NN
            h = act(jnp.einsum('bsd,bsdl->bsl', x, w1[leaf]) + b1[leaf])
            return jnp.einsum('bsl,bsld->bsd', h, w2[leaf]) + b2[leaf]

        def _forward(x, q_nw, q_nb, q_w1, q_b1, q_w2, q_b2, k_nw, k_nb, k_w1, k_b1, k_w2, k_b2, v_nw, v_nb, v_w1, v_b1, v_w2, v_b2, f_nw, f_nb, f_w1, f_b1, f_w2, f_b2):
            mu = jnp.mean(x, -1, keepdims=True)
            sd = jnp.std(x, -1, ddof=1, keepdims=True)
            xn = (x - mu) / jnp.sqrt(sd + 1e-05)
            relu = jax.nn.relu
            q = _fff(xn, q_nw, q_nb, q_w1, q_b1, q_w2, q_b2, relu)
            k = _fff(xn, k_nw, k_nb, k_w1, k_b1, k_w2, k_b2, relu)
            v = _fff(xn, v_nw, v_nb, v_w1, v_b1, v_w2, v_b2, relu)
            att = jax.nn.softmax(jnp.einsum('bqd,bkd->bqk', q, k) / jnp.sqrt(jnp.float32(D)), axis=-1)
            y = xn + jnp.einsum('bqk,bkd->bqd', att, v)
            gelu = lambda t: jax.nn.gelu(t, approximate=False)
            return y + _fff(y, f_nw, f_nb, f_w1, f_b1, f_w2, f_b2, gelu)

        def _make_fff_params(key, scale_in, scale_leaf):
            ks = jax.random.split(key, 4)
            nw = jax.random.normal(ks[0], (NN, D), jnp.float32) * scale_in
            nb = jnp.zeros((NN,), jnp.float32)
            w1 = jax.random.normal(ks[1], (NL, D, LW), jnp.float32) * scale_in
            b1 = jax.random.normal(ks[2], (NL, LW), jnp.float32) * 0.01
            w2 = jax.random.normal(ks[3], (NL, LW, D), jnp.float32) * scale_leaf
            b2 = jnp.zeros((NL, D), jnp.float32)
            return (nw, nb, w1, b1, w2, b2)
        key = jax.random.key(seed)
        kx, kq, kk, kv, kf = jax.random.split(key, 5)
        s_in = 1.0 / np.sqrt(D)
        s_lf = 1.0 / np.sqrt(LW)
        inp = {'x': jax.random.normal(kx, (B, S, D), jnp.float32)}
        for name, kk_ in (('q', kq), ('k', kk), ('v', kv), ('f', kf)):
            nw, nb, w1, b1, w2, b2 = _make_fff_params(kk_, s_in, s_lf)
            inp.update({f'{name}_nw': nw, f'{name}_nb': nb, f'{name}_w1': w1, f'{name}_b1': b1, f'{name}_w2': w2, f'{name}_b2': b2})
        return inp
    _L0_ffn_in = _L0_ffn_setup()

    def _L1_attn_setup():
        import jax, jax.numpy as jnp
        import numpy as np
        B, S, D = (4, 512, 128)

        def _scan_causal(x_scan, a):

            def step(h, inp):
                a_t, x_t = inp
                h = a_t * h + x_t
                return (h, h)
            h0 = jnp.zeros(x_scan.shape[::2], dtype=x_scan.dtype)
            xs = (jnp.swapaxes(a, 0, 1), jnp.swapaxes(x_scan, 0, 1))
            _, out = jax.lax.scan(step, h0, xs)
            return jnp.swapaxes(out, 0, 1)
        key = jax.random.key(seed)
        ks = jax.random.split(key, 4)
        scale = 1.0 / np.sqrt(D)
        x = jax.random.normal(ks[0], (B, S, D), dtype=jnp.float32)
        Wg = jax.random.normal(ks[1], (D, D), dtype=jnp.float32) * scale
        Wv = jax.random.normal(ks[2], (D, D), dtype=jnp.float32) * scale
        Wd = jax.random.normal(ks[3], (D, D), dtype=jnp.float32) * scale
        bg = jnp.zeros((D,), dtype=jnp.float32)
        bv = jnp.zeros((D,), dtype=jnp.float32)
        bd = jnp.ones((D,), dtype=jnp.float32)
        return {'x': x, 'Wg': Wg, 'bg': bg, 'Wv': Wv, 'bv': bv, 'Wd': Wd, 'bd': bd}
    _L1_attn_in = _L1_attn_setup()

    def _L1_ffn_setup():
        import jax, jax.numpy as jnp
        import numpy as np
        DIM = 128
        DEPTH = 6
        HEADS = 16
        DIM_HEAD = 64
        WINDOW = 32
        INNER = HEADS * DIM_HEAD
        DIM_INNER = int(DIM * 4 * 2 / 3)
        QK_SCALE = 8.0

        def shift_tokens(t):
            a, s = jnp.split(t, 2, -1)
            s = jnp.pad(s, ((0, 0), (1, 0), (0, 0)))[:, :-1]
            return jnp.concatenate([a, s], -1)

        def l2norm(t):
            return t / jnp.maximum(jnp.linalg.norm(t, axis=-1, keepdims=True), 1e-12)

        def rotate_half(x):
            x1, x2 = jnp.split(x, 2, -1)
            return jnp.concatenate([-x2, x1], -1)

        def rotary_tables(n):
            half = jnp.arange(0, DIM_HEAD, 2, dtype=jnp.float32)
            inv_freq = 1.0 / 10000.0 ** (half / DIM_HEAD)
            t = jnp.arange(n, dtype=jnp.float32)
            freqs = t[:, None] * inv_freq[None, :]
            freqs = jnp.concatenate([freqs, freqs], -1)
            base_scale = (half + 0.4 * DIM_HEAD) / (1.4 * DIM_HEAD)
            power = (t - n // 2) / (WINDOW // 2)
            scale = base_scale[None, :] ** power[:, None]
            scale = jnp.concatenate([scale, scale], -1)
            return (freqs, scale)

        def local_attention(q, k, v):
            b, h, n, d = q.shape
            w = WINDOW
            nw = n // w
            bq = q.reshape(b, h, nw, w, d)
            bk = k.reshape(b, h, nw, w, d)
            bv = v.reshape(b, h, nw, w, d)

            def look(t):
                p = jnp.pad(t, ((0, 0), (0, 0), (1, 0), (0, 0), (0, 0)))
                return jnp.concatenate([p[:, :, :nw], p[:, :, 1:]], axis=3)
            bk2, bv2 = (look(bk), look(bv))
            seq = jnp.arange(n).reshape(nw, w)
            seq_p = jnp.pad(seq, ((1, 0), (0, 0)), constant_values=-1)
            jt = jnp.concatenate([seq_p[:nw], seq_p[1:]], axis=1)
            it = seq[:, :, None]
            jb = jt[:, None, :]
            mask = (it < jb) | (it > jb + w) | (jb == -1)
            sim = jnp.einsum('bhwie,bhwje->bhwij', bq, bk2) * QK_SCALE
            sim = jnp.where(mask, -jnp.finfo(sim.dtype).max, sim)
            attn = jax.nn.softmax(sim, -1)
            out = jnp.einsum('bhwij,bhwje->bhwie', attn, bv2)
            return out.reshape(b, h, n, d)

        def attn_layer(x, Wqkv, qs, ksc, Wo):
            b, n, _ = x.shape
            qkv = x @ Wqkv
            q, k, v = jnp.split(qkv, 3, -1)
            sh = lambda t: t.reshape(b, n, HEADS, DIM_HEAD).transpose(0, 2, 1, 3)
            q, k, v = (sh(q), sh(k), sh(v))
            q = l2norm(q) * qs
            k = l2norm(k) * ksc
            freqs, scale = rotary_tables(n)
            cos, sin = (jnp.cos(freqs), jnp.sin(freqs))
            q = q * cos * scale + rotate_half(q) * sin * scale
            inv = 1.0 / scale
            k = k * cos * inv + rotate_half(k) * sin * inv
            out = local_attention(q, k, v)
            out = out.transpose(0, 2, 1, 3).reshape(b, n, INNER)
            return out @ Wo

        def ffn_layer(x, g, bln, W1, b1, W2, b2):
            mu = x.mean(-1, keepdims=True)
            var = ((x - mu) ** 2).mean(-1, keepdims=True)
            xn = (x - mu) / jnp.sqrt(var + 1e-05) * g + bln
            hg = xn @ W1 + b1
            a, gate = jnp.split(hg, 2, -1)
            return a * jax.nn.gelu(gate, approximate=False) @ W2 + b2
        key = jax.random.key(seed)
        ks = jax.random.split(key, 8)
        B, N = (2, 256)
        init = lambda k, shape: jax.random.normal(k, shape, jnp.float32) * 0.02
        return {'x': jax.random.normal(ks[0], (B, N, DIM), jnp.float32), 'Wqkv': init(ks[1], (DEPTH, DIM, 3 * INNER)), 'q_scale': jnp.ones((DEPTH, DIM_HEAD), jnp.float32), 'k_scale': jnp.ones((DEPTH, DIM_HEAD), jnp.float32), 'Wo': init(ks[2], (DEPTH, INNER, DIM)), 'ln_g': jnp.ones((DEPTH, DIM), jnp.float32), 'ln_b': jnp.zeros((DEPTH, DIM), jnp.float32), 'W1': init(ks[3], (DEPTH, DIM, 2 * DIM_INNER)), 'b1': jnp.zeros((DEPTH, 2 * DIM_INNER), jnp.float32), 'W2': init(ks[4], (DEPTH, DIM_INNER, DIM)), 'b2': jnp.zeros((DEPTH, DIM), jnp.float32)}
    _L1_ffn_in = _L1_ffn_setup()
    _d = {'L0_attn_x': _L0_attn_in['x'], 'L0_attn_W_qkv': _L0_attn_in['W_qkv'], 'L0_attn_b_qkv': _L0_attn_in['b_qkv'], 'L0_attn_W_proj': _L0_attn_in['W_proj'], 'L0_attn_b_proj': _L0_attn_in['b_proj'], 'L0_ffn_q_nw': _L0_ffn_in['q_nw'], 'L0_ffn_q_nb': _L0_ffn_in['q_nb'], 'L0_ffn_q_w1': _L0_ffn_in['q_w1'], 'L0_ffn_q_b1': _L0_ffn_in['q_b1'], 'L0_ffn_q_w2': _L0_ffn_in['q_w2'], 'L0_ffn_q_b2': _L0_ffn_in['q_b2'], 'L0_ffn_k_nw': _L0_ffn_in['k_nw'], 'L0_ffn_k_nb': _L0_ffn_in['k_nb'], 'L0_ffn_k_w1': _L0_ffn_in['k_w1'], 'L0_ffn_k_b1': _L0_ffn_in['k_b1'], 'L0_ffn_k_w2': _L0_ffn_in['k_w2'], 'L0_ffn_k_b2': _L0_ffn_in['k_b2'], 'L0_ffn_v_nw': _L0_ffn_in['v_nw'], 'L0_ffn_v_nb': _L0_ffn_in['v_nb'], 'L0_ffn_v_w1': _L0_ffn_in['v_w1'], 'L0_ffn_v_b1': _L0_ffn_in['v_b1'], 'L0_ffn_v_w2': _L0_ffn_in['v_w2'], 'L0_ffn_v_b2': _L0_ffn_in['v_b2'], 'L0_ffn_f_nw': _L0_ffn_in['f_nw'], 'L0_ffn_f_nb': _L0_ffn_in['f_nb'], 'L0_ffn_f_w1': _L0_ffn_in['f_w1'], 'L0_ffn_f_b1': _L0_ffn_in['f_b1'], 'L0_ffn_f_w2': _L0_ffn_in['f_w2'], 'L0_ffn_f_b2': _L0_ffn_in['f_b2'], 'L1_attn_Wg': _L1_attn_in['Wg'], 'L1_attn_bg': _L1_attn_in['bg'], 'L1_attn_Wv': _L1_attn_in['Wv'], 'L1_attn_bv': _L1_attn_in['bv'], 'L1_attn_Wd': _L1_attn_in['Wd'], 'L1_attn_bd': _L1_attn_in['bd'], 'L1_ffn_Wqkv': _L1_ffn_in['Wqkv'], 'L1_ffn_q_scale': _L1_ffn_in['q_scale'], 'L1_ffn_k_scale': _L1_ffn_in['k_scale'], 'L1_ffn_Wo': _L1_ffn_in['Wo'], 'L1_ffn_ln_g': _L1_ffn_in['ln_g'], 'L1_ffn_ln_b': _L1_ffn_in['ln_b'], 'L1_ffn_W1': _L1_ffn_in['W1'], 'L1_ffn_b1': _L1_ffn_in['b1'], 'L1_ffn_W2': _L1_ffn_in['W2'], 'L1_ffn_b2': _L1_ffn_in['b2']}
    _x0 = _d['L0_attn_x']
    _d['L0_attn_x'] = jax.random.normal(jax.random.fold_in(jax.random.key(seed), 1), (16, 256, 128), dtype=_x0.dtype)
    del _x0
    return _d

def reference(L0_attn_x, L0_attn_W_qkv, L0_attn_b_qkv, L0_attn_W_proj, L0_attn_b_proj, L0_ffn_q_nw, L0_ffn_q_nb, L0_ffn_q_w1, L0_ffn_q_b1, L0_ffn_q_w2, L0_ffn_q_b2, L0_ffn_k_nw, L0_ffn_k_nb, L0_ffn_k_w1, L0_ffn_k_b1, L0_ffn_k_w2, L0_ffn_k_b2, L0_ffn_v_nw, L0_ffn_v_nb, L0_ffn_v_w1, L0_ffn_v_b1, L0_ffn_v_w2, L0_ffn_v_b2, L0_ffn_f_nw, L0_ffn_f_nb, L0_ffn_f_w1, L0_ffn_f_b1, L0_ffn_f_w2, L0_ffn_f_b2, L1_attn_Wg, L1_attn_bg, L1_attn_Wv, L1_attn_bv, L1_attn_Wd, L1_attn_bd, L1_ffn_Wqkv, L1_ffn_q_scale, L1_ffn_k_scale, L1_ffn_Wo, L1_ffn_ln_g, L1_ffn_ln_b, L1_ffn_W1, L1_ffn_b1, L1_ffn_W2, L1_ffn_b2):

    def _L0_attn_ref(x, W_qkv, b_qkv, W_proj, b_proj):
        import jax, jax.numpy as jnp
        import numpy as np
        D_MODEL = 128
        N_HEADS = 16
        B, T = (4, 256)
        b, t, c = x.shape
        hd = c // N_HEADS
        qkv = x @ W_qkv + b_qkv
        q, k, v = jnp.split(qkv, 3, axis=2)

        def heads(z):
            return z.reshape(b, t, N_HEADS, hd).transpose(0, 2, 1, 3)
        q, k, v = (heads(q), heads(k), heads(v))
        att = jnp.einsum('bhqd,bhkd->bhqk', q, k) * (1.0 / np.sqrt(hd))
        causal = jnp.tril(jnp.ones((t, t), dtype=bool))
        att = jnp.where(causal, att, -jnp.inf)
        att = jax.nn.softmax(att, axis=-1)
        y = jnp.einsum('bhqk,bhkd->bhqd', att, v)
        y = y.transpose(0, 2, 1, 3).reshape(b, t, c)
        return y @ W_proj + b_proj

    def _L0_ffn_ref(x, q_nw, q_nb, q_w1, q_b1, q_w2, q_b2, k_nw, k_nb, k_w1, k_b1, k_w2, k_b2, v_nw, v_nb, v_w1, v_b1, v_w2, v_b2, f_nw, f_nb, f_w1, f_b1, f_w2, f_b2):
        import jax, jax.numpy as jnp
        import numpy as np
        D = 128
        LW = 16
        DEPTH = 8
        NN = 2 ** DEPTH - 1
        NL = 2 ** DEPTH
        B, S = (2, 128)

        def _fff(x, nw, nb, w1, b1, w2, b2, act):
            node = jnp.zeros(x.shape[:2], dtype=jnp.int32)
            for _ in range(DEPTH):
                logit = jnp.einsum('bsd,bsd->bs', x, nw[node]) + nb[node]
                node = 2 * node + 1 + (logit > 0).astype(jnp.int32)
            leaf = node - NN
            h = act(jnp.einsum('bsd,bsdl->bsl', x, w1[leaf]) + b1[leaf])
            return jnp.einsum('bsl,bsld->bsd', h, w2[leaf]) + b2[leaf]

        def _forward(x, q_nw, q_nb, q_w1, q_b1, q_w2, q_b2, k_nw, k_nb, k_w1, k_b1, k_w2, k_b2, v_nw, v_nb, v_w1, v_b1, v_w2, v_b2, f_nw, f_nb, f_w1, f_b1, f_w2, f_b2):
            mu = jnp.mean(x, -1, keepdims=True)
            sd = jnp.std(x, -1, ddof=1, keepdims=True)
            xn = (x - mu) / jnp.sqrt(sd + 1e-05)
            relu = jax.nn.relu
            q = _fff(xn, q_nw, q_nb, q_w1, q_b1, q_w2, q_b2, relu)
            k = _fff(xn, k_nw, k_nb, k_w1, k_b1, k_w2, k_b2, relu)
            v = _fff(xn, v_nw, v_nb, v_w1, v_b1, v_w2, v_b2, relu)
            att = jax.nn.softmax(jnp.einsum('bqd,bkd->bqk', q, k) / jnp.sqrt(jnp.float32(D)), axis=-1)
            y = xn + jnp.einsum('bqk,bkd->bqd', att, v)
            gelu = lambda t: jax.nn.gelu(t, approximate=False)
            return y + _fff(y, f_nw, f_nb, f_w1, f_b1, f_w2, f_b2, gelu)

        def _make_fff_params(key, scale_in, scale_leaf):
            ks = jax.random.split(key, 4)
            nw = jax.random.normal(ks[0], (NN, D), jnp.float32) * scale_in
            nb = jnp.zeros((NN,), jnp.float32)
            w1 = jax.random.normal(ks[1], (NL, D, LW), jnp.float32) * scale_in
            b1 = jax.random.normal(ks[2], (NL, LW), jnp.float32) * 0.01
            w2 = jax.random.normal(ks[3], (NL, LW, D), jnp.float32) * scale_leaf
            b2 = jnp.zeros((NL, D), jnp.float32)
            return (nw, nb, w1, b1, w2, b2)
        return _forward(x, q_nw, q_nb, q_w1, q_b1, q_w2, q_b2, k_nw, k_nb, k_w1, k_b1, k_w2, k_b2, v_nw, v_nb, v_w1, v_b1, v_w2, v_b2, f_nw, f_nb, f_w1, f_b1, f_w2, f_b2)

    def _L1_attn_ref(x, Wg, bg, Wv, bv, Wd, bd):
        import jax, jax.numpy as jnp
        import numpy as np
        B, S, D = (4, 512, 128)

        def _scan_causal(x_scan, a):

            def step(h, inp):
                a_t, x_t = inp
                h = a_t * h + x_t
                return (h, h)
            h0 = jnp.zeros(x_scan.shape[::2], dtype=x_scan.dtype)
            xs = (jnp.swapaxes(a, 0, 1), jnp.swapaxes(x_scan, 0, 1))
            _, out = jax.lax.scan(step, h0, xs)
            return jnp.swapaxes(out, 0, 1)
        g = jnp.einsum('bsd,ed->bse', x, Wg) + bg
        v = jnp.einsum('bsd,ed->bse', x, Wv) + bv
        d = jnp.einsum('bsd,ed->bse', x, Wd) + bd
        x_scan = jax.nn.sigmoid(g) * jnp.tanh(v)
        a = 0.001 + 0.998 * jax.nn.sigmoid(d)
        return _scan_causal(x_scan, a)

    def _L1_ffn_ref(x, Wqkv, q_scale, k_scale, Wo, ln_g, ln_b, W1, b1, W2, b2):
        import jax, jax.numpy as jnp
        import numpy as np
        DIM = 128
        DEPTH = 6
        HEADS = 16
        DIM_HEAD = 64
        WINDOW = 32
        INNER = HEADS * DIM_HEAD
        DIM_INNER = int(DIM * 4 * 2 / 3)
        QK_SCALE = 8.0

        def shift_tokens(t):
            a, s = jnp.split(t, 2, -1)
            s = jnp.pad(s, ((0, 0), (1, 0), (0, 0)))[:, :-1]
            return jnp.concatenate([a, s], -1)

        def l2norm(t):
            return t / jnp.maximum(jnp.linalg.norm(t, axis=-1, keepdims=True), 1e-12)

        def rotate_half(x):
            x1, x2 = jnp.split(x, 2, -1)
            return jnp.concatenate([-x2, x1], -1)

        def rotary_tables(n):
            half = jnp.arange(0, DIM_HEAD, 2, dtype=jnp.float32)
            inv_freq = 1.0 / 10000.0 ** (half / DIM_HEAD)
            t = jnp.arange(n, dtype=jnp.float32)
            freqs = t[:, None] * inv_freq[None, :]
            freqs = jnp.concatenate([freqs, freqs], -1)
            base_scale = (half + 0.4 * DIM_HEAD) / (1.4 * DIM_HEAD)
            power = (t - n // 2) / (WINDOW // 2)
            scale = base_scale[None, :] ** power[:, None]
            scale = jnp.concatenate([scale, scale], -1)
            return (freqs, scale)

        def local_attention(q, k, v):
            b, h, n, d = q.shape
            w = WINDOW
            nw = n // w
            bq = q.reshape(b, h, nw, w, d)
            bk = k.reshape(b, h, nw, w, d)
            bv = v.reshape(b, h, nw, w, d)

            def look(t):
                p = jnp.pad(t, ((0, 0), (0, 0), (1, 0), (0, 0), (0, 0)))
                return jnp.concatenate([p[:, :, :nw], p[:, :, 1:]], axis=3)
            bk2, bv2 = (look(bk), look(bv))
            seq = jnp.arange(n).reshape(nw, w)
            seq_p = jnp.pad(seq, ((1, 0), (0, 0)), constant_values=-1)
            jt = jnp.concatenate([seq_p[:nw], seq_p[1:]], axis=1)
            it = seq[:, :, None]
            jb = jt[:, None, :]
            mask = (it < jb) | (it > jb + w) | (jb == -1)
            sim = jnp.einsum('bhwie,bhwje->bhwij', bq, bk2) * QK_SCALE
            sim = jnp.where(mask, -jnp.finfo(sim.dtype).max, sim)
            attn = jax.nn.softmax(sim, -1)
            out = jnp.einsum('bhwij,bhwje->bhwie', attn, bv2)
            return out.reshape(b, h, n, d)

        def attn_layer(x, Wqkv, qs, ksc, Wo):
            b, n, _ = x.shape
            qkv = x @ Wqkv
            q, k, v = jnp.split(qkv, 3, -1)
            sh = lambda t: t.reshape(b, n, HEADS, DIM_HEAD).transpose(0, 2, 1, 3)
            q, k, v = (sh(q), sh(k), sh(v))
            q = l2norm(q) * qs
            k = l2norm(k) * ksc
            freqs, scale = rotary_tables(n)
            cos, sin = (jnp.cos(freqs), jnp.sin(freqs))
            q = q * cos * scale + rotate_half(q) * sin * scale
            inv = 1.0 / scale
            k = k * cos * inv + rotate_half(k) * sin * inv
            out = local_attention(q, k, v)
            out = out.transpose(0, 2, 1, 3).reshape(b, n, INNER)
            return out @ Wo

        def ffn_layer(x, g, bln, W1, b1, W2, b2):
            mu = x.mean(-1, keepdims=True)
            var = ((x - mu) ** 2).mean(-1, keepdims=True)
            xn = (x - mu) / jnp.sqrt(var + 1e-05) * g + bln
            hg = xn @ W1 + b1
            a, gate = jnp.split(hg, 2, -1)
            return a * jax.nn.gelu(gate, approximate=False) @ W2 + b2
        for i in range(DEPTH):
            x = attn_layer(shift_tokens(x), Wqkv[i], q_scale[i], k_scale[i], Wo[i]) + x
            x = ffn_layer(shift_tokens(x), ln_g[i], ln_b[i], W1[i], b1[i], W2[i], b2[i]) + x
        return x
    x = L0_attn_x
    x = _layernorm(x + _L0_attn_ref(x, L0_attn_W_qkv, L0_attn_b_qkv, L0_attn_W_proj, L0_attn_b_proj), axis=-1)
    x = _layernorm(x + _L0_ffn_ref(x, L0_ffn_q_nw, L0_ffn_q_nb, L0_ffn_q_w1, L0_ffn_q_b1, L0_ffn_q_w2, L0_ffn_q_b2, L0_ffn_k_nw, L0_ffn_k_nb, L0_ffn_k_w1, L0_ffn_k_b1, L0_ffn_k_w2, L0_ffn_k_b2, L0_ffn_v_nw, L0_ffn_v_nb, L0_ffn_v_w1, L0_ffn_v_b1, L0_ffn_v_w2, L0_ffn_v_b2, L0_ffn_f_nw, L0_ffn_f_nb, L0_ffn_f_w1, L0_ffn_f_b1, L0_ffn_f_w2, L0_ffn_f_b2), axis=-1)
    x = _layernorm(x + _L1_attn_ref(x, L1_attn_Wg, L1_attn_bg, L1_attn_Wv, L1_attn_bv, L1_attn_Wd, L1_attn_bd), axis=-1)
    x = _layernorm(x + _L1_ffn_ref(x, L1_ffn_Wqkv, L1_ffn_q_scale, L1_ffn_k_scale, L1_ffn_Wo, L1_ffn_ln_g, L1_ffn_ln_b, L1_ffn_W1, L1_ffn_b1, L1_ffn_W2, L1_ffn_b2), axis=-1)
    return x

_drawn_inputs = setup_inputs


def setup_inputs(seed=0):
    import zlib

    import numpy as np

    out = dict(_drawn_inputs(seed))
    spreads = {'L0_ffn_q_nb': (0.0, 0.1),
     'L0_ffn_q_b2': (0.0, 0.1),
     'L0_ffn_k_nb': (0.0, 0.1),
     'L0_ffn_k_b2': (0.0, 0.1),
     'L0_ffn_v_nb': (0.0, 0.1),
     'L0_ffn_v_b2': (0.0, 0.1),
     'L0_ffn_f_nb': (0.0, 0.1),
     'L0_ffn_f_b2': (0.0, 0.1),
     'L1_attn_bg': (0.0, 0.443),
     'L1_attn_bv': (0.0, 0.1),
     'L1_attn_bd': (1.0, 0.2),
     'L1_ffn_q_scale': (1.0, 0.6),
     'L1_ffn_k_scale': (1.0, 0.6),
     'L1_ffn_ln_g': (1.0, 0.6),
     'L1_ffn_ln_b': (0.0, 0.8),
     'L1_ffn_b1': (0.0, 0.8),
     'L1_ffn_b2': (0.0, 0.1)}
    factors = {'L0_ffn_q_b1': 7.894,
     'L0_ffn_k_b1': 5.907,
     'L0_ffn_v_b1': 4.079,
     'L0_ffn_f_b1': 8.0,
     'L1_ffn_W1': 3.678,
     'L1_ffn_W2': 3.604}
    for name, (base, spread) in spreads.items():
        noise = np.random.default_rng([zlib.crc32(name.encode()), seed]).standard_normal(out[name].shape)
        drawn = base * np.exp(spread * noise) if base else spread * noise
        out[name] = jnp.asarray(drawn.astype(out[name].dtype))
    for name, factor in factors.items():
        out[name] = (out[name] * factor).astype(out[name].dtype)
    return out
```

```python
from contextlib import ExitStack

import numpy as np

import concourse.bass as bass
from concourse import mybir

F32 = mybir.dt.float32
BF16 = mybir.dt.bfloat16
ALU = mybir.AluOpType
ACT = mybir.ActivationFunctionType
AX_X = mybir.AxisListType.X

SEQS = 16
T = 256
D = 128
PAD = 34
STRIDE = PAD + T


def clear_semaphores(nc, semaphores):
    with nc.Block() as block:
        @block.gpsimd
        def _(pool):
            for semaphore in semaphores.values():
                pool.sem_clear(semaphore)

A_HEADS = 16
A_DH = D // A_HEADS
A_G = 4
NEG = -1e30


def causal_attention(nc, dram, X):
    with ExitStack() as ctx:
        def sb(name, shape, dt=F32):
            return ctx.enter_context(nc.sbuf_tensor("a_" + name, shape, dt))

        Wq = sb("Wq", [128, A_G, 128])
        Wk = sb("Wk", [128, A_G, 128])
        Wv = sb("Wv", [128, 128])
        Wp = sb("Wp", [128, A_G, 128])
        qk_bias = sb("qk_bias", [128, 2, A_G])
        v_bias = sb("v_bias", [128, 128])
        p_bias = sb("p_bias", [128, 1])
        neg_ident = sb("neg_ident", [128, 128])
        ident_b = sb("ident_b", [128, 128], BF16)
        mask_q = sb("mask_q", [128, 256], BF16)
        mask_k = sb("mask_k", [128, 256], BF16)
        mean_w = sb("mean_w", [128, 128])
        ones = sb("ones", [128, 32])
        eps = sb("eps", [128, 1])
        xf = sb("xf", [128, 2, T])
        qT = sb("qT", [128, 2, A_G, T])
        kT = sb("kT", [128, 2, A_G, T])
        V = sb("V", [128, 2, 2, A_HEADS, 32])
        M = sb("M", [128, 2, A_G, 128])
        PTa = sb("PTa", [128, 4, A_G, T])
        PTb = sb("PTb", [128, 4, A_G, 128])
        rsum = sb("rsum", [128, 512])
        Y = sb("Y", [128, A_G, T])
        r = sb("r", [128, T])
        xc = sb("xc", [128, T])
        xsq = sb("xsq", [128, T])
        std = sb("std", [128, T])
        rstd = sb("rstd", [128, T])
        banks = [ctx.enter_context(nc.psum_tensor(f"a_bank{i}", [128, 512], F32)) for i in range(8)]

        names = """w_in memset_done xf_ready qkv_done qkv_taken s_done max_ready st_done pt_ready
            mt_done q_aug pv_done rsum_ready y_ready out_done r_ready mean_done xc_ready xsq_ready var_done
            std_ready rstd_ready x_ready gate""".split()
        s = {n: ctx.enter_context(nc.semaphore("a_" + n)) for n in names}
        ctx.callback(clear_semaphores, nc, s)

        def seq_wait(eng, name, seq, per=1, more=None):
            eng.wait_ge(s[name], seq * per + (per if more is None else more))

        block = ctx.enter_context(nc.Block())
        n_loads = 11

        def run(eng, slot):
            slot(0, 0, True, False, False)
            slot(1, 1, True, True, False)
            with eng.Fori(1, SEQS // 2) as half:
                slot(half * 2, 0, True, True, True)
                slot(half * 2 + 1, 1, True, True, True)
            slot(SEQS, 0, False, True, True)

        @block.sync
        def _(sp):
            for dst, name in ((Wq, "A_Wq"), (Wk, "A_Wk"), (Wv, "A_Wv"), (Wp, "A_Wp"), (qk_bias, "A_qk_bias"),
                              (p_bias, "A_p_bias"), (neg_ident, "neg_ident")):
                sp.dma_start(dst[:], dram[name]).then_inc(s["w_in"], 16)
            sp.dma_start(v_bias[:], dram["A_v_bias"].partition_broadcast(128)).then_inc(s["w_in"], 16)
            for dst, name in ((ident_b, "ident_b"), (mask_q, "mask_q"), (mask_k, "mask_k")):
                sp.dma_start(dst[:], dram[name]).then_inc(s["w_in"], 16)

        @block.tensor
        def _(pe):
            pe.wait_ge(s["w_in"], 16 * n_loads)
            pe.wait_ge(s["memset_done"], 5)

            def slot(k, par, cur, prev, pprev):
                p, was = k - 1, 1 - par
                if cur:
                    seq_wait(pe, "xf_ready", k)
                    if pprev:
                        seq_wait(pe, "xc_ready", k - 2)
                        seq_wait(pe, "std_ready", k - 2)
                    elif prev:
                        seq_wait(pe, "q_aug", p, 2)
                    for job in range(4):
                        if job >= 2:
                            seq_wait(pe, "qkv_taken", k, 5, job - 1)
                        W = (Wq, Wk)[job // 2]
                        for g in range(2):
                            mm = nc.tensor.matmul(banks[4 + job % 2][:, 256 * g:256 * g + 256],
                                                  W[:, 2 * (job % 2) + g, :], xf[:, par, :], start=True, stop=True)
                        mm.then_inc(s["qkv_done"], 1)
                    seq_wait(pe, "qkv_taken", k, 5, 3)
                    for t in range(2):
                        mm = nc.tensor.matmul(banks[4][:, 128 * t:128 * t + 128], xf[:, par, 128 * t:128 * t + 128], Wv[:],
                                              start=True, stop=True)
                    mm.then_inc(s["qkv_done"], 1)
                    seq_wait(pe, "qkv_taken", k, 5, 4)
                if prev:
                    seq_wait(pe, "q_aug", p, 2)
                for i in range(4):
                    rows = slice(32 * i, 32 * i + A_DH)
                    aug = slice(32 * i, 32 * i + A_DH + 1)
                    for j in range(3):
                        job = 3 * i + j
                        if cur:
                            bank = banks[job % 2]
                            if job >= 2:
                                seq_wait(pe, "max_ready", k, 12, job - 1)
                            elif prev:
                                seq_wait(pe, "max_ready", p, 12, 11 + job)
                            if j == 0:
                                nc.tensor.matmul(bank[:], ident_b[:], mask_q[:, 128:256].unsqueeze(1).to_broadcast([128, 4, 128]),
                                                 start=True, stop=False, skip_group_check=True)
                                for g in range(4):
                                    mm = nc.tensor.matmul(bank[:, 128 * g:128 * g + 128], qT[rows, par, g, 0:128],
                                                          kT[rows, par, g, 0:128], start=False, stop=g == 3,
                                                          skip_group_check=True)
                            else:
                                nc.tensor.matmul(bank[:], ident_b[:], mask_q[:].unsqueeze(1).to_broadcast([128, 2, 256]),
                                                 start=True, stop=False, skip_group_check=True)
                                for g in range(2):
                                    mm = nc.tensor.matmul(bank[:, 256 * g:256 * g + 256], qT[rows, par, 2 * (j - 1) + g, 128:256],
                                                          kT[rows, par, 2 * (j - 1) + g, :], start=False, stop=g == 1,
                                                          skip_group_check=True)
                            mm.then_inc(s["s_done"], 1)
                        if prev:
                            bank = banks[2 + job % 2]
                            if job >= 2:
                                seq_wait(pe, "pt_ready", p, 12, job - 1)
                            elif pprev:
                                seq_wait(pe, "pt_ready", k - 2, 12, 11 + job)
                            if j == 0:
                                nc.tensor.matmul(bank[:], ident_b[:], mask_k[:, 0:128].unsqueeze(1).to_broadcast([128, 4, 128]),
                                                 start=True, stop=False, skip_group_check=True)
                                for g in range(4):
                                    mm = nc.tensor.matmul(bank[:, 128 * g:128 * g + 128], kT[aug, was, g, 128:256],
                                                          qT[aug, was, g, 128:256], start=False, stop=g == 3,
                                                          skip_group_check=True)
                            else:
                                nc.tensor.matmul(bank[:], ident_b[:], mask_k[:].unsqueeze(1).to_broadcast([128, 2, 256]),
                                                 start=True, stop=False, skip_group_check=True)
                                for g in range(2):
                                    mm = nc.tensor.matmul(bank[:, 256 * g:256 * g + 256], kT[aug, was, 2 * (j - 1) + g, 0:128],
                                                          qT[aug, was, 2 * (j - 1) + g, :], start=False, stop=g == 1,
                                                          skip_group_check=True)
                            mm.then_inc(s["st_done"], 1)
                if prev:
                    seq_wait(pe, "pt_ready", p, 12)
                    for gp in range(2):
                        if gp == 1:
                            seq_wait(pe, "y_ready", p, 2, 1)
                        elif pprev:
                            seq_wait(pe, "y_ready", k - 2, 2)
                        for bank, what in ((banks[6], "y"), (banks[7], "sum")):
                            for g in range(2):
                                at = 256 * g
                                for tile in range(2):
                                    for i in range(4):
                                        G = 2 * gp + g
                                        w = V[:, was, tile, 4 * G + i, :] if what == "y" else ones[:]
                                        rhs = PTa[:, i, G, :] if tile == 0 else PTb[:, i, G, :]
                                        mm = nc.tensor.matmul(bank[32 * i:32 * i + 32, at + 128 * tile:at + 256], w, rhs,
                                                              start=tile == 0, stop=tile == 1, skip_group_check=True)
                        mm.then_inc(s["pv_done"], 1)
                if cur:
                    for t in range(2):
                        if t == 0:
                            seq_wait(pe, "max_ready", k, 12)
                            seq_wait(pe, "qkv_taken", k, 5)
                        for g in range(A_G):
                            mm = nc.tensor.matmul(banks[5 - t][:, 128 * g:128 * g + 128], M[:, t, g, :], neg_ident[:],
                                                  start=True, stop=True)
                        mm.then_inc(s["mt_done"], 1)
                if prev:
                    seq_wait(pe, "y_ready", p, 2)
                    if cur:
                        seq_wait(pe, "q_aug", k, 2, 1)
                    elif pprev:
                        seq_wait(pe, "std_ready", k - 2)
                    for g in range(A_G):
                        mm = nc.tensor.matmul(banks[5][:, 0:T], Wp[:, g, :], Y[:, g, :], start=g == 0, stop=g == A_G - 1)
                    mm.then_inc(s["out_done"], 1)
                    if cur:
                        seq_wait(pe, "q_aug", k, 2)
                    seq_wait(pe, "r_ready", p)
                    nc.tensor.matmul(banks[4][:, 0:T], mean_w[:], r[:], start=True, stop=True).then_inc(s["mean_done"], 1)
                    seq_wait(pe, "xsq_ready", p)
                    nc.tensor.matmul(banks[5][:, 0:T], mean_w[:], xsq[:], start=True, stop=True).then_inc(s["var_done"], 1)

            run(pe, slot)

        @block.scalar
        def _(act):
            act.wait_ge(s["memset_done"], 5)

            def slot(k, par, cur, prev, pprev):
                p = k - 1
                if prev:
                    for job in range(12):
                        i, j = divmod(job, 3)
                        seq_wait(act, "st_done", p, 12, job + 1)
                        if job == 0 and pprev:
                            seq_wait(act, "pv_done", k - 2, 2)
                        dst = PTb[:, i, :, :] if j == 0 else PTa[:, i, 2 * (j - 1):2 * j, :]
                        nc.scalar.activation(dst.rearrange("p g t -> p (g t)"), banks[2 + job % 2][:], ACT.Exp,
                                             scale=float(A_DH) ** -0.5).then_inc(s["pt_ready"], 1)
                    seq_wait(act, "var_done", p)
                    nc.scalar.activation(std[:], banks[5][:, 0:T], ACT.Sqrt, bias=eps[:, 0:1]).then_inc(s["std_ready"], 1)

            run(act, slot)

        @block.gpsimd
        def _(pool):
            nc.gpsimd.memset(eps[:], 1e-5).then_inc(s["memset_done"], 1)
            nc.gpsimd.memset(mean_w[:], 1.0 / 128).then_inc(s["memset_done"], 1)
            nc.gpsimd.memset(ones[:], 1.0).then_inc(s["memset_done"], 1)
            nc.gpsimd.memset(V[:], 0.0).then_inc(s["memset_done"], 1)
            nc.gpsimd.memset(M[:], 0.0).then_inc(s["memset_done"], 1)

            def slot(k, par, cur, prev, pprev):
                p = k - 1
                if cur:
                    if pprev:
                        seq_wait(pool, "qkv_done", k - 2, 5)
                        seq_wait(pool, "r_ready", k - 2)
                        pool.sem_inc(s["gate"], 1)
                    nc.gpsimd.tensor_copy(xf[:, par, :], X[:, k, PAD:]).then_inc(s["xf_ready"], 1)
                if prev:
                    seq_wait(pool, "xc_ready", p)
                    if pprev:
                        seq_wait(pool, "var_done", k - 2)
                    nc.gpsimd.tensor_tensor(xsq[:], xc[:], xc[:], ALU.mult).then_inc(s["xsq_ready"], 1)

            run(pool, slot)

        @block.vector
        def _(dve):
            dve.wait_ge(s["w_in"], 16 * n_loads)
            dve.wait_ge(s["memset_done"], 5)

            def slot(k, par, cur, prev, pprev):
                p, was = k - 1, 1 - par
                if cur:
                    for job in range(4):
                        half, pair = divmod(job, 2)
                        dst = (qT, kT)[half]
                        seq_wait(dve, "qkv_done", k, 5, job + 1)
                        if job == 0 and pprev:
                            seq_wait(dve, "st_done", k - 2, 12)
                        nc.vector.tensor_tensor(dst[:, par, 2 * pair:2 * pair + 2, :],
                                                banks[4 + job % 2][:].rearrange("p (g t) -> p g t", g=2),
                                                qk_bias[:, half, 2 * pair:2 * pair + 2].unsqueeze(2).to_broadcast([128, 2, T]),
                                                ALU.add).then_inc(s["qkv_taken"], 1)
                    seq_wait(dve, "qkv_done", k, 5)
                    if pprev:
                        seq_wait(dve, "pv_done", k - 2, 2)
                    nc.vector.tensor_tensor(V[:, par, :, :, 0:A_DH], banks[4][:, 0:256].rearrange("p (t h d) -> p t h d", t=2, d=A_DH),
                                            v_bias[:].rearrange("p (h d) -> p h d", d=A_DH).unsqueeze(1).to_broadcast([128, 2, A_HEADS, A_DH]),
                                            ALU.add).then_inc(s["qkv_taken"], 1)
                    for job in range(12):
                        i, j = divmod(job, 3)
                        seq_wait(dve, "s_done", k, 12, job + 1)
                        if job == 0 and prev:
                            seq_wait(dve, "mt_done", p, 2)
                        if j == 0:
                            dst, src = M[:, 0, :, 32 * i + A_DH], banks[job % 2][:].rearrange("p (g t) -> p g t", g=4)
                        else:
                            dst = M[:, 1, 2 * (j - 1):2 * j, 32 * i + A_DH]
                            src = banks[job % 2][:].rearrange("p (g t) -> p g t", g=2)
                        nc.vector.tensor_reduce(dst, src, AX_X, ALU.max).then_inc(s["max_ready"], 1)
                if prev:
                    for gp in range(2):
                        seq_wait(dve, "pv_done", p, 2, gp + 1)
                        if gp == 1:
                            seq_wait(dve, "y_ready", p, 2, 1)
                        elif pprev:
                            seq_wait(dve, "y_ready", k - 2, 2)
                            seq_wait(dve, "out_done", k - 2)
                        nc.vector.reciprocal(rsum[:], banks[7][:]).then_inc(s["rsum_ready"], 1)
                        seq_wait(dve, "rsum_ready", p, 2, gp + 1)
                        nc.vector.tensor_tensor(Y[:, 2 * gp:2 * gp + 2, :].rearrange("p g t -> p (g t)"), banks[6][:], rsum[:], ALU.mult)\
                            .then_inc(s["y_ready"], 1)
                if cur:
                    seq_wait(dve, "s_done", k, 12)
                    for t in range(2):
                        seq_wait(dve, "mt_done", k, 2, t + 1)
                        part = qT[:, par, :, 128 * t:128 * t + 128]
                        nc.vector.tensor_tensor(part, part, banks[5 - t][:].rearrange("p (g t) -> p g t", g=4), ALU.add)\
                            .then_inc(s["q_aug"], 1)
                if prev:
                    seq_wait(dve, "out_done", p)
                    nc.vector.scalar_tensor_tensor(r[:], banks[5][:, 0:T], p_bias[:, 0:1], xf[:, was, :], ALU.add, ALU.add)\
                        .then_inc(s["r_ready"], 1)
                    seq_wait(dve, "mean_done", p)
                    seq_wait(dve, "r_ready", p)
                    nc.vector.tensor_tensor(xc[:], r[:], banks[4][:, 0:T], ALU.subtract).then_inc(s["xc_ready"], 1)
                    seq_wait(dve, "std_ready", p)
                    nc.vector.reciprocal(rstd[:], std[:]).then_inc(s["rstd_ready"], 1)
                    seq_wait(dve, "rstd_ready", p)
                    nc.vector.tensor_tensor(X[:, p, PAD:], xc[:], rstd[:], ALU.mult).then_inc(s["x_ready"], 1)
                    seq_wait(dve, "x_ready", p)

            run(dve, slot)


def layouts_a(i):
    w = np.asarray(i["L0_attn_W_qkv"]).reshape(D, 3, A_G, 4, A_DH)
    b = np.asarray(i["L0_attn_b_qkv"]).reshape(3, A_G, 4, A_DH)
    out = {}
    for n, name in ((0, "A_Wq"), (1, "A_Wk")):
        a = np.zeros((D, A_G, 4, 32), np.float32)
        a[..., :A_DH] = w[:, n]
        out[name] = a.reshape(D, A_G, 128)
    bias = np.zeros((4, 32, 2, A_G), np.float32)
    bias[:, :A_DH] = b[0:2].transpose(2, 3, 0, 1)
    bias[:, A_DH, 1] = 1.0
    out["A_qk_bias"] = bias.reshape(128, 2, A_G)
    out["A_Wv"] = w[:, 2].reshape(D, D)
    out["A_v_bias"] = b[2].reshape(D)
    wp = np.zeros((4, 32, A_G, D), np.float32)
    wp[:, :A_DH] = np.asarray(i["L0_attn_W_proj"]).reshape(A_G, 4, A_DH, D).transpose(1, 2, 0, 3)
    out["A_Wp"] = wp.reshape(128, A_G, D)
    out["A_p_bias"] = np.asarray(i["L0_attn_b_proj"]).reshape(D, 1)
    return out


def constants_a():
    late = np.triu(np.ones((128, 128), bool), 1)
    q = np.zeros((128, 256), np.float32)
    q[:, 128:][late] = NEG
    k = np.zeros((128, 256), np.float32)
    k[:, :128][late.T] = NEG
    b = lambda a: a.astype(mybir.dt.np(BF16))
    eye = np.eye(128, dtype=np.float32)
    return {"neg_ident": -eye, "ident_b": b(eye), "mask_q": b(q), "mask_k": b(k)}


DEPTH = 8
LEAVES = 2 ** DEPTH
LW = 16
CH = LEAVES * LW // 128
NG = 8
GT = SEQS * T // NG
RING = 4


def standardise(nc, dram, X, XN):
    with ExitStack() as ctx:
        def sb(name, shape, dt=F32):
            return ctx.enter_context(nc.sbuf_tensor("n_" + name, shape, dt))

        mean_w = sb("mean_w", [128, 128])
        var_w = sb("var_w", [128, 128])
        eps = sb("eps", [128, 1])
        xc = sb("xc", [128, 2, T])
        xsq = sb("xsq", [128, 2, T])
        sd = sb("sd", [128, 2, T])
        root = sb("root", [128, 2, T])
        inv = sb("inv", [128, 2, T])
        ps = ctx.enter_context(nc.psum_tensor("n_ps", [128, 4, 512], F32))
        names = "memset_done mean_done xc_ready xsq_ready var_done sd_ready root_ready inv_ready xn_ready gate".split()
        s = {n: ctx.enter_context(nc.semaphore("n_" + n)) for n in names}
        ctx.callback(clear_semaphores, nc, s)

        def seq_wait(eng, name, seq):
            eng.wait_ge(s[name], seq + 1)

        block = ctx.enter_context(nc.Block())

        def run(eng, slot):
            slot(0, 0, False)
            slot(1, 1, False)
            with eng.Fori(1, SEQS // 2) as half:
                slot(half * 2, 0, True)
                slot(half * 2 + 1, 1, True)

        @block.tensor
        def _(pe):
            pe.wait_ge(s["memset_done"], 3)

            def slot(k, par, again):
                if again:
                    seq_wait(pe, "xc_ready", k - 2)
                nc.tensor.matmul(ps[:, par, 0:T], mean_w[:], X[:, k, PAD:], start=True, stop=True).then_inc(s["mean_done"], 1)
                seq_wait(pe, "xsq_ready", k)
                if again:
                    seq_wait(pe, "sd_ready", k - 2)
                nc.tensor.matmul(ps[:, 2 + par, 0:T], var_w[:], xsq[:, par, :], start=True, stop=True).then_inc(s["var_done"], 1)

            run(pe, slot)

        @block.scalar
        def _(act):
            act.wait_ge(s["memset_done"], 3)

            def slot(k, par, again):
                seq_wait(act, "var_done", k)
                nc.scalar.activation(sd[:, par, :], ps[:, 2 + par, 0:T], ACT.Sqrt).then_inc(s["sd_ready"], 1)
                seq_wait(act, "sd_ready", k)
                if again:
                    seq_wait(act, "inv_ready", k - 2)
                nc.scalar.activation(root[:, par, :], sd[:, par, :], ACT.Sqrt, bias=eps[:, 0:1]).then_inc(s["root_ready"], 1)

            run(act, slot)

        @block.gpsimd
        def _(pool):
            nc.gpsimd.memset(eps[:], 1e-5).then_inc(s["memset_done"], 1)
            nc.gpsimd.memset(mean_w[:], 1.0 / D).then_inc(s["memset_done"], 1)
            nc.gpsimd.memset(var_w[:], 1.0 / (D - 1)).then_inc(s["memset_done"], 1)

            def slot(k, par, again):
                seq_wait(pool, "xc_ready", k)
                nc.gpsimd.tensor_tensor(xsq[:, par, :], xc[:, par, :], xc[:, par, :], ALU.mult).then_inc(s["xsq_ready"], 1)

            run(pool, slot)

        @block.vector
        def _(dve):
            def slot(k, par, again):
                seq_wait(dve, "mean_done", k)
                if again:
                    seq_wait(dve, "xn_ready", k - 2)
                nc.vector.tensor_tensor(xc[:, par, :], X[:, k, PAD:], ps[:, par, 0:T], ALU.subtract).then_inc(s["xc_ready"], 1)
                seq_wait(dve, "root_ready", k)
                nc.vector.reciprocal(inv[:, par, :], root[:, par, :]).then_inc(s["inv_ready"], 1)
                seq_wait(dve, "inv_ready", k)
                nc.vector.tensor_tensor(XN[:, bass.ds(k * T, T)], xc[:, par, :], inv[:, par, :], ALU.mult).then_inc(s["xn_ready"], 1)

            run(dve, slot)


def fast_feedforwards(nc, dram, modules, act_func):
    with ExitStack() as ctx:
        n_mod = len(modules)
        tag = modules[0][0]

        def sb(name, shape, dt=F32):
            return ctx.enter_context(nc.sbuf_tensor(f"{tag}_{name}", shape, dt))

        nbuf = 2 if n_mod > 1 else 1
        nodes = sb("nodes", [128, nbuf, LEAVES])
        node_b = sb("node_b", [128, nbuf, 2])
        W1 = sb("W1", [128, nbuf, CH * 128])
        b1 = sb("b1", [128, nbuf, CH])
        W2 = sb("W2", [128, nbuf, CH, 128])
        b2 = sb("b2", [128, nbuf, 2, 128])
        paths = sb("paths", [128, 2, LEAVES], BF16)
        rights = sb("rights", [128, 2])
        leaf_no = sb("leaf_no", [128, 2, 128])
        chunk_leaf = sb("chunk_leaf", [128, CH])
        bits = sb("bits", [128, 2, GT], BF16)
        onehot = sb("onehot", [128, 2, 2, GT])
        routed = sb("routed", [128, 2, GT])
        hid = sb("hid", [128, RING, GT])
        hm = sb("hm", [128, RING, GT])
        pp = ctx.enter_context(nc.psum_tensor(f"{tag}_ps_prep", [128, 2, 512], F32))
        ph = ctx.enter_context(nc.psum_tensor(f"{tag}_ps_hid", [128, RING, 512], F32))
        po = ctx.enter_context(nc.psum_tensor(f"{tag}_ps_out", [128, 2, 512], F32))
        names = """consts_in w_in0 w_in1 bits_done bits_ready match_done onehot_ready routed_done routed_ready
            hid_done hid_ready hm_ready second_done out_done out_ready gate_act""".split()
        s = {n: ctx.enter_context(nc.semaphore(f"{tag}_{n}")) for n in names}
        ctx.callback(clear_semaphores, nc, s)

        def group_wait(eng, name, group, per=1, more=None):
            eng.wait_ge(s[name], group * per + (per if more is None else more))

        block = ctx.enter_context(nc.Block())

        def run(eng, slot):
            for m in range(n_mod):
                if m == 0:
                    slot(0, 0, 0, 0, True, False, False)
                    slot(0, 1, 1, 1, True, True, False)
                else:
                    slot(m, m * NG, 0, 0, True, True, True)
                    slot(m, m * NG + 1, 1, 1, True, True, True)
                with eng.Fori(1, NG // 2) as half:
                    slot(m, half * 2 + m * NG, half * 2, 0, True, True, True)
                    slot(m, half * 2 + (m * NG + 1), half * 2 + 1, 1, True, True, True)
            slot(n_mod, n_mod * NG, 0, 0, False, True, True)

        @block.sync
        def _(sp):
            for dst, name in ((paths, "paths"), (rights, "rights"), (leaf_no, "leaf_no"), (chunk_leaf, "chunk_leaf")):
                sp.dma_start(dst[:], dram[name]).then_inc(s["consts_in"], 16)
            for m, (name, _, _) in enumerate(modules):
                buf = m % nbuf
                if m >= nbuf:
                    sp.wait_ge(s["out_done"], NG * (m - nbuf + 1))
                for dst, part in ((nodes, "nw"), (node_b, "nb"), (W1, "w1"), (b1, "b1"), (W2, "w2"), (b2, "b2")):
                    sp.dma_start(dst[:, buf], dram[f"{name}_{part}"]).then_inc(s[f"w_in{buf}"], 16)

        @block.tensor
        def _(pe):
            pe.wait_ge(s["consts_in"], 64)

            def slot(m, n, g, par, cur, prev, pprev):
                q = n - 1
                buf = m % nbuf
                prep = []
                if cur:
                    src = modules[m][1]
                    cols = bass.ds(g * GT, GT)

                    def route_bits(j):
                        if isinstance(n, int) and n % NG == 0 and j == 0:
                            pe.wait_ge(s[f"w_in{buf}"], 96 * (m // nbuf + 1))
                        if prev:
                            group_wait(pe, "routed_ready", q)
                            group_wait(pe, "onehot_ready", q, 2)
                        nc.tensor.matmul(pp[:, j, :], nodes[:, buf, 128 * j:128 * j + 128], src[:, cols], start=True, stop=True)\
                            .then_inc(s["bits_done"], 1)

                    def match(j):
                        group_wait(pe, "bits_ready", n, 2)
                        for half in range(2):
                            mm = nc.tensor.matmul(pp[:, j, :], paths[:, half, 128 * j:128 * j + 128], bits[:, half, :],
                                                  start=half == 0, stop=half == 1)
                        mm.then_inc(s["match_done"], 1)

                    def leaf_number():
                        group_wait(pe, "onehot_ready", n, 2)
                        for half in range(2):
                            mm = nc.tensor.matmul(pp[:, 0, :], leaf_no[:, half, :], onehot[:, par, half, :],
                                                  start=half == 0, stop=half == 1)
                        mm.then_inc(s["routed_done"], 1)

                    prep = [(2, lambda: route_bits(0)), (3, lambda: route_bits(1)), (8, lambda: match(0)),
                            (9, lambda: match(1)), (14, leaf_number)]
                if prev:
                    first = isinstance(n, int) and n % NG == 0
                    qm = m - 1 if first else m
                    qbuf, qpar = qm % nbuf, 1 - par
                    qcols = bass.ds(((NG - 1) if first else g - 1) * GT, GT)
                    qsrc = modules[qm][1]

                    def hidden(c):
                        if c >= RING:
                            group_wait(pe, "hid_ready", q, CH, c - RING + 1)
                        elif pprev:
                            group_wait(pe, "hid_ready", n - 2, CH, CH - RING + c + 1)
                        nc.tensor.matmul(ph[:, c % RING, :], W1[:, qbuf, 128 * c:128 * c + 128], qsrc[:, qcols],
                                         start=True, stop=True).then_inc(s["hid_done"], 1)

                    def second(c):
                        group_wait(pe, "hm_ready", q, CH, c + 1)
                        mm = nc.tensor.matmul(po[:, qpar, :], W2[:, qbuf, c, :], hm[:, c % RING, :], start=False, stop=c == CH - 1)
                        mm.then_inc(s["out_done"] if c == CH - 1 else s["second_done"], 1)

                    if pprev:
                        group_wait(pe, "out_ready", n - 2)
                    for half in range(2):
                        nc.tensor.matmul(po[:, qpar, :], b2[:, qbuf, half, :], onehot[:, qpar, half, :], start=half == 0, stop=False)
                    for c in range(CH + 2):
                        for at, step in prep:
                            if at == c:
                                step()
                        if c < CH:
                            hidden(c)
                        if c >= 2:
                            second(c - 2)
                else:
                    for _, step in prep:
                        step()

            run(pe, slot)

        @block.scalar
        def _(act):
            def slot(m, n, g, par, cur, prev, pprev):
                q = n - 1
                if prev:
                    first = isinstance(n, int) and n % NG == 0
                    qm = m - 1 if first else m
                    qbuf, qpar = qm % nbuf, 1 - par
                    dst = modules[qm][2]
                    qcols = bass.ds(((NG - 1) if first else g - 1) * GT, GT)
                    for c in range(CH):
                        if cur and c == 15:
                            leaf_number(n, par)
                        group_wait(act, "hid_done", q, CH, c + 1)
                        if c >= RING:
                            group_wait(act, "hm_ready", q, CH, c - RING + 1)
                        nc.scalar.activation(hid[:, c % RING, :], ph[:, c % RING, :], act_func, bias=b1[:, qbuf, c:c + 1])\
                            .then_inc(s["hid_ready"], 1)
                    group_wait(act, "out_done", q)
                    act.sem_inc(s["gate_act"], 1)
                    nc.scalar.activation(dst[:, qcols], po[:, qpar, :], ACT.Copy).then_inc(s["out_ready"], 1)
                else:
                    leaf_number(n, par)

            def leaf_number(n, par):
                group_wait(act, "routed_done", n)
                nc.scalar.activation(routed[:, par, :], pp[:, 0, :], ACT.Copy).then_inc(s["routed_ready"], 1)

            run(act, slot)

        @block.vector
        def _(dve):
            dve.wait_ge(s["consts_in"], 64)

            def route_bits(m, n, j, prev):
                group_wait(dve, "bits_done", n, 2, j + 1)
                if prev and j == 0:
                    group_wait(dve, "match_done", n - 1, 2)
                nc.vector.tensor_scalar(bits[:, j, :], pp[:, j, :], node_b[:, m % nbuf, j:j + 1], 0.0, ALU.add, ALU.is_gt)\
                    .then_inc(s["bits_ready"], 1)

            def match(n, par, j, pprev):
                group_wait(dve, "match_done", n, 2, j + 1)
                if pprev and j == 0:
                    group_wait(dve, "out_done", n - 2)
                nc.vector.tensor_scalar(onehot[:, par, j, :], pp[:, j, :], rights[:, j:j + 1], None, ALU.is_equal)\
                    .then_inc(s["onehot_ready"], 1)

            def slot(m, n, g, par, cur, prev, pprev):
                q = n - 1
                if prev:
                    qpar = 1 - par
                    for c in range(CH):
                        if cur and c in (3, 4):
                            route_bits(m, n, c - 3, prev)
                        if cur and c in (9, 10):
                            match(n, par, c - 9, pprev)
                        group_wait(dve, "hid_ready", q, CH, c + 1)
                        if c == 0:
                            group_wait(dve, "routed_ready", q)
                        if c >= RING:
                            group_wait(dve, "second_done", q, CH - 1, c - RING + 1)
                        elif pprev:
                            group_wait(dve, "out_done", n - 2)
                        nc.vector.scalar_tensor_tensor(hm[:, c % RING, :], routed[:, qpar, :], chunk_leaf[:, c:c + 1],
                                                       hid[:, c % RING, :], ALU.is_equal, ALU.mult).then_inc(s["hm_ready"], 1)
                else:
                    for j in range(2):
                        route_bits(m, n, j, prev)
                    for j in range(2):
                        match(n, par, j, pprev)

            run(dve, slot)


def leaf_attention(nc, dram, XN, Q, K, V):
    with ExitStack() as ctx:
        def sb(name, shape, dt=F32):
            return ctx.enter_context(nc.sbuf_tensor("t_" + name, shape, dt))

        ident = sb("ident", [128, 128])
        qf = sb("qf", [128, 2, T])
        vf = sb("vf", [128, 2, T])
        Vt = sb("Vt", [128, 2, T])
        mx = sb("mx", [128, 2])
        nm = sb("nm", [128, 2])
        P = sb("P", [128, 2, T])
        den = sb("den", [128, 2])
        rden = sb("rden", [128, 2])
        Pn = sb("Pn", [128, 2, T])
        PT = sb("PT", [128, 2, T])
        ps_s = ctx.enter_context(nc.psum_tensor("t_s", [128, 512], F32))
        ps_v = ctx.enter_context(nc.psum_tensor("t_v", [128, 512], F32))
        ps_t = ctx.enter_context(nc.psum_tensor("t_t", [128, 512], F32))
        ps_o = ctx.enter_context(nc.psum_tensor("t_o", [128, 512], F32))
        names = """ident_in qf_ready vf_ready s_done mx_ready nm_ready p_ready rden_ready pn_ready pt_done pt_ready
            vt_done vt_ready o_done y_ready gate""".split()
        s = {n: ctx.enter_context(nc.semaphore("t_" + n)) for n in names}
        ctx.callback(clear_semaphores, nc, s)

        def seq_wait(eng, name, seq, per=1, more=None):
            eng.wait_ge(s[name], seq * per + (per if more is None else more))

        scale = float(D) ** -0.5
        block = ctx.enter_context(nc.Block())

        def run(eng, slot):
            slot(0, 0, True, False, False)
            slot(1, 1, True, True, False)
            with eng.Fori(1, SEQS // 2) as half:
                slot(half * 2, 0, True, True, True)
                slot(half * 2 + 1, 1, True, True, True)
            slot(SEQS, 0, False, True, True)

        @block.sync
        def _(sp):
            sp.dma_start(ident[:], dram["ident"]).then_inc(s["ident_in"], 16)

        @block.gpsimd
        def _(pool):
            def slot(k, par, cur, prev, pprev):
                if cur:
                    if pprev:
                        seq_wait(pool, "s_done", k - 2)
                        seq_wait(pool, "vt_done", k - 2)
                        pool.sem_inc(s["gate"], 1)
                    nc.gpsimd.tensor_copy(qf[:, par, :], Q[:, bass.ds(k * T, T)]).then_inc(s["qf_ready"], 1)
                    nc.gpsimd.tensor_copy(vf[:, par, :], V[:, bass.ds(k * T, T)]).then_inc(s["vf_ready"], 1)

            run(pool, slot)

        @block.tensor
        def _(pe):
            pe.wait_ge(s["ident_in"], 16)

            def slot(k, par, cur, prev, pprev):
                p = k - 1
                if cur:
                    seq_wait(pe, "qf_ready", k)
                    if prev:
                        seq_wait(pe, "p_ready", p, 2)
                        seq_wait(pe, "mx_ready", p)
                    for t in range(2):
                        mm = nc.tensor.matmul(ps_s[:, T * t:T * t + T], qf[:, par, 128 * t:128 * t + 128], K[:, bass.ds(k * T, T)],
                                              start=True, stop=True)
                    mm.then_inc(s["s_done"], 1)
                    seq_wait(pe, "vf_ready", k)
                    if prev:
                        seq_wait(pe, "vt_ready", p)
                    for t in range(2):
                        mm = nc.tensor.transpose(ps_v[:, 128 * t:128 * t + 128], vf[:, par, 128 * t:128 * t + 128], ident[:])
                    mm.then_inc(s["vt_done"], 1)
                if prev:
                    seq_wait(pe, "pn_ready", p, 2)
                    if pprev:
                        seq_wait(pe, "pt_ready", k - 2)
                    for tq in range(2):
                        for tk in range(2):
                            mm = nc.tensor.transpose(ps_t[:, T * tk + 128 * tq:T * tk + 128 * tq + 128],
                                                     Pn[:, tq, 128 * tk:128 * tk + 128], ident[:])
                    mm.then_inc(s["pt_done"], 1)
                    seq_wait(pe, "pt_ready", p)
                    seq_wait(pe, "vt_ready", p)
                    if pprev:
                        seq_wait(pe, "y_ready", k - 2)
                    for t in range(2):
                        mm = nc.tensor.matmul(ps_o[:, 0:T], Vt[:, 1 - par, 128 * t:128 * t + 128], PT[:, t, :],
                                              start=t == 0, stop=t == 1)
                    mm.then_inc(s["o_done"], 1)

            run(pe, slot)

        @block.scalar
        def _(act):
            def slot(k, par, cur, prev, pprev):
                p = k - 1
                if cur:
                    seq_wait(act, "nm_ready", k)
                    if prev:
                        seq_wait(act, "pn_ready", p, 2)
                    for t in range(2):
                        nc.scalar.activation(P[:, t, :], ps_s[:, T * t:T * t + T], ACT.Exp, bias=nm[:, t:t + 1], scale=scale,
                                             accum_out=den[:, t:t + 1]).then_inc(s["p_ready"], 1)
                    seq_wait(act, "vt_done", k)
                    if pprev:
                        seq_wait(act, "o_done", k - 2)
                    nc.scalar.activation(Vt[:, par, :], ps_v[:, 0:T], ACT.Copy).then_inc(s["vt_ready"], 1)
                if prev:
                    seq_wait(act, "pt_done", p)
                    if pprev:
                        seq_wait(act, "o_done", k - 2)
                    nc.scalar.activation(PT[:].rearrange("p a t -> p (a t)"), ps_t[:], ACT.Copy).then_inc(s["pt_ready"], 1)

            run(act, slot)

        @block.vector
        def _(dve):
            def slot(k, par, cur, prev, pprev):
                p = k - 1
                if prev:
                    seq_wait(dve, "p_ready", p, 2)
                    nc.vector.reciprocal(rden[:], den[:]).then_inc(s["rden_ready"], 1)
                    seq_wait(dve, "rden_ready", p)
                    if pprev:
                        seq_wait(dve, "pt_done", k - 2)
                    for t in range(2):
                        nc.vector.tensor_scalar(Pn[:, t, :], P[:, t, :], rden[:, t:t + 1], None, ALU.mult).then_inc(s["pn_ready"], 1)
                if cur:
                    seq_wait(dve, "s_done", k)
                    nc.vector.tensor_reduce(mx[:], ps_s[:].rearrange("p (t k) -> p t k", t=2), AX_X, ALU.max).then_inc(s["mx_ready"], 1)
                    seq_wait(dve, "mx_ready", k)
                    nc.vector.tensor_scalar(nm[:], mx[:], -scale, None, ALU.mult).then_inc(s["nm_ready"], 1)
                if prev:
                    seq_wait(dve, "o_done", p)
                    part = XN[:, bass.ds(p * T, T)]
                    nc.vector.tensor_tensor(part, part, ps_o[:, 0:T], ALU.add).then_inc(s["y_ready"], 1)

            run(dve, slot)


def add_and_norm(nc, X, Y, Z, tag):
    with ExitStack() as ctx:
        def sb(name, shape, dt=F32):
            return ctx.enter_context(nc.sbuf_tensor(f"{tag}_{name}", shape, dt))

        mean_w = sb("mean_w", [128, 128])
        eps = sb("eps", [128, 1])
        yz = sb("yz", [128, 2, T])
        r = sb("r", [128, 2, T])
        xc = sb("xc", [128, 2, T])
        xsq = sb("xsq", [128, 2, T])
        std = sb("std", [128, 2, T])
        rstd = sb("rstd", [128, 2, T])
        ps = ctx.enter_context(nc.psum_tensor(f"{tag}_ps", [128, 4, 512], F32))
        names = "memset_done yz_ready r_ready mean_done xc_ready xsq_ready var_done std_ready rstd_ready x_ready".split()
        s = {n: ctx.enter_context(nc.semaphore(f"{tag}_{n}")) for n in names}
        ctx.callback(clear_semaphores, nc, s)

        def seq_wait(eng, name, seq):
            eng.wait_ge(s[name], seq + 1)

        block = ctx.enter_context(nc.Block())

        def run(eng, slot):
            slot(0, 0, False)
            slot(1, 1, False)
            with eng.Fori(1, SEQS // 2) as half:
                slot(half * 2, 0, True)
                slot(half * 2 + 1, 1, True)

        @block.tensor
        def _(pe):
            pe.wait_ge(s["memset_done"], 2)

            def slot(k, par, again):
                seq_wait(pe, "r_ready", k)
                if again:
                    seq_wait(pe, "xc_ready", k - 2)
                nc.tensor.matmul(ps[:, par, 0:T], mean_w[:], r[:, par, :], start=True, stop=True).then_inc(s["mean_done"], 1)
                seq_wait(pe, "xsq_ready", k)
                if again:
                    seq_wait(pe, "std_ready", k - 2)
                nc.tensor.matmul(ps[:, 2 + par, 0:T], mean_w[:], xsq[:, par, :], start=True, stop=True).then_inc(s["var_done"], 1)

            run(pe, slot)

        @block.scalar
        def _(act):
            act.wait_ge(s["memset_done"], 2)

            def slot(k, par, again):
                seq_wait(act, "var_done", k)
                if again:
                    seq_wait(act, "rstd_ready", k - 2)
                nc.scalar.activation(std[:, par, :], ps[:, 2 + par, 0:T], ACT.Sqrt, bias=eps[:, 0:1]).then_inc(s["std_ready"], 1)

            run(act, slot)

        @block.gpsimd
        def _(pool):
            nc.gpsimd.memset(eps[:], 1e-5).then_inc(s["memset_done"], 1)
            nc.gpsimd.memset(mean_w[:], 1.0 / D).then_inc(s["memset_done"], 1)

            def slot(k, par, again):
                seq_wait(pool, "xc_ready", k)
                if again:
                    seq_wait(pool, "var_done", k - 2)
                nc.gpsimd.tensor_tensor(xsq[:, par, :], xc[:, par, :], xc[:, par, :], ALU.mult).then_inc(s["xsq_ready"], 1)

            run(pool, slot)

        @block.vector
        def _(dve):
            def slot(k, par, again):
                cols = bass.ds(k * T, T)
                if again:
                    seq_wait(dve, "r_ready", k - 2)
                if Z is not None:
                    nc.vector.tensor_tensor(yz[:, par, :], Y[:, cols], Z[:, cols], ALU.add).then_inc(s["yz_ready"], 1)
                    seq_wait(dve, "yz_ready", k)
                if again:
                    seq_wait(dve, "mean_done", k - 2)
                nc.vector.tensor_tensor(r[:, par, :], X[:, k, PAD:], yz[:, par, :] if Z is not None else Y[:, cols], ALU.add)\
                    .then_inc(s["r_ready"], 1)
                seq_wait(dve, "mean_done", k)
                seq_wait(dve, "r_ready", k)
                if again:
                    seq_wait(dve, "x_ready", k - 2)
                nc.vector.tensor_tensor(xc[:, par, :], r[:, par, :], ps[:, par, 0:T], ALU.subtract).then_inc(s["xc_ready"], 1)
                seq_wait(dve, "std_ready", k)
                nc.vector.reciprocal(rstd[:, par, :], std[:, par, :]).then_inc(s["rstd_ready"], 1)
                seq_wait(dve, "rstd_ready", k)
                nc.vector.tensor_tensor(X[:, k, PAD:], xc[:, par, :], rstd[:, par, :], ALU.mult).then_inc(s["x_ready"], 1)

            run(dve, slot)


def fast_feedforward_block(nc, dram, X):
    with ExitStack() as ctx:
        def flat(name):
            return ctx.enter_context(nc.sbuf_tensor(name, [128, SEQS * T], F32))

        XN, Q, K, V = flat("b_XN"), flat("b_Q"), flat("b_K"), flat("b_V")
        standardise(nc, dram, X, XN)
        fast_feedforwards(nc, dram, [("q", XN, Q), ("k", XN, K), ("v", XN, V)], ACT.Relu)
        leaf_attention(nc, dram, XN, Q, K, V)
        fast_feedforwards(nc, dram, [("f", XN, Q)], ACT.Gelu)
        add_and_norm(nc, X, XN, Q, "l")


def layouts_b(i):
    out = {}
    for m in "qkvf":
        a = lambda n: np.asarray(i[f"L0_ffn_{m}_{n}"])
        nw = np.zeros((LEAVES, D), np.float32)
        nw[:LEAVES - 1] = a("nw")
        nb = np.zeros(LEAVES, np.float32)
        nb[:LEAVES - 1] = a("nb")
        out[m + "_nw"] = nw.T
        out[m + "_nb"] = nb.reshape(2, 128).T
        out[m + "_w1"] = a("w1").transpose(1, 0, 2).reshape(D, LEAVES * LW)
        out[m + "_b1"] = a("b1").reshape(CH, 128).T
        out[m + "_w2"] = a("w2").reshape(CH, 128, D).transpose(1, 0, 2)
        out[m + "_b2"] = a("b2").reshape(2, 128, D).transpose(1, 0, 2)
    return out


def constants_b():
    paths = np.zeros((LEAVES, LEAVES), np.float32)
    for leaf in range(LEAVES):
        node = 0
        for level in range(DEPTH):
            right = (leaf >> (DEPTH - 1 - level)) & 1
            paths[node, leaf] = 1.0 if right else -1.0
            node = 2 * node + 1 + right
    rights = (paths > 0).sum(0).astype(np.float32)
    number = np.arange(LEAVES, dtype=np.float32).reshape(2, 128)
    return {"paths": paths.reshape(2, 128, LEAVES).transpose(1, 0, 2).astype(mybir.dt.np(BF16)),
            "rights": rights.reshape(2, 128).T,
            "leaf_no": np.repeat(number.T[:, :, None], 128, 2),
            "chunk_leaf": (8 * np.arange(CH)[None, :] + np.arange(128)[:, None] // LW).astype(np.float32),
            "ident": np.eye(128, dtype=np.float32)}




def gated_scan(nc, dram, X, X0):
    with ExitStack() as ctx:
        def sb(name, shape, dt=F32):
            return ctx.enter_context(nc.sbuf_tensor("c_" + name, shape, dt))

        W = sb("W", [128, 3, 128])
        bias = sb("bias", [128, 3])
        mean_w = sb("mean_w", [128, 128])
        eps = sb("eps", [128, 1])
        gate = sb("gate", [128, 3, T])
        u = sb("u", [128, T])
        a = sb("a", [128, T])
        h = sb("h", [128, T])
        r = sb("r", [128, 2, T])
        xc = sb("xc", [128, T])
        xsq = sb("xsq", [128, T])
        std = sb("std", [128, T])
        rstd = sb("rstd", [128, T])
        ps = ctx.enter_context(nc.psum_tensor("c_gates", [128, 3, 512], F32))
        ps_mean = ctx.enter_context(nc.psum_tensor("c_mean", [128, 512], F32))
        ps_var = ctx.enter_context(nc.psum_tensor("c_var", [128, 512], F32))
        names = """w_in memset_done gates_done gate_ready u_ready a_ready h_ready r_ready mean_done xc_ready
            xsq_ready var_done std_ready rstd_ready x_ready copied gate""".split()
        s = {n: ctx.enter_context(nc.semaphore("c_" + n)) for n in names}
        ctx.callback(clear_semaphores, nc, s)

        def seq_wait(eng, name, seq, per=1, more=None):
            eng.wait_ge(s[name], seq * per + (per if more is None else more))

        block = ctx.enter_context(nc.Block())

        def run(eng, slot):
            slot(0, 0, True, False, False)
            slot(1, 1, True, True, False)
            with eng.Fori(1, SEQS // 2) as half:
                slot(half * 2, 0, True, True, True)
                slot(half * 2 + 1, 1, True, True, True)
            slot(SEQS, 0, False, True, True)

        @block.sync
        def _(sp):
            sp.dma_start(W[:], dram["C_W"]).then_inc(s["w_in"], 16)
            sp.dma_start(bias[:], dram["C_bias"]).then_inc(s["w_in"], 16)

        @block.tensor
        def _(pe):
            pe.wait_ge(s["w_in"], 32)
            pe.wait_ge(s["memset_done"], 2)

            def slot(k, par, cur, prev, pprev):
                p = k - 1
                if cur:
                    if prev:
                        seq_wait(pe, "gate_ready", p, 3)
                    for n in range(3):
                        nc.tensor.matmul(ps[:, n, 0:T], W[:, n, :], X[:, k, PAD:], start=True, stop=True)\
                            .then_inc(s["gates_done"], 1)
                if prev:
                    seq_wait(pe, "r_ready", p)
                    if pprev:
                        seq_wait(pe, "xc_ready", k - 2)
                    nc.tensor.matmul(ps_mean[:, 0:T], mean_w[:], r[:, 1 - par, :], start=True, stop=True).then_inc(s["mean_done"], 1)
                    seq_wait(pe, "xsq_ready", p)
                    if pprev:
                        seq_wait(pe, "std_ready", k - 2)
                    nc.tensor.matmul(ps_var[:, 0:T], mean_w[:], xsq[:], start=True, stop=True).then_inc(s["var_done"], 1)

            run(pe, slot)

        @block.scalar
        def _(act):
            act.wait_ge(s["memset_done"], 2)
            act.wait_ge(s["w_in"], 32)

            def slot(k, par, cur, prev, pprev):
                p = k - 1
                if cur:
                    if prev:
                        seq_wait(act, "a_ready", p)
                        seq_wait(act, "u_ready", p)
                    for n in range(3):
                        seq_wait(act, "gates_done", k, 3, n + 1)
                        nc.scalar.activation(gate[:, n, :], ps[:, n, 0:T], (ACT.Sigmoid, ACT.Tanh, ACT.Sigmoid)[n],
                                             bias=bias[:, n:n + 1]).then_inc(s["gate_ready"], 1)
                if prev:
                    seq_wait(act, "var_done", p)
                    if pprev:
                        seq_wait(act, "rstd_ready", k - 2)
                    nc.scalar.activation(std[:], ps_var[:, 0:T], ACT.Sqrt, bias=eps[:, 0:1]).then_inc(s["std_ready"], 1)

            run(act, slot)

        @block.gpsimd
        def _(pool):
            nc.gpsimd.memset(eps[:], 1e-5).then_inc(s["memset_done"], 1)
            nc.gpsimd.memset(mean_w[:], 1.0 / 128).then_inc(s["memset_done"], 1)

            def slot(k, par, cur, prev, pprev):
                p = k - 1
                if prev:
                    seq_wait(pool, "xc_ready", p)
                    if pprev:
                        seq_wait(pool, "var_done", k - 2)
                    nc.gpsimd.tensor_tensor(xsq[:], xc[:], xc[:], ALU.mult).then_inc(s["xsq_ready"], 1)
                    seq_wait(pool, "x_ready", p)
                    seq_wait(pool, "r_ready", p)
                    pool.sem_inc(s["gate"], 1)
                    nc.gpsimd.tensor_copy(X[:, p, PAD:], X0[:, bass.ds(p * T, T)]).then_inc(s["copied"], 1)

            run(pool, slot)

        @block.vector
        def _(dve):
            def slot(k, par, cur, prev, pprev):
                p = k - 1
                if prev:
                    seq_wait(dve, "mean_done", p)
                    if pprev:
                        seq_wait(dve, "x_ready", k - 2)
                    nc.vector.tensor_tensor(xc[:], r[:, 1 - par, :], ps_mean[:, 0:T], ALU.subtract).then_inc(s["xc_ready"], 1)
                if cur:
                    seq_wait(dve, "gate_ready", k, 3)
                    if prev:
                        seq_wait(dve, "h_ready", p)
                    nc.vector.tensor_tensor(u[:], gate[:, 0, :], gate[:, 1, :], ALU.mult).then_inc(s["u_ready"], 1)
                    nc.vector.tensor_scalar(a[:], gate[:, 2, :], 0.998, 0.001, ALU.mult, ALU.add).then_inc(s["a_ready"], 1)
                    seq_wait(dve, "u_ready", k)
                    seq_wait(dve, "a_ready", k)
                    if prev:
                        seq_wait(dve, "r_ready", p)
                    nc.vector.tensor_tensor_scan(h[:], a[:], u[:], 0.0, ALU.mult, ALU.add).then_inc(s["h_ready"], 1)
                    seq_wait(dve, "h_ready", k)
                    if pprev:
                        seq_wait(dve, "mean_done", k - 2)
                    nc.vector.tensor_tensor(r[:, par, :], X[:, k, PAD:], h[:], ALU.add).then_inc(s["r_ready"], 1)
                if prev:
                    seq_wait(dve, "std_ready", p)
                    nc.vector.reciprocal(rstd[:], std[:]).then_inc(s["rstd_ready"], 1)
                    seq_wait(dve, "rstd_ready", p)
                    nc.vector.tensor_tensor(X0[:, bass.ds(p * T, T)], xc[:], rstd[:], ALU.mult).then_inc(s["x_ready"], 1)

            run(dve, slot)


def layouts_c(i):
    return {"C_W": np.stack([np.asarray(i["L1_attn_W" + n]).T for n in "gvd"], 1),
            "C_bias": np.stack([np.asarray(i["L1_attn_b" + n]) for n in "gvd"], 1)}


LAYERS = 6
HEADS = 16
DH = 64
WIN = 32
INNER = HEADS * DH
HP = HEADS // 2
HID = 341
HCH = 3
HROWS = [128, 128, HID - 256]
HEAD_COLS = HP * DH


def local_attention_layers(nc, dram, X, XM):
    with ExitStack() as ctx:
        def sb(name, shape):
            return ctx.enter_context(nc.sbuf_tensor(name, shape, F32))

        def sem(name):
            return ctx.enter_context(nc.semaphore("d_" + name))

        Wqk = sb("d_Wqk", [128, 2 * INNER])
        Wv = sb("d_Wv", [128, 2, HEAD_COLS])
        Wo = sb("d_Wo", [128, HP, 128])
        W1 = sb("d_W1", [128, 2 * HID])
        W2 = sb("d_W2", [128, HCH, 128])
        vecs = sb("d_vecs", [128, 9])
        qkscale = sb("d_qkscale", [128, 2, DH])
        rot_const = sb("d_rot_const", [128, 2, 2, 2, DH])
        rot = sb("d_rot", [128, 2, 2, 2, DH])
        mask = sb("d_mask", [128, 2, DH])
        ident = sb("d_ident", [128, 128])
        mean_w = sb("d_mean_w", [128, 128])
        eps = sb("d_eps", [128, 1])
        xs = sb("d_xs", [128, 2, WIN + 128])
        raw = sb("d_raw", [128, 2 * INNER])
        sq = sb("d_sq", [128, 2, INNER])
        rs = sb("d_rs", [128, 2 * INNER])
        rc = sb("d_rc", [128, 2 * INNER])
        ss = sb("d_ss", [128, 2, HEADS])
        length = sb("d_length", [128, 2, HEADS])
        norm = sb("d_norm", [128, 2, HEADS])
        inv = sb("d_inv", [128, 2, HEADS])
        QT = sb("d_QT", [128, HP, 128])
        KT = sb("d_KT", [128, HP, WIN + 256])
        sm = sb("d_sm", [128, 2, HP, DH])
        sc = sb("d_sc", [128, 2, HP, DH])
        mx = sb("d_mx", [128, HEADS])
        P = sb("d_P", [128, HP, 2, DH])
        den = sb("d_den", [128, HEADS])
        rden = sb("d_rden", [128, HEADS])
        PT = sb("d_PT", [128, HP, 128])
        VP = sb("d_VP", [128, 4, HEAD_COLS])
        On = sb("d_On", [128, HP, 2, DH])
        OT = sb("d_OT", [128, HP, 128])
        xs2 = sb("d_xs2", [128, 128])
        xc = sb("d_xc", [128, 128])
        xsq = sb("d_xsq", [128, 128])
        std = sb("d_std", [128, 128])
        rstd = sb("d_rstd", [128, 128])
        xh = sb("d_xh", [128, 128])
        xn = sb("d_xn", [128, 128])
        G = sb("d_G", [128, HCH, 128])
        H = sb("d_H", [128, HCH, 128])
        bank = [ctx.enter_context(nc.psum_tensor(f"d_bank{i}", [128, 2, 512], F32)) for i in range(3)]
        b6 = ctx.enter_context(nc.psum_tensor("d_b6", [128, 512], F32))
        b7 = ctx.enter_context(nc.psum_tensor("d_b7", [128, 512], F32))
        ps_k, ps_q, ps_a = bank

        names = """wqk_in wv_in wo_in w1_in w2_in vecs_in qks_in consts_in
            memset_done tables_done xs_ready
            qk_done raw_ready sq_ready ss_ready length_ready norm_ready inv_ready rden_ready rstd_ready rs_ready rc_ready rc_added rc_final
            t_done qt_ready kt_ready s_done sm_ready mx_ready sc_ready p_ready den_ready
            pt_done pt_ready vp_done vp_ready o_done on_ready ot_done ot_ready
            proj_done xm_ready xs2_ready mean_done xc_ready xsq_ready var_done std_ready xh_ready
            xn_ready up_done gelu_ready h_ready down_done x_ready gate_pe gate_act gate_pool""".split()
        s = {n: sem(n) for n in names}
        ctx.callback(clear_semaphores, nc, s)

        def raise_one(name):
            return s[name], 1

        def tile_wait(eng, name, tile, per=1, more=None):
            more = per if more is None else more
            eng.wait_ge(s[name], tile * per + more)

        w_dram = dram["Wqkv"]
        block = ctx.enter_context(nc.Block())

        def columns(tile_buf, b, par, ahead=0, shift=0):
            lo = PAD + 128 * par - ahead - shift
            return tile_buf[:, b, lo:lo + 128 + ahead]

        def run(eng, slot):
            def pair(l, b, first_layer, start):
                k = l * 32 + b * 2
                slot(k, 0, b, True, not start, not start, l, first_layer, layer_start(b, 0))
                slot(k + 1, 1, b, True, True, not start, l, first_layer, layer_start(b, 1))

            def layer_start(b, par):
                return isinstance(b, int) and b == 0 and par == 0

            pair(0, 0, True, True)
            with eng.Fori(1, SEQS) as b:
                pair(0, b, True, False)
            with eng.Fori(1, LAYERS) as l:
                pair(l, 0, False, False)
                with eng.Fori(1, SEQS) as b:
                    pair(l, b, False, False)
            last = LAYERS * 32
            slot(last, 0, SEQS, False, True, True, LAYERS, False, False)
            slot(last + 1, 1, SEQS, False, False, True, LAYERS, False, False)

        def f_place(b, par):
            return (SEQS - 1 if isinstance(b, int) and b == 0 else b - 1), par

        def p_place(b, par):
            return (b, 0) if par == 1 else ((SEQS - 1 if isinstance(b, int) and b == 0 else b - 1), 1)

        @block.sync
        def _(sp):
            sp.dma_start(ident[:], dram["ident"]).then_inc(s["consts_in"], 16)
            sp.dma_start(rot_const[:], dram["rotary"]).then_inc(s["consts_in"], 16)
            sp.dma_start(mask[:], dram["window_mask"]).then_inc(s["consts_in"], 16)

            def load(l):
                def layer(ap):
                    return ap[bass.ds(l, 1)]
                if not isinstance(l, int):
                    sp.wait_ge(s["tables_done"], 8 * l)
                sp.dma_start(qkscale[:], layer(dram["qk_scale"]).rearrange("o a d -> (o a d)").partition_broadcast(128)
                             .rearrange("p (a d) -> p a d", a=2)).then_inc(s["qks_in"], 16)
                if not isinstance(l, int):
                    sp.wait_ge(s["qk_done"], 64 * l)
                sp.dma_start(Wqk[:], layer(w_dram)[:, :, 0:2, :].rearrange("o p a n -> p (o a n)")).then_inc(s["wqk_in"], 16)
                if not isinstance(l, int):
                    sp.wait_ge(s["vp_done"], 128 * l)
                sp.dma_start(Wv[:, 0, :], layer(dram["Wv"])[:, :, 0, :].rearrange("o p n -> p (o n)")).then_inc(s["wv_in"], 16)
                sp.dma_start(Wv[:, 1, :], layer(dram["Wv"])[:, :, 1, :].rearrange("o p n -> p (o n)")).then_inc(s["wv_in"], 16)
                if not isinstance(l, int):
                    sp.wait_ge(s["proj_done"], 32 * l)
                sp.dma_start(Wo[:], layer(dram["Wo"]).rearrange("o (h p) n -> p (o h) n", p=128)).then_inc(s["wo_in"], 16)
                if not isinstance(l, int):
                    sp.wait_ge(s["down_done"], 32 * l)
                    sp.wait_ge(s["x_ready"], 32 * l)
                sp.dma_start(W1[:], layer(dram["W1"]).rearrange("o p n -> p (o n)")).then_inc(s["w1_in"], 16)
                sp.dma_start(W2[:], layer(dram["W2"]).rearrange("o p c n -> p (o c) n")).then_inc(s["w2_in"], 16)
                sp.dma_start(vecs[:], layer(dram["vecs"]).rearrange("o p n -> p (o n)")).then_inc(s["vecs_in"], 16)

            load(0)
            with sp.Fori(1, LAYERS) as l:
                load(l)

        @block.tensor
        def _(pe):
            pe.wait_ge(s["consts_in"], 48)
            pe.wait_ge(s["memset_done"], 5)

            def slot(k, par, b, cur, prev, ffn, l, first_layer, layer_start):
                p, f = k - 1, k - 2
                if prev:
                    tile_wait(pe, "qt_ready", p)
                    tile_wait(pe, "kt_ready", p)
                    tile_wait(pe, "ot_ready", p - 1) if ffn else None
                    pe.sem_inc(s["gate_pe"], 1)
                    at = 128 * (1 - par)
                    for hp in range(HP):
                        for odd in range(2):
                            rows = slice(64 * odd, 64 * odd + 64)
                            for w in range(4):
                                mm = nc.tensor.matmul(
                                    ps_a[WIN * w:WIN * w + WIN, odd, hp * DH:hp * DH + DH],
                                    QT[rows, hp, WIN * w:WIN * w + WIN],
                                    KT[rows, hp, at + WIN * w:at + WIN * w + 2 * WIN], start=True, stop=True)
                    mm.then_inc(*raise_one("s_done"))
                if cur:
                    if layer_start:
                        pe.wait_ge(s["wqk_in"], 16 * l + 16)
                    tile_wait(pe, "xs_ready", k, 2)
                    if prev:
                        tile_wait(pe, "qt_ready", p)
                        tile_wait(pe, "kt_ready", p)
                    for half, ps in ((0, ps_q), (1, ps_k)):
                        for j in range(2):
                            c = INNER * half + 512 * j
                            mm = nc.tensor.matmul(ps[:, j, :], xs[:, par, WIN:], Wqk[:, c:c + 512], start=True, stop=True)
                        mm.then_inc(*raise_one("qk_done"))
                if ffn:
                    tile_wait(pe, "xs2_ready", f, 2)
                    if f_before(f):
                        tile_wait(pe, "x_ready", f - 1)
                    nc.tensor.matmul(b6[:, 0:128], mean_w[:], xs2[:], start=True, stop=True).then_inc(*raise_one("mean_done"))
                if prev:
                    if (par == 1 and layer_one_before(b)):
                        pe.wait_ge(s["wv_in"], 32 * l + 32)
                    for w in range(4):
                        out = (b7, ps_a[:, 0, :], ps_a[:, 1, :], b7)[w]
                        if w == 0 and ffn:
                            tile_wait(pe, "xm_ready", p - 1)
                        if w == 1:
                            tile_wait(pe, "sm_ready", p)
                        if w == 3:
                            tile_wait(pe, "vp_ready", p, 4, 1)
                        for odd in range(2):
                            mm = nc.tensor.matmul(out[64 * odd:64 * odd + 64, :],
                                                  xs[:, 1 - par, WIN * w:WIN * w + 2 * WIN], Wv[:, odd, :], start=True, stop=True)
                        mm.then_inc(*raise_one("vp_done"))
                if ffn:
                    tile_wait(pe, "xsq_ready", f)
                    nc.tensor.matmul(b6[:, 0:128], mean_w[:], xsq[:], start=True, stop=True).then_inc(*raise_one("var_done"))
                if prev:
                    tile_wait(pe, "p_ready", p)
                    tile_wait(pe, "vp_ready", p, 4, 3)
                    for hp in range(HP):
                        mm = nc.tensor.transpose(ps_a[:, hp // 4, (hp % 4) * 128:(hp % 4) * 128 + 128],
                                                 P[:, hp, :, :].rearrange("p a d -> p (a d)"), ident[:])
                    mm.then_inc(*raise_one("pt_done"))
                if ffn:
                    if needs_new_ffn_weights(b, par):
                        pe.wait_ge(s["w1_in"], 16 * l + 16)
                        pe.wait_ge(s["w2_in"], 16 * l + 16)
                    tile_wait(pe, "xn_ready", f)
                    if prev:
                        tile_wait(pe, "vp_ready", p, 4)
                    for side, ps in ((1, b7), (0, b6)):
                        for c in range(HCH):
                            at = HID * side + 128 * c
                            mm = nc.tensor.matmul(ps[0:HROWS[c], 128 * c:128 * c + 128], W1[:, at:at + HROWS[c]], xn[:],
                                                  start=True, stop=True)
                        mm.then_inc(*raise_one("up_done"))
                if prev:
                    tile_wait(pe, "pt_ready", p)
                    tile_wait(pe, "vp_ready", p, 4)
                    if cur:
                        tile_wait(pe, "raw_ready", k, 2)
                        tile_wait(pe, "sq_ready", k, 2)
                    pe.sem_inc(s["gate_pe"], 1)
                    for hp in range(HP):
                        for odd in range(2):
                            rows = slice(64 * odd, 64 * odd + 64)
                            for w in range(4):
                                mm = nc.tensor.matmul(
                                    ps_k[WIN * w:WIN * w + WIN, odd, hp * DH:hp * DH + DH],
                                    PT[rows, hp, WIN * w:WIN * w + WIN],
                                    VP[rows, w, hp * DH:hp * DH + DH], start=True, stop=True)
                    mm.then_inc(*raise_one("o_done"))
                if ffn:
                    tile_wait(pe, "h_ready", f, HCH)
                    for c in range(HCH):
                        mm = nc.tensor.matmul(b6[:, 0:128], W2[0:HROWS[c], c, :], H[0:HROWS[c], c, :],
                                              start=c == 0, stop=c == HCH - 1)
                    mm.then_inc(*raise_one("down_done"))
                if cur:
                    tile_wait(pe, "rc_final", k, 2, 1)
                    for hp in range(HP):
                        mm = nc.tensor.transpose(ps_q[:, hp // 4, (hp % 4) * 128:(hp % 4) * 128 + 128],
                                                 rc[:, hp * 128:hp * 128 + 128], ident[:])
                    mm.then_inc(*raise_one("t_done"))
                if prev:
                    tile_wait(pe, "on_ready", p)
                    for hp in range(HP):
                        mm = nc.tensor.transpose(ps_a[:, hp // 4, (hp % 4) * 128:(hp % 4) * 128 + 128],
                                                 On[:, hp, :, :].rearrange("p a d -> p (a d)"), ident[:])
                    mm.then_inc(*raise_one("ot_done"))
                if cur:
                    tile_wait(pe, "rc_final", k, 2)
                    for hp in range(HP):
                        mm = nc.tensor.transpose(ps_k[:, hp // 4, (hp % 4) * 128:(hp % 4) * 128 + 128],
                                                 rc[:, INNER + hp * 128:INNER + hp * 128 + 128], ident[:])
                    mm.then_inc(*raise_one("t_done"))
                if prev:
                    if par == 1 and layer_one_before(b):
                        pe.wait_ge(s["wo_in"], 16 * l + 16)
                    tile_wait(pe, "ot_ready", p)
                    if ffn:
                        tile_wait(pe, "gelu_ready", f, HCH)
                    for hp in range(HP):
                        mm = nc.tensor.matmul(b7[:, 0:128], Wo[:, hp, :], OT[:, hp, :], start=hp == 0, stop=hp == HP - 1)
                    mm.then_inc(*raise_one("proj_done"))

            def f_before(f):
                return not (isinstance(f, int) and f == 0)

            def layer_one_before(b):
                return isinstance(b, int) and b == 0

            def needs_new_ffn_weights(b, par):
                return not (isinstance(b, int) and b in (0, SEQS))

            run(pe, slot)

        @block.scalar
        def _(act):
            act.wait_ge(s["memset_done"], 5)

            def slot(k, par, b, cur, prev, ffn, l, first_layer, layer_start):
                p, f = k - 1, k - 2
                if cur:
                    for half, ps in ((0, ps_q), (1, ps_k)):
                        cols = slice(INNER * half, INNER * half + INNER)
                        flat = ps[:].rearrange("p a n -> p (a n)")
                        tile_wait(act, "qk_done", k, 2, half + 1)
                        if prev:
                            tile_wait(act, "rc_ready", p, 2, half + 1)
                            tile_wait(act, "rs_ready", p, 2, half + 1)
                        nc.scalar.activation(raw[:, cols], flat, ACT.Copy).then_inc(*raise_one("raw_ready"))
                        if prev:
                            tile_wait(act, "ss_ready", p, 2, half + 1)
                        nc.scalar.activation(sq[:, half, :], flat, ACT.Square).then_inc(*raise_one("sq_ready"))
                if prev:
                    tile_wait(act, "sc_ready", p)
                    if ffn:
                        tile_wait(act, "pt_done", p - 1)
                    for odd in range(2):
                        ins = nc.scalar.activation(P[:, :, odd, :], sc[:, odd, :, :], ACT.Exp, scale=8.0)
                    ins.then_inc(*raise_one("p_ready"))
                    for w in range(4):
                        tile_wait(act, "vp_done", p, 4, w + 1)
                        if w == 0 and ffn:
                            tile_wait(act, "o_done", p - 1)
                        src = (b7[:], ps_a[:, 0, :], ps_a[:, 1, :], b7[:])[w]
                        nc.scalar.activation(VP[:, w, :], src, ACT.Copy).then_inc(*raise_one("vp_ready"))
                if cur:
                    tile_wait(act, "ss_ready", k, 2)
                    nc.scalar.activation(length[:], ss[:], ACT.Sqrt).then_inc(*raise_one("length_ready"))
                if ffn:
                    tile_wait(act, "var_done", f)
                    nc.scalar.activation(std[:], b6[:, 0:128], ACT.Sqrt, bias=eps[:, 0:1]).then_inc(*raise_one("std_ready"))
                if prev:
                    tile_wait(act, "pt_done", p)
                    if ffn:
                        tile_wait(act, "o_done", p - 1)
                    nc.scalar.activation(PT[:].rearrange("p h t -> p (h t)"), ps_a[:].rearrange("p a n -> p (a n)"), ACT.Copy)\
                        .then_inc(*raise_one("pt_ready"))
                if ffn:
                    tile_wait(act, "up_done", f, 2, 1)
                    if f_before(f):
                        tile_wait(act, "h_ready", f - 1, HCH)
                    if not (isinstance(b, int) and b in (0, SEQS)):
                        act.wait_ge(s["vecs_in"], 16 * l + 16)
                    for c in range(HCH):
                        r = HROWS[c]
                        nc.scalar.activation(G[0:r, c, :], b7[0:r, 128 * c:128 * c + 128], ACT.Gelu,
                                             bias=vecs[0:r, 5 + c:6 + c]).then_inc(*raise_one("gelu_ready"))
                if cur:
                    tile_wait(act, "t_done", k, 2, 1)
                    nc.scalar.activation(QT[:].rearrange("p h t -> p (h t)"), ps_q[:].rearrange("p a n -> p (a n)"), ACT.Copy)\
                        .then_inc(*raise_one("qt_ready"))
                if prev:
                    tile_wait(act, "ot_done", p)
                    if ffn:
                        tile_wait(act, "proj_done", p - 1)
                    nc.scalar.activation(OT[:].rearrange("p h t -> p (h t)"), ps_a[:].rearrange("p a n -> p (a n)"), ACT.Copy)\
                        .then_inc(*raise_one("ot_ready"))
                if cur:
                    tile_wait(act, "t_done", k, 2)
                    at = WIN + 128 * par
                    nc.scalar.activation(KT[:, :, at:at + 128], ps_k[:].rearrange("p a (h t) -> p (a h) t", t=128), ACT.Copy)\
                        .then_inc(*raise_one("kt_ready"))

            def f_before(f):
                return not (isinstance(f, int) and f == 0)

            run(act, slot)

        @block.gpsimd
        def _(pool):
            nc.gpsimd.memset(eps[:], 1e-5).then_inc(*raise_one("memset_done"))
            nc.gpsimd.memset(mean_w[:], 1.0 / 128).then_inc(*raise_one("memset_done"))
            nc.gpsimd.memset(KT[:, :, 0:WIN], 0.0).then_inc(*raise_one("memset_done"))
            nc.gpsimd.memset(X[:, :, 0:PAD], 0.0).then_inc(*raise_one("memset_done"))
            nc.gpsimd.memset(XM[:, :, 0:PAD], 0.0).then_inc(*raise_one("memset_done"))
            pool.wait_ge(s["memset_done"], 5)

            def slot(k, par, b, cur, prev, ffn, l, first_layer, layer_start):
                p, f = k - 1, k - 2
                if cur:
                    if not first_layer:
                        tile_wait(pool, "x_ready", k - 32)
                    if ffn:
                        tile_wait(pool, "vp_done", f, 4)
                    if ffn:
                        tile_wait(pool, "xs2_ready", f, 2)
                    elif prev:
                        tile_wait(pool, "rs_ready", p, 2)
                    pool.sem_inc(s["gate_pool"], 1)
                    nc.gpsimd.tensor_copy(xs[0:64, par, :], columns(X, b, par, WIN)[0:64]).then_inc(*raise_one("xs_ready"))
                    tile_wait(pool, "xs_ready", k, 2, 1)
                    pool.sem_inc(s["gate_pool"], 1)
                    nc.gpsimd.tensor_copy(xs[64:128, par, :], columns(X, b, par, WIN, 1)[64:128]).then_inc(*raise_one("xs_ready"))
                    tile_wait(pool, "xs_ready", k, 2)
                    pool.sem_inc(s["gate_pool"], 1)
                if prev:
                    if not cur:
                        tile_wait(pool, "xs2_ready", f, 2)
                    tile_wait(pool, "mx_ready", p)
                    if ffn:
                        tile_wait(pool, "p_ready", p - 1)
                    nc.gpsimd.tensor_tensor(sc[:].rearrange("p a h n -> p (a h) n"), sm[:].rearrange("p a h n -> p (a h) n"),
                                            mx[:].unsqueeze(2).to_broadcast([128, HEADS, DH]), ALU.subtract)\
                        .then_inc(*raise_one("sc_ready"))
                if ffn:
                    tile_wait(pool, "xc_ready", f)
                    if f_before(f):
                        tile_wait(pool, "var_done", f - 1)
                    nc.gpsimd.tensor_tensor(xsq[:], xc[:], xc[:], ALU.mult).then_inc(*raise_one("xsq_ready"))
                if cur:
                    for half in range(2):
                        cols = slice(INNER * half, INNER * half + INNER)
                        tile_wait(pool, "raw_ready", k, 2, half + 1)
                        if layer_start:
                            pool.wait_ge(s["tables_done"], 8 * l + 8)
                        if prev:
                            tile_wait(pool, "rc_added", p, 4, 2 * half + 2)
                        nc.gpsimd.tensor_tensor(rs[:, cols].rearrange("p (h d) -> p h d", d=DH),
                                                raw[:, cols].rearrange("p (h d) -> p h d", d=DH),
                                                rot[:, par, half, 1, :].unsqueeze(1).to_broadcast([128, HEADS, DH]), ALU.mult)\
                            .then_inc(*raise_one("rs_ready"))
                if prev:
                    tile_wait(pool, "xm_ready", p)
                    if ffn:
                        tile_wait(pool, "xc_ready", f)
                    if cur:
                        tile_wait(pool, "rs_ready", k, 2)
                    else:
                        tile_wait(pool, "sc_ready", p)
                        tile_wait(pool, "xsq_ready", f)
                    pool.sem_inc(s["gate_pool"], 1)
                    pb, pp = p_place(b, par)
                    nc.gpsimd.tensor_copy(xs2[0:64, :], columns(XM, pb, pp)[0:64]).then_inc(*raise_one("xs2_ready"))
                    tile_wait(pool, "xs2_ready", p, 2, 1)
                    pool.sem_inc(s["gate_pool"], 1)
                    nc.gpsimd.tensor_copy(xs2[64:128, :], columns(XM, pb, pp, 0, 1)[64:128]).then_inc(*raise_one("xs2_ready"))

            def f_before(f):
                return not (isinstance(f, int) and f == 0)

            run(pool, slot)

        @block.vector
        def _(dve):
            dve.wait_ge(s["consts_in"], 48)
            dve.wait_ge(s["memset_done"], 5)

            def tables(l):
                dve.wait_ge(s["qks_in"], 16 * l + 16)
                if not isinstance(l, int):
                    dve.wait_ge(s["rs_ready"], 64 * l)
                for par in range(2):
                    for half in range(2):
                        for cs in range(2):
                            nc.vector.tensor_tensor(rot[:, par, half, cs, :], rot_const[:, par, half, cs, :],
                                                    qkscale[:, half, :], ALU.mult).then_inc(*raise_one("tables_done"))
                dve.wait_ge(s["tables_done"], 8 * l + 8)

            def squares(k, half):
                tile_wait(dve, "sq_ready", k, 2, half + 1)
                nc.vector.tensor_reduce(ss[:, half, :], sq[:, half, :].rearrange("p (h d) -> p h d", d=DH), AX_X, ALU.add)\
                    .then_inc(*raise_one("ss_ready"))

            def rotate(k, par, half, prev):
                cols = slice(INNER * half, INNER * half + INNER)
                heads = lambda t: t[:, cols].rearrange("p (h d) -> p h d", d=DH)
                halves = lambda t: t[:, cols].rearrange("p (h a d) -> p h a d", a=2, d=DH // 2)
                if prev:
                    tile_wait(dve, "t_done", k - 1, 2, half + 1)
                nc.vector.tensor_tensor(heads(rc), heads(raw), rot[:, par, half, 0, :].unsqueeze(1).to_broadcast([128, HEADS, DH]),
                                        ALU.mult).then_inc(*raise_one("rc_ready"))
                tile_wait(dve, "rc_ready", k, 2, half + 1)
                tile_wait(dve, "rs_ready", k, 2, half + 1)
                for a in range(2):
                    nc.vector.tensor_tensor(halves(rc)[:, :, a, :], halves(rc)[:, :, a, :], halves(rs)[:, :, 1 - a, :], ALU.add)\
                        .then_inc(*raise_one("rc_added"))

            def unit_length(k, half):
                cols = slice(INNER * half, INNER * half + INNER)
                heads = rc[:, cols].rearrange("p (h d) -> p h d", d=DH)
                tile_wait(dve, "inv_ready", k)
                tile_wait(dve, "rc_added", k, 4, 2 * half + 2)
                nc.vector.tensor_tensor(heads, heads, inv[:, half, :].unsqueeze(2).to_broadcast([128, HEADS, DH]), ALU.mult)\
                    .then_inc(*raise_one("rc_final"))

            def lengths(k):
                tile_wait(dve, "length_ready", k)
                nc.vector.tensor_scalar(norm[:], length[:], 1e-12, None, ALU.max).then_inc(*raise_one("norm_ready"))
                tile_wait(dve, "norm_ready", k)
                nc.vector.reciprocal(inv[:], norm[:]).then_inc(*raise_one("inv_ready"))

            def slot(k, par, b, cur, prev, ffn, l, first_layer, layer_start):
                p, f = k - 1, k - 2
                if layer_start:
                    tables(l)
                if prev:
                    tile_wait(dve, "s_done", p)
                    if ffn:
                        tile_wait(dve, "sc_ready", p - 1)
                    nc.vector.tensor_tensor(sm[:].rearrange("p a h n -> p (a h) n"), ps_a[:].rearrange("p a (h n) -> p (a h) n", n=DH),
                                            mask[:, 1 - par, :].unsqueeze(1).to_broadcast([128, HEADS, DH]), ALU.add)\
                        .then_inc(*raise_one("sm_ready"))
                    tile_wait(dve, "sm_ready", p)
                    nc.vector.tensor_reduce(mx[:], sm[:].rearrange("p a h n -> p (a h) n"), AX_X, ALU.max)\
                        .then_inc(*raise_one("mx_ready"))
                if ffn:
                    tile_wait(dve, "mean_done", f)
                    if f_before(f):
                        tile_wait(dve, "xh_ready", f - 1)
                    nc.vector.tensor_tensor(xc[:], xs2[:], b6[:, 0:128], ALU.subtract).then_inc(*raise_one("xc_ready"))
                if cur:
                    squares(k, 0)
                    squares(k, 1)
                    rotate(k, par, 0, prev)
                if prev:
                    tile_wait(dve, "p_ready", p)
                    nc.vector.tensor_reduce(den[:], P[:].rearrange("p h a d -> p (h a) d"), AX_X, ALU.add)\
                        .then_inc(*raise_one("den_ready"))
                    tile_wait(dve, "den_ready", p)
                    nc.vector.reciprocal(rden[:], den[:]).then_inc(*raise_one("rden_ready"))
                if cur:
                    lengths(k)
                    unit_length(k, 0)
                if ffn:
                    tile_wait(dve, "std_ready", f)
                    nc.vector.reciprocal(rstd[:], std[:]).then_inc(*raise_one("rstd_ready"))
                    tile_wait(dve, "rstd_ready", f)
                    nc.vector.tensor_tensor(xh[:], xc[:], rstd[:], ALU.mult).then_inc(*raise_one("xh_ready"))
                    tile_wait(dve, "xh_ready", f)
                    if not (isinstance(b, int) and b in (0, SEQS)):
                        dve.wait_ge(s["vecs_in"], 16 * l + 16)
                    if f_before(f):
                        tile_wait(dve, "up_done", f - 1, 2)
                    nc.vector.tensor_scalar(xn[:], xh[:], vecs[:, 0:1], vecs[:, 1:2], ALU.mult, ALU.add).then_inc(*raise_one("xn_ready"))
                if cur:
                    rotate(k, par, 1, prev)
                    unit_length(k, 1)
                if ffn:
                    tile_wait(dve, "up_done", f, 2)
                    if f_before(f):
                        tile_wait(dve, "down_done", f - 1)
                    for c in range(HCH):
                        r = HROWS[c]
                        tile_wait(dve, "gelu_ready", f, HCH, c + 1)
                        nc.vector.scalar_tensor_tensor(H[0:r, c, :], b6[0:r, 128 * c:128 * c + 128], vecs[0:r, 2 + c:3 + c],
                                                       G[0:r, c, :], ALU.add, ALU.mult).then_inc(*raise_one("h_ready"))
                if prev:
                    tile_wait(dve, "o_done", p)
                    tile_wait(dve, "rden_ready", p)
                    if ffn:
                        tile_wait(dve, "ot_done", p - 1)
                    nc.vector.tensor_tensor(On[:].rearrange("p h a d -> p a h d"), ps_k[:].rearrange("p a (h d) -> p a h d", d=DH),
                                            rden[:].rearrange("p (h a) -> p a h", a=2).unsqueeze(3).to_broadcast([128, 2, HP, DH]),
                                            ALU.mult).then_inc(*raise_one("on_ready"))
                if ffn:
                    fb, fp = f_place(b, par)
                    tile_wait(dve, "down_done", f)
                    tile_wait(dve, "xm_ready", f)
                    nc.vector.scalar_tensor_tensor(columns(X, fb, fp), b6[:, 0:128], vecs[:, 8:9],
                                                   columns(XM, fb, fp), ALU.add, ALU.add).then_inc(*raise_one("x_ready"))
                if prev:
                    pb, pp = p_place(b, par)
                    tile_wait(dve, "proj_done", p)
                    nc.vector.tensor_tensor(columns(XM, pb, pp), columns(X, pb, pp), b7[:, 0:128], ALU.add)\
                        .then_inc(*raise_one("xm_ready"))

            def f_before(f):
                return not (isinstance(f, int) and f == 0)

            run(dve, slot)


def constants():
    half = np.arange(0, DH, 2, dtype=np.float32)
    inv_freq = (np.float32(1.0) / np.float32(10000.0) ** (half / np.float32(DH))).astype(np.float32)
    t = np.arange(T, dtype=np.float32)
    freqs = t[:, None] * inv_freq[None, :]
    freqs = np.concatenate([freqs, freqs], -1)
    base = (half + np.float32(0.4 * DH)) / np.float32(1.4 * DH)
    power = (t - T // 2) / np.float32(WIN // 2)
    scale = base[None, :] ** power[:, None]
    scale = np.concatenate([scale, scale], -1).astype(np.float32)
    cos, sin = np.cos(freqs), np.sin(freqs)
    sign = np.where(np.arange(DH) < DH // 2, 1.0, -1.0).astype(np.float32)
    rotary = np.zeros((128, 2, 2, 2, DH), np.float32)
    for par in range(2):
        rows = slice(128 * par, 128 * par + 128)
        for half_, s in ((0, scale), (1, np.float32(1.0) / scale)):
            rotary[:, par, half_, 0] = cos[rows] * s[rows]
            rotary[:, par, half_, 1] = sin[rows] * sign * s[rows]
    query = np.arange(128)[:, None] % WIN
    slot = np.arange(2 * WIN)[None, :]
    seen = (slot >= query) & (slot <= query + WIN)
    first = seen & ((np.arange(128)[:, None] >= WIN) | (slot >= WIN))
    mask = np.where(np.stack([first, seen], 1), 0.0, -1e30).astype(np.float32)
    return {"ident": np.eye(128, dtype=np.float32), "rotary": rotary, "window_mask": mask}


def layouts_d(i):
    a = lambda n: np.asarray(i["L1_ffn_" + n])
    out = {"Wqkv": a("Wqkv").reshape(LAYERS, D, 3, INNER)}
    out["Wv"] = np.ascontiguousarray(a("Wqkv").reshape(LAYERS, D, 3, HP, 2, DH)[:, :, 2].transpose(0, 1, 3, 2, 4)
                                     ).reshape(LAYERS, D, 2, HEAD_COLS)
    out["qk_scale"] = np.stack([a("q_scale"), a("k_scale")], 1)
    out["Wo"] = a("Wo")
    out["W1"] = a("W1")
    w2 = np.zeros((LAYERS, HCH * 128, D), np.float32)
    w2[:, :HID] = a("W2")
    out["W2"] = np.ascontiguousarray(w2.reshape(LAYERS, HCH, 128, D).transpose(0, 2, 1, 3))
    b1 = np.zeros((LAYERS, 2, HCH * 128), np.float32)
    b1[:, :, :HID] = a("b1").reshape(LAYERS, 2, HID)
    cols = [a("ln_g"), a("ln_b")] + [b1[:, s, 128 * c:128 * c + 128] for s in range(2) for c in range(HCH)] + [a("b2")]
    out["vecs"] = np.stack(cols, 2)
    return out


def build(nc, dram, out):
    with ExitStack() as ctx:
        X = ctx.enter_context(nc.sbuf_tensor("X", [128, SEQS, STRIDE], F32))
        s_in = ctx.enter_context(nc.semaphore("x_in"))
        s_out = ctx.enter_context(nc.semaphore("x_out"))
        with nc.Block() as block:
            @block.sync
            def _(sp):
                sp.dma_start(X[:, :, PAD:], dram["x"].rearrange("d (b t) -> d b t", t=T)).then_inc(s_in, 16)
                sp.wait_ge(s_in, 16)
        causal_attention(nc, dram, X)
        fast_feedforward_block(nc, dram, X)
        X0 = ctx.enter_context(nc.sbuf_tensor("X0", [128, SEQS * T], F32))
        gated_scan(nc, dram, X, X0)
        with ExitStack() as inner:
            XM = inner.enter_context(nc.sbuf_tensor("XM", [128, SEQS, STRIDE], F32))
            local_attention_layers(nc, dram, X, XM)
        add_and_norm(nc, X, X0, None, "o")
        with nc.Block() as block:
            @block.sync
            def _(sp):
                sp.dma_start(out.rearrange("d (b t) -> d b t", t=T), X[:, :, PAD:]).then_inc(s_out, 16)
                sp.wait_ge(s_out, 16)


def kernel(**inputs):
    import concourse.bacc as _bacc
    from concourse.bass_utils import run_bass_kernel_spmd as _run

    nc = _bacc.Bacc("TRN2", target_bir_lowering=False, num_devices=1)
    arrays = {"x": np.asarray(inputs["L0_attn_x"]).reshape(SEQS * T, D).T}
    for part in (constants(), constants_a(), constants_b(), layouts_a(inputs), layouts_b(inputs), layouts_c(inputs),
                 layouts_d(inputs)):
        arrays.update(part)
    dram = {}
    for name, a in arrays.items():
        arrays[name] = a = np.ascontiguousarray(a)
        dram[name] = nc.dram_tensor(name + "_dram", a.shape, mybir.dt.from_np(a.dtype), kind="ExternalInput").ap()
    out = nc.dram_tensor("out_dram", (D, SEQS * T), F32, kind="ExternalOutput").ap()
    build(nc, dram, out)
    r = _run(nc, [{name + "_dram": a for name, a in arrays.items()}], core_ids=[0])
    return np.ascontiguousarray(r.results[0]["out_dram"].T).reshape(SEQS, T, D)
```

```python
from contextlib import ExitStack

import numpy as np

import concourse.bass as bass
from concourse import mybir

F32 = mybir.dt.float32
BF16 = mybir.dt.bfloat16
ALU = mybir.AluOpType
ACT = mybir.ActivationFunctionType
AX_X = mybir.AxisListType.X

SEQS = 16
T = 256
D = 128
PAD = 34
STRIDE = PAD + T


def clear_semaphores(nc, semaphores):
    with nc.Block() as block:
        @block.gpsimd
        def _(pool):
            for semaphore in semaphores.values():
                pool.sem_clear(semaphore)

A_HEADS = 16
A_DH = D // A_HEADS
A_G = 4
NEG = -1e30


def causal_attention(nc, dram, X):
    with ExitStack() as ctx:
        def sb(name, shape, dt=F32):
            return ctx.enter_context(nc.sbuf_tensor("a_" + name, shape, dt))

        Wq = sb("Wq", [128, A_G, 128])
        Wk = sb("Wk", [128, A_G, 128])
        Wv = sb("Wv", [128, 128])
        Wp = sb("Wp", [128, A_G, 128])
        qk_bias = sb("qk_bias", [128, 2, A_G])
        v_bias = sb("v_bias", [128, 128])
        p_bias = sb("p_bias", [128, 1])
        neg_ident = sb("neg_ident", [128, 128])
        ident_b = sb("ident_b", [128, 128], BF16)
        mask_q = sb("mask_q", [128, 256], BF16)
        mask_k = sb("mask_k", [128, 256], BF16)
        mean_w = sb("mean_w", [128, 128])
        ones = sb("ones", [128, 32])
        eps = sb("eps", [128, 1])
        xf = sb("xf", [128, 2, T])
        qT = sb("qT", [128, 2, A_G, T])
        kT = sb("kT", [128, 2, A_G, T])
        V = sb("V", [128, 2, 2, A_HEADS, 32])
        M = sb("M", [128, 2, A_G, 128])
        PTa = sb("PTa", [128, 4, A_G, T])
        PTb = sb("PTb", [128, 4, A_G, 128])
        rsum = sb("rsum", [128, 512])
        Y = sb("Y", [128, A_G, T])
        r = sb("r", [128, T])
        xc = sb("xc", [128, T])
        xsq = sb("xsq", [128, T])
        std = sb("std", [128, T])
        rstd = sb("rstd", [128, T])
        banks = [ctx.enter_context(nc.psum_tensor(f"a_bank{i}", [128, 512], F32)) for i in range(8)]

        names = """w_in memset_done xf_ready qkv_done qkv_taken s_done max_ready st_done pt_ready
            mt_done q_aug pv_done rsum_ready y_ready out_done r_ready mean_done xc_ready xsq_ready var_done
            std_ready rstd_ready x_ready gate""".split()
        s = {n: ctx.enter_context(nc.semaphore("a_" + n)) for n in names}
        ctx.callback(clear_semaphores, nc, s)

        def seq_wait(eng, name, seq, per=1, more=None):
            eng.wait_ge(s[name], seq * per + (per if more is None else more))

        block = ctx.enter_context(nc.Block())
        n_loads = 11

        def run(eng, slot):
            slot(0, 0, True, False, False)
            slot(1, 1, True, True, False)
            with eng.Fori(1, SEQS // 2) as half:
                slot(half * 2, 0, True, True, True)
                slot(half * 2 + 1, 1, True, True, True)
            slot(SEQS, 0, False, True, True)

        @block.sync
        def _(sp):
            for dst, name in ((Wq, "A_Wq"), (Wk, "A_Wk"), (Wv, "A_Wv"), (Wp, "A_Wp"), (qk_bias, "A_qk_bias"),
                              (p_bias, "A_p_bias"), (neg_ident, "neg_ident")):
                sp.dma_start(dst[:], dram[name]).then_inc(s["w_in"], 16)
            sp.dma_start(v_bias[:], dram["A_v_bias"].partition_broadcast(128)).then_inc(s["w_in"], 16)
            for dst, name in ((ident_b, "ident_b"), (mask_q, "mask_q"), (mask_k, "mask_k")):
                sp.dma_start(dst[:], dram[name]).then_inc(s["w_in"], 16)

        @block.tensor
        def _(pe):
            pe.wait_ge(s["w_in"], 16 * n_loads)
            pe.wait_ge(s["memset_done"], 5)

            def slot(k, par, cur, prev, pprev):
                p, was = k - 1, 1 - par
                if cur:
                    seq_wait(pe, "xf_ready", k)
                    if pprev:
                        seq_wait(pe, "xc_ready", k - 2)
                        seq_wait(pe, "std_ready", k - 2)
                    elif prev:
                        seq_wait(pe, "q_aug", p, 2)
                    for job in range(4):
                        if job >= 2:
                            seq_wait(pe, "qkv_taken", k, 5, job - 1)
                        W = (Wq, Wk)[job // 2]
                        for g in range(2):
                            mm = nc.tensor.matmul(banks[4 + job % 2][:, 256 * g:256 * g + 256],
                                                  W[:, 2 * (job % 2) + g, :], xf[:, par, :], start=True, stop=True)
                        mm.then_inc(s["qkv_done"], 1)
                    seq_wait(pe, "qkv_taken", k, 5, 3)
                    for t in range(2):
                        mm = nc.tensor.matmul(banks[4][:, 128 * t:128 * t + 128], xf[:, par, 128 * t:128 * t + 128], Wv[:],
                                              start=True, stop=True)
                    mm.then_inc(s["qkv_done"], 1)
                    seq_wait(pe, "qkv_taken", k, 5, 4)
                if prev:
                    seq_wait(pe, "q_aug", p, 2)
                for i in range(4):
                    rows = slice(32 * i, 32 * i + A_DH)
                    aug = slice(32 * i, 32 * i + A_DH + 1)
                    for j in range(3):
                        job = 3 * i + j
                        if cur:
                            bank = banks[job % 2]
                            if job >= 2:
                                seq_wait(pe, "max_ready", k, 12, job - 1)
                            elif prev:
                                seq_wait(pe, "max_ready", p, 12, 11 + job)
                            if j == 0:
                                nc.tensor.matmul(bank[:], ident_b[:], mask_q[:, 128:256].unsqueeze(1).to_broadcast([128, 4, 128]),
                                                 start=True, stop=False, skip_group_check=True)
                                for g in range(4):
                                    mm = nc.tensor.matmul(bank[:, 128 * g:128 * g + 128], qT[rows, par, g, 0:128],
                                                          kT[rows, par, g, 0:128], start=False, stop=g == 3,
                                                          skip_group_check=True)
                            else:
                                nc.tensor.matmul(bank[:], ident_b[:], mask_q[:].unsqueeze(1).to_broadcast([128, 2, 256]),
                                                 start=True, stop=False, skip_group_check=True)
                                for g in range(2):
                                    mm = nc.tensor.matmul(bank[:, 256 * g:256 * g + 256], qT[rows, par, 2 * (j - 1) + g, 128:256],
                                                          kT[rows, par, 2 * (j - 1) + g, :], start=False, stop=g == 1,
                                                          skip_group_check=True)
                            mm.then_inc(s["s_done"], 1)
                        if prev:
                            bank = banks[2 + job % 2]
                            if job >= 2:
                                seq_wait(pe, "pt_ready", p, 12, job - 1)
                            elif pprev:
                                seq_wait(pe, "pt_ready", k - 2, 12, 11 + job)
                            if j == 0:
                                nc.tensor.matmul(bank[:], ident_b[:], mask_k[:, 0:128].unsqueeze(1).to_broadcast([128, 4, 128]),
                                                 start=True, stop=False, skip_group_check=True)
                                for g in range(4):
                                    mm = nc.tensor.matmul(bank[:, 128 * g:128 * g + 128], kT[aug, was, g, 128:256],
                                                          qT[aug, was, g, 128:256], start=False, stop=g == 3,
                                                          skip_group_check=True)
                            else:
                                nc.tensor.matmul(bank[:], ident_b[:], mask_k[:].unsqueeze(1).to_broadcast([128, 2, 256]),
                                                 start=True, stop=False, skip_group_check=True)
                                for g in range(2):
                                    mm = nc.tensor.matmul(bank[:, 256 * g:256 * g + 256], kT[aug, was, 2 * (j - 1) + g, 0:128],
                                                          qT[aug, was, 2 * (j - 1) + g, :], start=False, stop=g == 1,
                                                          skip_group_check=True)
                            mm.then_inc(s["st_done"], 1)
                if prev:
                    seq_wait(pe, "pt_ready", p, 12)
                    for gp in range(2):
                        if gp == 1:
                            seq_wait(pe, "y_ready", p, 2, 1)
                        elif pprev:
                            seq_wait(pe, "y_ready", k - 2, 2)
                        for bank, what in ((banks[6], "y"), (banks[7], "sum")):
                            for g in range(2):
                                at = 256 * g
                                for tile in range(2):
                                    for i in range(4):
                                        G = 2 * gp + g
                                        w = V[:, was, tile, 4 * G + i, :] if what == "y" else ones[:]
                                        rhs = PTa[:, i, G, :] if tile == 0 else PTb[:, i, G, :]
                                        mm = nc.tensor.matmul(bank[32 * i:32 * i + 32, at + 128 * tile:at + 256], w, rhs,
                                                              start=tile == 0, stop=tile == 1, skip_group_check=True)
                        mm.then_inc(s["pv_done"], 1)
                if cur:
                    for t in range(2):
                        if t == 0:
                            seq_wait(pe, "max_ready", k, 12)
                            seq_wait(pe, "qkv_taken", k, 5)
                        for g in range(A_G):
                            mm = nc.tensor.matmul(banks[5 - t][:, 128 * g:128 * g + 128], M[:, t, g, :], neg_ident[:],
                                                  start=True, stop=True)
                        mm.then_inc(s["mt_done"], 1)
                if prev:
                    seq_wait(pe, "y_ready", p, 2)
                    if cur:
                        seq_wait(pe, "q_aug", k, 2, 1)
                    elif pprev:
                        seq_wait(pe, "std_ready", k - 2)
                    for g in range(A_G):
                        mm = nc.tensor.matmul(banks[5][:, 0:T], Wp[:, g, :], Y[:, g, :], start=g == 0, stop=g == A_G - 1)
                    mm.then_inc(s["out_done"], 1)
                    if cur:
                        seq_wait(pe, "q_aug", k, 2)
                    seq_wait(pe, "r_ready", p)
                    nc.tensor.matmul(banks[4][:, 0:T], mean_w[:], r[:], start=True, stop=True).then_inc(s["mean_done"], 1)
                    seq_wait(pe, "xsq_ready", p)
                    nc.tensor.matmul(banks[5][:, 0:T], mean_w[:], xsq[:], start=True, stop=True).then_inc(s["var_done"], 1)

            run(pe, slot)

        @block.scalar
        def _(act):
            act.wait_ge(s["memset_done"], 5)

            def slot(k, par, cur, prev, pprev):
                p = k - 1
                if prev:
                    for job in range(12):
                        i, j = divmod(job, 3)
                        seq_wait(act, "st_done", p, 12, job + 1)
                        if job == 0 and pprev:
                            seq_wait(act, "pv_done", k - 2, 2)
                        dst = PTb[:, i, :, :] if j == 0 else PTa[:, i, 2 * (j - 1):2 * j, :]
                        nc.scalar.activation(dst.rearrange("p g t -> p (g t)"), banks[2 + job % 2][:], ACT.Exp,
                                             scale=float(A_DH) ** -0.5).then_inc(s["pt_ready"], 1)
                    seq_wait(act, "var_done", p)
                    nc.scalar.activation(std[:], banks[5][:, 0:T], ACT.Sqrt, bias=eps[:, 0:1]).then_inc(s["std_ready"], 1)

            run(act, slot)

        @block.gpsimd
        def _(pool):
            nc.gpsimd.memset(eps[:], 1e-5).then_inc(s["memset_done"], 1)
            nc.gpsimd.memset(mean_w[:], 1.0 / 128).then_inc(s["memset_done"], 1)
            nc.gpsimd.memset(ones[:], 1.0).then_inc(s["memset_done"], 1)
            nc.gpsimd.memset(V[:], 0.0).then_inc(s["memset_done"], 1)
            nc.gpsimd.memset(M[:], 0.0).then_inc(s["memset_done"], 1)

            def slot(k, par, cur, prev, pprev):
                p = k - 1
                if cur:
                    if pprev:
                        seq_wait(pool, "qkv_done", k - 2, 5)
                        seq_wait(pool, "r_ready", k - 2)
                        pool.sem_inc(s["gate"], 1)
                    nc.gpsimd.tensor_copy(xf[:, par, :], X[:, k, PAD:]).then_inc(s["xf_ready"], 1)
                if prev:
                    seq_wait(pool, "xc_ready", p)
                    if pprev:
                        seq_wait(pool, "var_done", k - 2)
                    nc.gpsimd.tensor_tensor(xsq[:], xc[:], xc[:], ALU.mult).then_inc(s["xsq_ready"], 1)

            run(pool, slot)

        @block.vector
        def _(dve):
            dve.wait_ge(s["w_in"], 16 * n_loads)
            dve.wait_ge(s["memset_done"], 5)

            def slot(k, par, cur, prev, pprev):
                p, was = k - 1, 1 - par
                if cur:
                    for job in range(4):
                        half, pair = divmod(job, 2)
                        dst = (qT, kT)[half]
                        seq_wait(dve, "qkv_done", k, 5, job + 1)
                        if job == 0 and pprev:
                            seq_wait(dve, "st_done", k - 2, 12)
                        nc.vector.tensor_tensor(dst[:, par, 2 * pair:2 * pair + 2, :],
                                                banks[4 + job % 2][:].rearrange("p (g t) -> p g t", g=2),
                                                qk_bias[:, half, 2 * pair:2 * pair + 2].unsqueeze(2).to_broadcast([128, 2, T]),
                                                ALU.add).then_inc(s["qkv_taken"], 1)
                    seq_wait(dve, "qkv_done", k, 5)
                    if pprev:
                        seq_wait(dve, "pv_done", k - 2, 2)
                    nc.vector.tensor_tensor(V[:, par, :, :, 0:A_DH], banks[4][:, 0:256].rearrange("p (t h d) -> p t h d", t=2, d=A_DH),
                                            v_bias[:].rearrange("p (h d) -> p h d", d=A_DH).unsqueeze(1).to_broadcast([128, 2, A_HEADS, A_DH]),
                                            ALU.add).then_inc(s["qkv_taken"], 1)
                    for job in range(12):
                        i, j = divmod(job, 3)
                        seq_wait(dve, "s_done", k, 12, job + 1)
                        if job == 0 and prev:
                            seq_wait(dve, "mt_done", p, 2)
                        if j == 0:
                            dst, src = M[:, 0, :, 32 * i + A_DH], banks[job % 2][:].rearrange("p (g t) -> p g t", g=4)
                        else:
                            dst = M[:, 1, 2 * (j - 1):2 * j, 32 * i + A_DH]
                            src = banks[job % 2][:].rearrange("p (g t) -> p g t", g=2)
                        nc.vector.tensor_reduce(dst, src, AX_X, ALU.max).then_inc(s["max_ready"], 1)
                if prev:
                    for gp in range(2):
                        seq_wait(dve, "pv_done", p, 2, gp + 1)
                        if gp == 1:
                            seq_wait(dve, "y_ready", p, 2, 1)
                        elif pprev:
                            seq_wait(dve, "y_ready", k - 2, 2)
                            seq_wait(dve, "out_done", k - 2)
                        nc.vector.reciprocal(rsum[:], banks[7][:]).then_inc(s["rsum_ready"], 1)
                        seq_wait(dve, "rsum_ready", p, 2, gp + 1)
                        nc.vector.tensor_tensor(Y[:, 2 * gp:2 * gp + 2, :].rearrange("p g t -> p (g t)"), banks[6][:], rsum[:], ALU.mult)\
                            .then_inc(s["y_ready"], 1)
                if cur:
                    seq_wait(dve, "s_done", k, 12)
                    for t in range(2):
                        seq_wait(dve, "mt_done", k, 2, t + 1)
                        part = qT[:, par, :, 128 * t:128 * t + 128]
                        nc.vector.tensor_tensor(part, part, banks[5 - t][:].rearrange("p (g t) -> p g t", g=4), ALU.add)\
                            .then_inc(s["q_aug"], 1)
                if prev:
                    seq_wait(dve, "out_done", p)
                    nc.vector.scalar_tensor_tensor(r[:], banks[5][:, 0:T], p_bias[:, 0:1], xf[:, was, :], ALU.add, ALU.add)\
                        .then_inc(s["r_ready"], 1)
                    seq_wait(dve, "mean_done", p)
                    seq_wait(dve, "r_ready", p)
                    nc.vector.tensor_tensor(xc[:], r[:], banks[4][:, 0:T], ALU.subtract).then_inc(s["xc_ready"], 1)
                    seq_wait(dve, "std_ready", p)
                    nc.vector.reciprocal(rstd[:], std[:]).then_inc(s["rstd_ready"], 1)
                    seq_wait(dve, "rstd_ready", p)
                    nc.vector.tensor_tensor(X[:, p, PAD:], xc[:], rstd[:], ALU.mult).then_inc(s["x_ready"], 1)
                    seq_wait(dve, "x_ready", p)

            run(dve, slot)


def layouts_a(i):
    w = np.asarray(i["L0_attn_W_qkv"]).reshape(D, 3, A_G, 4, A_DH)
    b = np.asarray(i["L0_attn_b_qkv"]).reshape(3, A_G, 4, A_DH)
    out = {}
    for n, name in ((0, "A_Wq"), (1, "A_Wk")):
        a = np.zeros((D, A_G, 4, 32), np.float32)
        a[..., :A_DH] = w[:, n]
        out[name] = a.reshape(D, A_G, 128)
    bias = np.zeros((4, 32, 2, A_G), np.float32)
    bias[:, :A_DH] = b[0:2].transpose(2, 3, 0, 1)
    bias[:, A_DH, 1] = 1.0
    out["A_qk_bias"] = bias.reshape(128, 2, A_G)
    out["A_Wv"] = w[:, 2].reshape(D, D)
    out["A_v_bias"] = b[2].reshape(D)
    wp = np.zeros((4, 32, A_G, D), np.float32)
    wp[:, :A_DH] = np.asarray(i["L0_attn_W_proj"]).reshape(A_G, 4, A_DH, D).transpose(1, 2, 0, 3)
    out["A_Wp"] = wp.reshape(128, A_G, D)
    out["A_p_bias"] = np.asarray(i["L0_attn_b_proj"]).reshape(D, 1)
    return out


def constants_a():
    late = np.triu(np.ones((128, 128), bool), 1)
    q = np.zeros((128, 256), np.float32)
    q[:, 128:][late] = NEG
    k = np.zeros((128, 256), np.float32)
    k[:, :128][late.T] = NEG
    b = lambda a: a.astype(mybir.dt.np(BF16))
    eye = np.eye(128, dtype=np.float32)
    return {"neg_ident": -eye, "ident_b": b(eye), "mask_q": b(q), "mask_k": b(k)}


DEPTH = 8
LEAVES = 2 ** DEPTH
LW = 16
CH = LEAVES * LW // 128
NG = 8
GT = SEQS * T // NG
RING = 4


def standardise(nc, dram, X, XN):
    with ExitStack() as ctx:
        def sb(name, shape, dt=F32):
            return ctx.enter_context(nc.sbuf_tensor("n_" + name, shape, dt))

        mean_w = sb("mean_w", [128, 128])
        var_w = sb("var_w", [128, 128])
        eps = sb("eps", [128, 1])
        xc = sb("xc", [128, 2, T])
        xsq = sb("xsq", [128, 2, T])
        sd = sb("sd", [128, 2, T])
        root = sb("root", [128, 2, T])
        inv = sb("inv", [128, 2, T])
        ps = ctx.enter_context(nc.psum_tensor("n_ps", [128, 4, 512], F32))
        names = "memset_done mean_done xc_ready xsq_ready var_done sd_ready root_ready inv_ready xn_ready gate".split()
        s = {n: ctx.enter_context(nc.semaphore("n_" + n)) for n in names}
        ctx.callback(clear_semaphores, nc, s)

        def seq_wait(eng, name, seq):
            eng.wait_ge(s[name], seq + 1)

        block = ctx.enter_context(nc.Block())

        def run(eng, slot):
            slot(0, 0, False)
            slot(1, 1, False)
            with eng.Fori(1, SEQS // 2) as half:
                slot(half * 2, 0, True)
                slot(half * 2 + 1, 1, True)

        @block.tensor
        def _(pe):
            pe.wait_ge(s["memset_done"], 3)

            def slot(k, par, again):
                if again:
                    seq_wait(pe, "xc_ready", k - 2)
                nc.tensor.matmul(ps[:, par, 0:T], mean_w[:], X[:, k, PAD:], start=True, stop=True).then_inc(s["mean_done"], 1)
                seq_wait(pe, "xsq_ready", k)
                if again:
                    seq_wait(pe, "sd_ready", k - 2)
                nc.tensor.matmul(ps[:, 2 + par, 0:T], var_w[:], xsq[:, par, :], start=True, stop=True).then_inc(s["var_done"], 1)

            run(pe, slot)

        @block.scalar
        def _(act):
            act.wait_ge(s["memset_done"], 3)

            def slot(k, par, again):
                seq_wait(act, "var_done", k)
                nc.scalar.activation(sd[:, par, :], ps[:, 2 + par, 0:T], ACT.Sqrt).then_inc(s["sd_ready"], 1)
                seq_wait(act, "sd_ready", k)
                if again:
                    seq_wait(act, "inv_ready", k - 2)
                nc.scalar.activation(root[:, par, :], sd[:, par, :], ACT.Sqrt, bias=eps[:, 0:1]).then_inc(s["root_ready"], 1)

            run(act, slot)

        @block.gpsimd
        def _(pool):
            nc.gpsimd.memset(eps[:], 1e-5).then_inc(s["memset_done"], 1)
            nc.gpsimd.memset(mean_w[:], 1.0 / D).then_inc(s["memset_done"], 1)
            nc.gpsimd.memset(var_w[:], 1.0 / (D - 1)).then_inc(s["memset_done"], 1)

            def slot(k, par, again):
                seq_wait(pool, "xc_ready", k)
                nc.gpsimd.tensor_tensor(xsq[:, par, :], xc[:, par, :], xc[:, par, :], ALU.mult).then_inc(s["xsq_ready"], 1)

            run(pool, slot)

        @block.vector
        def _(dve):
            def slot(k, par, again):
                seq_wait(dve, "mean_done", k)
                if again:
                    seq_wait(dve, "xn_ready", k - 2)
                nc.vector.tensor_tensor(xc[:, par, :], X[:, k, PAD:], ps[:, par, 0:T], ALU.subtract).then_inc(s["xc_ready"], 1)
                seq_wait(dve, "root_ready", k)
                nc.vector.reciprocal(inv[:, par, :], root[:, par, :]).then_inc(s["inv_ready"], 1)
                seq_wait(dve, "inv_ready", k)
                nc.vector.tensor_tensor(XN[:, bass.ds(k * T, T)], xc[:, par, :], inv[:, par, :], ALU.mult).then_inc(s["xn_ready"], 1)

            run(dve, slot)


def fast_feedforwards(nc, dram, modules, act_func):
    with ExitStack() as ctx:
        n_mod = len(modules)
        tag = modules[0][0]

        def sb(name, shape, dt=F32):
            return ctx.enter_context(nc.sbuf_tensor(f"{tag}_{name}", shape, dt))

        nbuf = 2 if n_mod > 1 else 1
        nodes = sb("nodes", [128, nbuf, LEAVES])
        node_b = sb("node_b", [128, nbuf, 2])
        W1 = sb("W1", [128, nbuf, CH * 128])
        b1 = sb("b1", [128, nbuf, CH])
        W2 = sb("W2", [128, nbuf, CH, 128])
        b2 = sb("b2", [128, nbuf, 2, 128])
        paths = sb("paths", [128, 2, LEAVES], BF16)
        rights = sb("rights", [128, 2])
        leaf_no = sb("leaf_no", [128, 2, 128])
        chunk_leaf = sb("chunk_leaf", [128, CH])
        bits = sb("bits", [128, 2, GT], BF16)
        onehot = sb("onehot", [128, 2, 2, GT])
        routed = sb("routed", [128, 2, GT])
        hid = sb("hid", [128, RING, GT])
        hm = sb("hm", [128, RING, GT])
        pp = ctx.enter_context(nc.psum_tensor(f"{tag}_ps_prep", [128, 2, 512], F32))
        ph = ctx.enter_context(nc.psum_tensor(f"{tag}_ps_hid", [128, RING, 512], F32))
        po = ctx.enter_context(nc.psum_tensor(f"{tag}_ps_out", [128, 2, 512], F32))
        names = """consts_in w_in0 w_in1 bits_done bits_ready match_done onehot_ready routed_done routed_ready
            hid_done hid_ready hm_ready second_done out_done out_ready gate_act""".split()
        s = {n: ctx.enter_context(nc.semaphore(f"{tag}_{n}")) for n in names}
        ctx.callback(clear_semaphores, nc, s)

        def group_wait(eng, name, group, per=1, more=None):
            eng.wait_ge(s[name], group * per + (per if more is None else more))

        block = ctx.enter_context(nc.Block())

        def run(eng, slot):
            for m in range(n_mod):
                if m == 0:
                    slot(0, 0, 0, 0, True, False, False)
                    slot(0, 1, 1, 1, True, True, False)
                else:
                    slot(m, m * NG, 0, 0, True, True, True)
                    slot(m, m * NG + 1, 1, 1, True, True, True)
                with eng.Fori(1, NG // 2) as half:
                    slot(m, half * 2 + m * NG, half * 2, 0, True, True, True)
                    slot(m, half * 2 + (m * NG + 1), half * 2 + 1, 1, True, True, True)
            slot(n_mod, n_mod * NG, 0, 0, False, True, True)

        @block.sync
        def _(sp):
            for dst, name in ((paths, "paths"), (rights, "rights"), (leaf_no, "leaf_no"), (chunk_leaf, "chunk_leaf")):
                sp.dma_start(dst[:], dram[name]).then_inc(s["consts_in"], 16)
            for m, (name, _, _) in enumerate(modules):
                buf = m % nbuf
                if m >= nbuf:
                    sp.wait_ge(s["out_done"], NG * (m - nbuf + 1))
                for dst, part in ((nodes, "nw"), (node_b, "nb"), (W1, "w1"), (b1, "b1"), (W2, "w2"), (b2, "b2")):
                    sp.dma_start(dst[:, buf], dram[f"{name}_{part}"]).then_inc(s[f"w_in{buf}"], 16)

        @block.tensor
        def _(pe):
            pe.wait_ge(s["consts_in"], 64)

            def slot(m, n, g, par, cur, prev, pprev):
                q = n - 1
                buf = m % nbuf
                prep = []
                if cur:
                    src = modules[m][1]
                    cols = bass.ds(g * GT, GT)

                    def route_bits(j):
                        if isinstance(n, int) and n % NG == 0 and j == 0:
                            pe.wait_ge(s[f"w_in{buf}"], 96 * (m // nbuf + 1))
                        if prev:
                            group_wait(pe, "routed_ready", q)
                            group_wait(pe, "onehot_ready", q, 2)
                        nc.tensor.matmul(pp[:, j, :], nodes[:, buf, 128 * j:128 * j + 128], src[:, cols], start=True, stop=True)\
                            .then_inc(s["bits_done"], 1)

                    def match(j):
                        group_wait(pe, "bits_ready", n, 2)
                        for half in range(2):
                            mm = nc.tensor.matmul(pp[:, j, :], paths[:, half, 128 * j:128 * j + 128], bits[:, half, :],
                                                  start=half == 0, stop=half == 1)
                        mm.then_inc(s["match_done"], 1)

                    def leaf_number():
                        group_wait(pe, "onehot_ready", n, 2)
                        for half in range(2):
                            mm = nc.tensor.matmul(pp[:, 0, :], leaf_no[:, half, :], onehot[:, par, half, :],
                                                  start=half == 0, stop=half == 1)
                        mm.then_inc(s["routed_done"], 1)

                    prep = [(2, lambda: route_bits(0)), (3, lambda: route_bits(1)), (8, lambda: match(0)),
                            (9, lambda: match(1)), (14, leaf_number)]
                if prev:
                    first = isinstance(n, int) and n % NG == 0
                    qm = m - 1 if first else m
                    qbuf, qpar = qm % nbuf, 1 - par
                    qcols = bass.ds(((NG - 1) if first else g - 1) * GT, GT)
                    qsrc = modules[qm][1]

                    def hidden(c):
                        if c >= RING:
                            group_wait(pe, "hid_ready", q, CH, c - RING + 1)
                        elif pprev:
                            group_wait(pe, "hid_ready", n - 2, CH, CH - RING + c + 1)
                        nc.tensor.matmul(ph[:, c % RING, :], W1[:, qbuf, 128 * c:128 * c + 128], qsrc[:, qcols],
                                         start=True, stop=True).then_inc(s["hid_done"], 1)

                    def second(c):
                        group_wait(pe, "hm_ready", q, CH, c + 1)
                        mm = nc.tensor.matmul(po[:, qpar, :], W2[:, qbuf, c, :], hm[:, c % RING, :], start=False, stop=c == CH - 1)
                        mm.then_inc(s["out_done"] if c == CH - 1 else s["second_done"], 1)

                    if pprev:
                        group_wait(pe, "out_ready", n - 2)
                    for half in range(2):
                        nc.tensor.matmul(po[:, qpar, :], b2[:, qbuf, half, :], onehot[:, qpar, half, :], start=half == 0, stop=False)
                    for c in range(CH + 2):
                        for at, step in prep:
                            if at == c:
                                step()
                        if c < CH:
                            hidden(c)
                        if c >= 2:
                            second(c - 2)
                else:
                    for _, step in prep:
                        step()

            run(pe, slot)

        @block.scalar
        def _(act):
            def slot(m, n, g, par, cur, prev, pprev):
                q = n - 1
                if prev:
                    first = isinstance(n, int) and n % NG == 0
                    qm = m - 1 if first else m
                    qbuf, qpar = qm % nbuf, 1 - par
                    dst = modules[qm][2]
                    qcols = bass.ds(((NG - 1) if first else g - 1) * GT, GT)
                    for c in range(CH):
                        if cur and c == 15:
                            leaf_number(n, par)
                        group_wait(act, "hid_done", q, CH, c + 1)
                        if c >= RING:
                            group_wait(act, "hm_ready", q, CH, c - RING + 1)
                        nc.scalar.activation(hid[:, c % RING, :], ph[:, c % RING, :], act_func, bias=b1[:, qbuf, c:c + 1])\
                            .then_inc(s["hid_ready"], 1)
                    group_wait(act, "out_done", q)
                    act.sem_inc(s["gate_act"], 1)
                    nc.scalar.activation(dst[:, qcols], po[:, qpar, :], ACT.Copy).then_inc(s["out_ready"], 1)
                else:
                    leaf_number(n, par)

            def leaf_number(n, par):
                group_wait(act, "routed_done", n)
                nc.scalar.activation(routed[:, par, :], pp[:, 0, :], ACT.Copy).then_inc(s["routed_ready"], 1)

            run(act, slot)

        @block.vector
        def _(dve):
            dve.wait_ge(s["consts_in"], 64)

            def route_bits(m, n, j, prev):
                group_wait(dve, "bits_done", n, 2, j + 1)
                if prev and j == 0:
                    group_wait(dve, "match_done", n - 1, 2)
                nc.vector.tensor_scalar(bits[:, j, :], pp[:, j, :], node_b[:, m % nbuf, j:j + 1], 0.0, ALU.add, ALU.is_gt)\
                    .then_inc(s["bits_ready"], 1)

            def match(n, par, j, pprev):
                group_wait(dve, "match_done", n, 2, j + 1)
                if pprev and j == 0:
                    group_wait(dve, "out_done", n - 2)
                nc.vector.tensor_scalar(onehot[:, par, j, :], pp[:, j, :], rights[:, j:j + 1], None, ALU.is_equal)\
                    .then_inc(s["onehot_ready"], 1)

            def slot(m, n, g, par, cur, prev, pprev):
                q = n - 1
                if prev:
                    qpar = 1 - par
                    for c in range(CH):
                        if cur and c in (3, 4):
                            route_bits(m, n, c - 3, prev)
                        if cur and c in (9, 10):
                            match(n, par, c - 9, pprev)
                        group_wait(dve, "hid_ready", q, CH, c + 1)
                        if c == 0:
                            group_wait(dve, "routed_ready", q)
                        if c >= RING:
                            group_wait(dve, "second_done", q, CH - 1, c - RING + 1)
                        elif pprev:
                            group_wait(dve, "out_done", n - 2)
                        nc.vector.scalar_tensor_tensor(hm[:, c % RING, :], routed[:, qpar, :], chunk_leaf[:, c:c + 1],
                                                       hid[:, c % RING, :], ALU.is_equal, ALU.mult).then_inc(s["hm_ready"], 1)
                else:
                    for j in range(2):
                        route_bits(m, n, j, prev)
                    for j in range(2):
                        match(n, par, j, pprev)

            run(dve, slot)


def leaf_attention(nc, dram, XN, Q, K, V):
    with ExitStack() as ctx:
        def sb(name, shape, dt=F32):
            return ctx.enter_context(nc.sbuf_tensor("t_" + name, shape, dt))

        ident = sb("ident", [128, 128])
        qf = sb("qf", [128, 2, T])
        vf = sb("vf", [128, 2, T])
        Vt = sb("Vt", [128, 2, T])
        mx = sb("mx", [128, 2])
        nm = sb("nm", [128, 2])
        P = sb("P", [128, 2, T])
        den = sb("den", [128, 2])
        rden = sb("rden", [128, 2])
        Pn = sb("Pn", [128, 2, T])
        PT = sb("PT", [128, 2, T])
        ps_s = ctx.enter_context(nc.psum_tensor("t_s", [128, 512], F32))
        ps_v = ctx.enter_context(nc.psum_tensor("t_v", [128, 512], F32))
        ps_t = ctx.enter_context(nc.psum_tensor("t_t", [128, 512], F32))
        ps_o = ctx.enter_context(nc.psum_tensor("t_o", [128, 512], F32))
        names = """ident_in qf_ready vf_ready s_done mx_ready nm_ready p_ready rden_ready pn_ready pt_done pt_ready
            vt_done vt_ready o_done y_ready gate""".split()
        s = {n: ctx.enter_context(nc.semaphore("t_" + n)) for n in names}
        ctx.callback(clear_semaphores, nc, s)

        def seq_wait(eng, name, seq, per=1, more=None):
            eng.wait_ge(s[name], seq * per + (per if more is None else more))

        scale = float(D) ** -0.5
        block = ctx.enter_context(nc.Block())

        def run(eng, slot):
            slot(0, 0, True, False, False)
            slot(1, 1, True, True, False)
            with eng.Fori(1, SEQS // 2) as half:
                slot(half * 2, 0, True, True, True)
                slot(half * 2 + 1, 1, True, True, True)
            slot(SEQS, 0, False, True, True)

        @block.sync
        def _(sp):
            sp.dma_start(ident[:], dram["ident"]).then_inc(s["ident_in"], 16)

        @block.gpsimd
        def _(pool):
            def slot(k, par, cur, prev, pprev):
                if cur:
                    if pprev:
                        seq_wait(pool, "s_done", k - 2)
                        seq_wait(pool, "vt_done", k - 2)
                        pool.sem_inc(s["gate"], 1)
                    nc.gpsimd.tensor_copy(qf[:, par, :], Q[:, bass.ds(k * T, T)]).then_inc(s["qf_ready"], 1)
                    nc.gpsimd.tensor_copy(vf[:, par, :], V[:, bass.ds(k * T, T)]).then_inc(s["vf_ready"], 1)

            run(pool, slot)

        @block.tensor
        def _(pe):
            pe.wait_ge(s["ident_in"], 16)

            def slot(k, par, cur, prev, pprev):
                p = k - 1
                if cur:
                    seq_wait(pe, "qf_ready", k)
                    if prev:
                        seq_wait(pe, "p_ready", p, 2)
                        seq_wait(pe, "mx_ready", p)
                    for t in range(2):
                        mm = nc.tensor.matmul(ps_s[:, T * t:T * t + T], qf[:, par, 128 * t:128 * t + 128], K[:, bass.ds(k * T, T)],
                                              start=True, stop=True)
                    mm.then_inc(s["s_done"], 1)
                    seq_wait(pe, "vf_ready", k)
                    if prev:
                        seq_wait(pe, "vt_ready", p)
                    for t in range(2):
                        mm = nc.tensor.transpose(ps_v[:, 128 * t:128 * t + 128], vf[:, par, 128 * t:128 * t + 128], ident[:])
                    mm.then_inc(s["vt_done"], 1)
                if prev:
                    seq_wait(pe, "pn_ready", p, 2)
                    if pprev:
                        seq_wait(pe, "pt_ready", k - 2)
                    for tq in range(2):
                        for tk in range(2):
                            mm = nc.tensor.transpose(ps_t[:, T * tk + 128 * tq:T * tk + 128 * tq + 128],
                                                     Pn[:, tq, 128 * tk:128 * tk + 128], ident[:])
                    mm.then_inc(s["pt_done"], 1)
                    seq_wait(pe, "pt_ready", p)
                    seq_wait(pe, "vt_ready", p)
                    if pprev:
                        seq_wait(pe, "y_ready", k - 2)
                    for t in range(2):
                        mm = nc.tensor.matmul(ps_o[:, 0:T], Vt[:, 1 - par, 128 * t:128 * t + 128], PT[:, t, :],
                                              start=t == 0, stop=t == 1)
                    mm.then_inc(s["o_done"], 1)

            run(pe, slot)

        @block.scalar
        def _(act):
            def slot(k, par, cur, prev, pprev):
                p = k - 1
                if cur:
                    seq_wait(act, "nm_ready", k)
                    if prev:
                        seq_wait(act, "pn_ready", p, 2)
                    for t in range(2):
                        nc.scalar.activation(P[:, t, :], ps_s[:, T * t:T * t + T], ACT.Exp, bias=nm[:, t:t + 1], scale=scale,
                                             accum_out=den[:, t:t + 1]).then_inc(s["p_ready"], 1)
                    seq_wait(act, "vt_done", k)
                    if pprev:
                        seq_wait(act, "o_done", k - 2)
                    nc.scalar.activation(Vt[:, par, :], ps_v[:, 0:T], ACT.Copy).then_inc(s["vt_ready"], 1)
                if prev:
                    seq_wait(act, "pt_done", p)
                    if pprev:
                        seq_wait(act, "o_done", k - 2)
                    nc.scalar.activation(PT[:].rearrange("p a t -> p (a t)"), ps_t[:], ACT.Copy).then_inc(s["pt_ready"], 1)

            run(act, slot)

        @block.vector
        def _(dve):
            def slot(k, par, cur, prev, pprev):
                p = k - 1
                if prev:
                    seq_wait(dve, "p_ready", p, 2)
                    nc.vector.reciprocal(rden[:], den[:]).then_inc(s["rden_ready"], 1)
                    seq_wait(dve, "rden_ready", p)
                    if pprev:
                        seq_wait(dve, "pt_done", k - 2)
                    for t in range(2):
                        nc.vector.tensor_scalar(Pn[:, t, :], P[:, t, :], rden[:, t:t + 1], None, ALU.mult).then_inc(s["pn_ready"], 1)
                if cur:
                    seq_wait(dve, "s_done", k)
                    nc.vector.tensor_reduce(mx[:], ps_s[:].rearrange("p (t k) -> p t k", t=2), AX_X, ALU.max).then_inc(s["mx_ready"], 1)
                    seq_wait(dve, "mx_ready", k)
                    nc.vector.tensor_scalar(nm[:], mx[:], -scale, None, ALU.mult).then_inc(s["nm_ready"], 1)
                if prev:
                    seq_wait(dve, "o_done", p)
                    part = XN[:, bass.ds(p * T, T)]
                    nc.vector.tensor_tensor(part, part, ps_o[:, 0:T], ALU.add).then_inc(s["y_ready"], 1)

            run(dve, slot)


def add_and_norm(nc, X, Y, Z, tag):
    with ExitStack() as ctx:
        def sb(name, shape, dt=F32):
            return ctx.enter_context(nc.sbuf_tensor(f"{tag}_{name}", shape, dt))

        mean_w = sb("mean_w", [128, 128])
        eps = sb("eps", [128, 1])
        yz = sb("yz", [128, 2, T])
        r = sb("r", [128, 2, T])
        xc = sb("xc", [128, 2, T])
        xsq = sb("xsq", [128, 2, T])
        std = sb("std", [128, 2, T])
        rstd = sb("rstd", [128, 2, T])
        ps = ctx.enter_context(nc.psum_tensor(f"{tag}_ps", [128, 4, 512], F32))
        names = "memset_done yz_ready r_ready mean_done xc_ready xsq_ready var_done std_ready rstd_ready x_ready".split()
        s = {n: ctx.enter_context(nc.semaphore(f"{tag}_{n}")) for n in names}
        ctx.callback(clear_semaphores, nc, s)

        def seq_wait(eng, name, seq):
            eng.wait_ge(s[name], seq + 1)

        block = ctx.enter_context(nc.Block())

        def run(eng, slot):
            slot(0, 0, False)
            slot(1, 1, False)
            with eng.Fori(1, SEQS // 2) as half:
                slot(half * 2, 0, True)
                slot(half * 2 + 1, 1, True)

        @block.tensor
        def _(pe):
            pe.wait_ge(s["memset_done"], 2)

            def slot(k, par, again):
                seq_wait(pe, "r_ready", k)
                if again:
                    seq_wait(pe, "xc_ready", k - 2)
                nc.tensor.matmul(ps[:, par, 0:T], mean_w[:], r[:, par, :], start=True, stop=True).then_inc(s["mean_done"], 1)
                seq_wait(pe, "xsq_ready", k)
                if again:
                    seq_wait(pe, "std_ready", k - 2)
                nc.tensor.matmul(ps[:, 2 + par, 0:T], mean_w[:], xsq[:, par, :], start=True, stop=True).then_inc(s["var_done"], 1)

            run(pe, slot)

        @block.scalar
        def _(act):
            act.wait_ge(s["memset_done"], 2)

            def slot(k, par, again):
                seq_wait(act, "var_done", k)
                if again:
                    seq_wait(act, "rstd_ready", k - 2)
                nc.scalar.activation(std[:, par, :], ps[:, 2 + par, 0:T], ACT.Sqrt, bias=eps[:, 0:1]).then_inc(s["std_ready"], 1)

            run(act, slot)

        @block.gpsimd
        def _(pool):
            nc.gpsimd.memset(eps[:], 1e-5).then_inc(s["memset_done"], 1)
            nc.gpsimd.memset(mean_w[:], 1.0 / D).then_inc(s["memset_done"], 1)

            def slot(k, par, again):
                seq_wait(pool, "xc_ready", k)
                if again:
                    seq_wait(pool, "var_done", k - 2)
                nc.gpsimd.tensor_tensor(xsq[:, par, :], xc[:, par, :], xc[:, par, :], ALU.mult).then_inc(s["xsq_ready"], 1)

            run(pool, slot)

        @block.vector
        def _(dve):
            def slot(k, par, again):
                cols = bass.ds(k * T, T)
                if again:
                    seq_wait(dve, "r_ready", k - 2)
                if Z is not None:
                    nc.vector.tensor_tensor(yz[:, par, :], Y[:, cols], Z[:, cols], ALU.add).then_inc(s["yz_ready"], 1)
                    seq_wait(dve, "yz_ready", k)
                if again:
                    seq_wait(dve, "mean_done", k - 2)
                nc.vector.tensor_tensor(r[:, par, :], X[:, k, PAD:], yz[:, par, :] if Z is not None else Y[:, cols], ALU.add)\
                    .then_inc(s["r_ready"], 1)
                seq_wait(dve, "mean_done", k)
                seq_wait(dve, "r_ready", k)
                if again:
                    seq_wait(dve, "x_ready", k - 2)
                nc.vector.tensor_tensor(xc[:, par, :], r[:, par, :], ps[:, par, 0:T], ALU.subtract).then_inc(s["xc_ready"], 1)
                seq_wait(dve, "std_ready", k)
                nc.vector.reciprocal(rstd[:, par, :], std[:, par, :]).then_inc(s["rstd_ready"], 1)
                seq_wait(dve, "rstd_ready", k)
                nc.vector.tensor_tensor(X[:, k, PAD:], xc[:, par, :], rstd[:, par, :], ALU.mult).then_inc(s["x_ready"], 1)

            run(dve, slot)


def fast_feedforward_block(nc, dram, X):
    with ExitStack() as ctx:
        def flat(name):
            return ctx.enter_context(nc.sbuf_tensor(name, [128, SEQS * T], F32))

        XN, Q, K, V = flat("b_XN"), flat("b_Q"), flat("b_K"), flat("b_V")
        standardise(nc, dram, X, XN)
        fast_feedforwards(nc, dram, [("q", XN, Q), ("k", XN, K), ("v", XN, V)], ACT.Relu)
        leaf_attention(nc, dram, XN, Q, K, V)
        fast_feedforwards(nc, dram, [("f", XN, Q)], ACT.Gelu)
        add_and_norm(nc, X, XN, Q, "l")


def layouts_b(i):
    out = {}
    for m in "qkvf":
        a = lambda n: np.asarray(i[f"L0_ffn_{m}_{n}"])
        nw = np.zeros((LEAVES, D), np.float32)
        nw[:LEAVES - 1] = a("nw")
        nb = np.zeros(LEAVES, np.float32)
        nb[:LEAVES - 1] = a("nb")
        out[m + "_nw"] = nw.T
        out[m + "_nb"] = nb.reshape(2, 128).T
        out[m + "_w1"] = a("w1").transpose(1, 0, 2).reshape(D, LEAVES * LW)
        out[m + "_b1"] = a("b1").reshape(CH, 128).T
        out[m + "_w2"] = a("w2").reshape(CH, 128, D).transpose(1, 0, 2)
        out[m + "_b2"] = a("b2").reshape(2, 128, D).transpose(1, 0, 2)
    return out


def constants_b():
    paths = np.zeros((LEAVES, LEAVES), np.float32)
    for leaf in range(LEAVES):
        node = 0
        for level in range(DEPTH):
            right = (leaf >> (DEPTH - 1 - level)) & 1
            paths[node, leaf] = 1.0 if right else -1.0
            node = 2 * node + 1 + right
    rights = (paths > 0).sum(0).astype(np.float32)
    number = np.arange(LEAVES, dtype=np.float32).reshape(2, 128)
    return {"paths": paths.reshape(2, 128, LEAVES).transpose(1, 0, 2).astype(mybir.dt.np(BF16)),
            "rights": rights.reshape(2, 128).T,
            "leaf_no": np.repeat(number.T[:, :, None], 128, 2),
            "chunk_leaf": (8 * np.arange(CH)[None, :] + np.arange(128)[:, None] // LW).astype(np.float32),
            "ident": np.eye(128, dtype=np.float32)}




def gated_scan(nc, dram, X, X0):
    with ExitStack() as ctx:
        def sb(name, shape, dt=F32):
            return ctx.enter_context(nc.sbuf_tensor("c_" + name, shape, dt))

        W = sb("W", [128, 3, 128])
        bias = sb("bias", [128, 3])
        mean_w = sb("mean_w", [128, 128])
        eps = sb("eps", [128, 1])
        gate = sb("gate", [128, 3, T])
        u = sb("u", [128, T])
        a = sb("a", [128, T])
        h = sb("h", [128, T])
        r = sb("r", [128, 2, T])
        xc = sb("xc", [128, T])
        xsq = sb("xsq", [128, T])
        std = sb("std", [128, T])
        rstd = sb("rstd", [128, T])
        ps = ctx.enter_context(nc.psum_tensor("c_gates", [128, 3, 512], F32))
        ps_mean = ctx.enter_context(nc.psum_tensor("c_mean", [128, 512], F32))
        ps_var = ctx.enter_context(nc.psum_tensor("c_var", [128, 512], F32))
        names = """w_in memset_done gates_done gate_ready u_ready a_ready h_ready r_ready mean_done xc_ready
            xsq_ready var_done std_ready rstd_ready x_ready copied gate""".split()
        s = {n: ctx.enter_context(nc.semaphore("c_" + n)) for n in names}
        ctx.callback(clear_semaphores, nc, s)

        def seq_wait(eng, name, seq, per=1, more=None):
            eng.wait_ge(s[name], seq * per + (per if more is None else more))

        block = ctx.enter_context(nc.Block())

        def run(eng, slot):
            slot(0, 0, True, False, False)
            slot(1, 1, True, True, False)
            with eng.Fori(1, SEQS // 2) as half:
                slot(half * 2, 0, True, True, True)
                slot(half * 2 + 1, 1, True, True, True)
            slot(SEQS, 0, False, True, True)

        @block.sync
        def _(sp):
            sp.dma_start(W[:], dram["C_W"]).then_inc(s["w_in"], 16)
            sp.dma_start(bias[:], dram["C_bias"]).then_inc(s["w_in"], 16)

        @block.tensor
        def _(pe):
            pe.wait_ge(s["w_in"], 32)
            pe.wait_ge(s["memset_done"], 2)

            def slot(k, par, cur, prev, pprev):
                p = k - 1
                if cur:
                    if prev:
                        seq_wait(pe, "gate_ready", p, 3)
                    for n in range(3):
                        nc.tensor.matmul(ps[:, n, 0:T], W[:, n, :], X[:, k, PAD:], start=True, stop=True)\
                            .then_inc(s["gates_done"], 1)
                if prev:
                    seq_wait(pe, "r_ready", p)
                    if pprev:
                        seq_wait(pe, "xc_ready", k - 2)
                    nc.tensor.matmul(ps_mean[:, 0:T], mean_w[:], r[:, 1 - par, :], start=True, stop=True).then_inc(s["mean_done"], 1)
                    seq_wait(pe, "xsq_ready", p)
                    if pprev:
                        seq_wait(pe, "std_ready", k - 2)
                    nc.tensor.matmul(ps_var[:, 0:T], mean_w[:], xsq[:], start=True, stop=True).then_inc(s["var_done"], 1)

            run(pe, slot)

        @block.scalar
        def _(act):
            act.wait_ge(s["memset_done"], 2)
            act.wait_ge(s["w_in"], 32)

            def slot(k, par, cur, prev, pprev):
                p = k - 1
                if cur:
                    if prev:
                        seq_wait(act, "a_ready", p)
                        seq_wait(act, "u_ready", p)
                    for n in range(3):
                        seq_wait(act, "gates_done", k, 3, n + 1)
                        nc.scalar.activation(gate[:, n, :], ps[:, n, 0:T], (ACT.Sigmoid, ACT.Tanh, ACT.Sigmoid)[n],
                                             bias=bias[:, n:n + 1]).then_inc(s["gate_ready"], 1)
                if prev:
                    seq_wait(act, "var_done", p)
                    if pprev:
                        seq_wait(act, "rstd_ready", k - 2)
                    nc.scalar.activation(std[:], ps_var[:, 0:T], ACT.Sqrt, bias=eps[:, 0:1]).then_inc(s["std_ready"], 1)

            run(act, slot)

        @block.gpsimd
        def _(pool):
            nc.gpsimd.memset(eps[:], 1e-5).then_inc(s["memset_done"], 1)
            nc.gpsimd.memset(mean_w[:], 1.0 / 128).then_inc(s["memset_done"], 1)

            def slot(k, par, cur, prev, pprev):
                p = k - 1
                if prev:
                    seq_wait(pool, "xc_ready", p)
                    if pprev:
                        seq_wait(pool, "var_done", k - 2)
                    nc.gpsimd.tensor_tensor(xsq[:], xc[:], xc[:], ALU.mult).then_inc(s["xsq_ready"], 1)
                    seq_wait(pool, "x_ready", p)
                    seq_wait(pool, "r_ready", p)
                    pool.sem_inc(s["gate"], 1)
                    nc.gpsimd.tensor_copy(X[:, p, PAD:], X0[:, bass.ds(p * T, T)]).then_inc(s["copied"], 1)

            run(pool, slot)

        @block.vector
        def _(dve):
            def slot(k, par, cur, prev, pprev):
                p = k - 1
                if prev:
                    seq_wait(dve, "mean_done", p)
                    if pprev:
                        seq_wait(dve, "x_ready", k - 2)
                    nc.vector.tensor_tensor(xc[:], r[:, 1 - par, :], ps_mean[:, 0:T], ALU.subtract).then_inc(s["xc_ready"], 1)
                if cur:
                    seq_wait(dve, "gate_ready", k, 3)
                    if prev:
                        seq_wait(dve, "h_ready", p)
                    nc.vector.tensor_tensor(u[:], gate[:, 0, :], gate[:, 1, :], ALU.mult).then_inc(s["u_ready"], 1)
                    nc.vector.tensor_scalar(a[:], gate[:, 2, :], 0.998, 0.001, ALU.mult, ALU.add).then_inc(s["a_ready"], 1)
                    seq_wait(dve, "u_ready", k)
                    seq_wait(dve, "a_ready", k)
                    if prev:
                        seq_wait(dve, "r_ready", p)
                    nc.vector.tensor_tensor_scan(h[:], a[:], u[:], 0.0, ALU.mult, ALU.add).then_inc(s["h_ready"], 1)
                    seq_wait(dve, "h_ready", k)
                    if pprev:
                        seq_wait(dve, "mean_done", k - 2)
                    nc.vector.tensor_tensor(r[:, par, :], X[:, k, PAD:], h[:], ALU.add).then_inc(s["r_ready"], 1)
                if prev:
                    seq_wait(dve, "std_ready", p)
                    nc.vector.reciprocal(rstd[:], std[:]).then_inc(s["rstd_ready"], 1)
                    seq_wait(dve, "rstd_ready", p)
                    nc.vector.tensor_tensor(X0[:, bass.ds(p * T, T)], xc[:], rstd[:], ALU.mult).then_inc(s["x_ready"], 1)

            run(dve, slot)


def layouts_c(i):
    return {"C_W": np.stack([np.asarray(i["L1_attn_W" + n]).T for n in "gvd"], 1),
            "C_bias": np.stack([np.asarray(i["L1_attn_b" + n]) for n in "gvd"], 1)}


LAYERS = 6
TILES = LAYERS * SEQS * 2
HEADS = 16
DH = 64
WIN = 32
INNER = HEADS * DH
HP = HEADS // 2
HID = 341
HCH = 3
HROWS = [128, 128, HID - 256]
HEAD_COLS = HP * DH


def local_attention_layers(nc, dram, X, XM):
    with ExitStack() as ctx:
        def sb(name, shape):
            return ctx.enter_context(nc.sbuf_tensor(name, shape, F32))

        Wqk = sb("d_Wqk", [128, 2 * INNER])
        Wv = sb("d_Wv", [128, 2, HEAD_COLS])
        Wo = sb("d_Wo", [128, HP, 128])
        W1 = sb("d_W1", [128, 2 * HID])
        W2 = sb("d_W2", [128, HCH, 128])
        vecs = sb("d_vecs", [128, 9])
        qkscale = sb("d_qkscale", [128, 2, DH])
        rot_const = sb("d_rot_const", [128, 2, 2, 2, DH])
        rot = sb("d_rot", [128, 2, 2, 2, DH])
        mask = sb("d_mask", [128, 2, DH])
        ident = sb("d_ident", [128, 128])
        mean_w = sb("d_mean_w", [128, 128])
        eps = sb("d_eps", [128, 1])
        xs = sb("d_xs", [128, 2, WIN + 128])
        raw = sb("d_raw", [128, 2 * INNER])
        sq = sb("d_sq", [128, 2, INNER])
        rs = sb("d_rs", [128, 2 * INNER])
        rc = sb("d_rc", [128, 2 * INNER])
        ss = sb("d_ss", [128, 2, HEADS])
        length = sb("d_length", [128, 2, HEADS])
        norm = sb("d_norm", [128, 2, HEADS])
        inv = sb("d_inv", [128, 2, HEADS])
        QT = sb("d_QT", [128, HP, 128])
        KT = sb("d_KT", [128, HP, WIN + 256])
        sm = sb("d_sm", [128, 2, HP, DH])
        sc = sb("d_sc", [128, 2, HP, DH])
        mx = sb("d_mx", [128, HEADS])
        P = sb("d_P", [128, HP, 2, DH])
        den = sb("d_den", [128, HEADS])
        rden = sb("d_rden", [128, HEADS])
        PT = sb("d_PT", [128, HP, 128])
        VP = sb("d_VP", [128, 4, HEAD_COLS])
        On = sb("d_On", [128, HP, 2, DH])
        OT = sb("d_OT", [128, HP, 128])
        xs2 = sb("d_xs2", [128, 128])
        xc = sb("d_xc", [128, 128])
        xsq = sb("d_xsq", [128, 128])
        std = sb("d_std", [128, 128])
        rstd = sb("d_rstd", [128, 128])
        xh = sb("d_xh", [128, 128])
        xn = sb("d_xn", [128, 128])
        G = sb("d_G", [128, HCH, 128])
        H = sb("d_H", [128, HCH, 128])
        pair = [ctx.enter_context(nc.psum_tensor(f"d_pair{i}", [128, 2, 512], F32)) for i in range(3)]
        b6 = ctx.enter_context(nc.psum_tensor("d_b6", [128, 512], F32))
        b7 = ctx.enter_context(nc.psum_tensor("d_b7", [128, 512], F32))
        b0, b1, b2, b3 = pair[0][:, 0, :], pair[0][:, 1, :], pair[1][:, 0, :], pair[1][:, 1, :]
        q_pair = k_pair = pair[2]
        v_bank = (b2, b7[:], b6[:], b1)

        names = """wqk_in wv_in wo_in w1_in w2_in vecs_in qks_in consts_in memset_done tables_q tables_k
            xs_ready qkq_done qkk_done sqq_ready rawq_ready sqk_ready rawk_ready ssq_ready ssk_ready
            len_ready norm_ready inv_ready rsq_ready rsk_ready rcq_ready rck_ready addq_ready addk_ready
            finq_ready fink_ready tq_done tk_done qt_ready kt_ready s_done sm_ready mx_ready sc_ready
            p_ready den_ready rden_ready v0_done v1_done v2_done v3_done vp0_ready vp1_ready vp2_ready
            vp3_ready pt_done pt_ready pv_done on_ready ot_done ot_ready proj_done xm_ready xs2_ready
            mean_done xc_ready xsq_ready var_done std_ready rstd_ready xh_ready xn_ready upa_done
            upg_done g_ready h_ready down_done x_ready gate_pe gate_pool""".split()
        s = {n: ctx.enter_context(nc.semaphore("d_" + n)) for n in names}
        ctx.callback(clear_semaphores, nc, s)

        def wait(eng, name, t, ahead=0, per=1, part=None):
            tile = t.k + ahead
            if isinstance(tile, int) and not 0 <= tile < TILES:
                return
            eng.wait_ge(s[name], tile * per + (per if part is None else part))

        class Tile:

            def __init__(self, l, b, par, behind):
                shift = (par - behind) // 2
                self.k = l * 32 + b * 2 + par - behind
                self.par = (par - behind) % 2
                self.b, self.l = (b + shift if shift else b), l
                if isinstance(self.b, int) and self.b < 0:
                    self.b, self.l = self.b + SEQS, l - 1
                self.live = not isinstance(self.k, int) or 0 <= self.k < TILES
                self.first = isinstance(self.b, int) and self.b == 0 and self.par == 0

        def run(eng, slot):
            def sequence(l, b):
                for par in range(2):
                    slot(lambda behind: Tile(l, b, par, behind))

            def layer(l):
                sequence(l, 0)
                sequence(l, 1)
                with eng.Fori(2, SEQS) as b:
                    sequence(l, b)

            layer(0)
            with eng.Fori(1, LAYERS) as l:
                layer(l)
            sequence(LAYERS, 0)
            slot(lambda behind: Tile(LAYERS, 1, 0, behind))

        def columns(stream, t, ahead=0, shift=0):
            lo = PAD + 128 * t.par - ahead - shift
            return stream[:, t.b, lo:lo + 128 + ahead]

        def by_head(flat, half):
            return flat[:, INNER * half:INNER * half + INNER].rearrange("p (h d) -> p h d", d=DH)

        def flat_pair(ps):
            return ps[:].rearrange("p a n -> p (a n)")

        w_dram = dram["Wqkv"]
        block = ctx.enter_context(nc.Block())

        @block.sync
        def _(sp):
            sp.dma_start(ident[:], dram["ident"]).then_inc(s["consts_in"], 16)
            sp.dma_start(rot_const[:], dram["rotary"]).then_inc(s["consts_in"], 16)
            sp.dma_start(mask[:], dram["window_mask"]).then_inc(s["consts_in"], 16)

            def load(l, again):
                def layer(ap):
                    return ap[bass.ds(l, 1)]
                if again:
                    sp.wait_ge(s["tables_q"], 4 * l)
                    sp.wait_ge(s["tables_k"], 4 * l)
                sp.dma_start(qkscale[:], layer(dram["qk_scale"]).rearrange("o a d -> (o a d)").partition_broadcast(128)
                             .rearrange("p (a d) -> p a d", a=2)).then_inc(s["qks_in"], 16)
                if again:
                    sp.wait_ge(s["qkq_done"], 32 * l)
                sp.dma_start(Wqk[:], layer(w_dram)[:, :, 0:2, :].rearrange("o p a n -> p (o a n)")).then_inc(s["wqk_in"], 16)
                if again:
                    sp.wait_ge(s["v3_done"], 32 * l)
                sp.dma_start(Wv[:, 0, :], layer(dram["Wv"])[:, :, 0, :].rearrange("o p n -> p (o n)")).then_inc(s["wv_in"], 16)
                sp.dma_start(Wv[:, 1, :], layer(dram["Wv"])[:, :, 1, :].rearrange("o p n -> p (o n)")).then_inc(s["wv_in"], 16)
                if again:
                    sp.wait_ge(s["proj_done"], 32 * l)
                sp.dma_start(Wo[:], layer(dram["Wo"]).rearrange("o (h p) n -> p (o h) n", p=128)).then_inc(s["wo_in"], 16)
                if again:
                    sp.wait_ge(s["down_done"], 32 * l)
                    sp.wait_ge(s["x_ready"], 32 * l)
                sp.dma_start(vecs[:], layer(dram["vecs"]).rearrange("o p n -> p (o n)")).then_inc(s["vecs_in"], 16)
                sp.dma_start(W1[:], layer(dram["W1"]).rearrange("o p n -> p (o n)")).then_inc(s["w1_in"], 16)
                sp.dma_start(W2[:], layer(dram["W2"]).rearrange("o p c n -> p (o c) n")).then_inc(s["w2_in"], 16)

            load(0, False)
            with sp.Fori(1, LAYERS) as l:
                load(l, True)

        @block.tensor
        def _(pe):
            pe.wait_ge(s["consts_in"], 48)
            pe.wait_ge(s["memset_done"], 5)

            def qk_half(t, half, ps, done):
                for j in range(2):
                    c = INNER * half + 512 * j
                    mm = nc.tensor.matmul(ps[:, j, :], xs[:, t.par, WIN:], Wqk[:, c:c + 512], start=True, stop=True)
                mm.then_inc(s[done], 1)

            def keys(t):
                if not t.live:
                    return
                if t.first:
                    pe.wait_ge(s["wqk_in"], 16 * t.l + 16)
                wait(pe, "xs_ready", t, per=2)
                wait(pe, "kt_ready", t, -1)
                qk_half(t, 1, k_pair, "qkk_done")

            def queries(t):
                if not t.live:
                    return
                wait(pe, "sqk_ready", t)
                wait(pe, "rawk_ready", t)
                qk_half(t, 0, q_pair, "qkq_done")

            def turn(t, ps, source, done):
                for hp in range(HP):
                    mm = nc.tensor.transpose(ps[:, hp // 4, (hp % 4) * 128:(hp % 4) * 128 + 128], source(hp), ident[:])
                mm.then_inc(s[done], 1)

            def queries_turned(t):
                if not t.live:
                    return
                wait(pe, "finq_ready", t)
                wait(pe, "std_ready", t, -2)
                wait(pe, "vp3_ready", t, -1)
                turn(t, pair[0], lambda hp: rc[:, hp * 128:hp * 128 + 128], "tq_done")

            def keys_turned(t):
                if not t.live:
                    return
                wait(pe, "fink_ready", t)
                wait(pe, "ot_ready", t, -2)
                turn(t, pair[2], lambda hp: rc[:, INNER + hp * 128:INNER + hp * 128 + 128], "tk_done")

            def scores(t):
                if not t.live:
                    return
                wait(pe, "kt_ready", t)
                wait(pe, "qt_ready", t)
                pe.sem_inc(s["gate_pe"], 1)
                at = 128 * t.par
                for hp in range(HP):
                    for odd in range(2):
                        rows = slice(64 * odd, 64 * odd + 64)
                        for w in range(4):
                            mm = nc.tensor.matmul(
                                pair[0][WIN * w:WIN * w + WIN, odd, hp * DH:hp * DH + DH],
                                QT[rows, hp, WIN * w:WIN * w + WIN],
                                KT[rows, hp, at + WIN * w:at + WIN * w + 2 * WIN], start=True, stop=True)
                mm.then_inc(s["s_done"], 1)

            def values(t, w):
                if not t.live:
                    return
                if t.first and w == 2:
                    pe.wait_ge(s["wv_in"], 32 * t.l + 32)
                if w == 0:
                    wait(pe, "on_ready", t, -1)
                if w == 1:
                    wait(pe, "g_ready", t, -2, HCH)
                if w == 2:
                    wait(pe, "xc_ready", t, -2)
                    wait(pe, "xs_ready", t, per=2)
                if w == 3:
                    wait(pe, "sm_ready", t)
                for odd in range(2):
                    mm = nc.tensor.matmul(v_bank[w][64 * odd:64 * odd + 64, :],
                                          xs[:, t.par, WIN * w:WIN * w + 2 * WIN], Wv[:, odd, :], start=True, stop=True)
                mm.then_inc(s[f"v{w}_done"], 1)

            def probabilities_turned(t):
                if not t.live:
                    return
                wait(pe, "p_ready", t)
                wait(pe, "vp0_ready", t)
                wait(pe, "xm_ready", t, -1)
                turn(t, pair[1], lambda hp: P[:, hp, :, :].rearrange("p a d -> p (a d)"), "pt_done")

            def attend(t):
                if not t.live:
                    return
                wait(pe, "vp3_ready", t)
                wait(pe, "pt_ready", t)
                pe.sem_inc(s["gate_pe"], 1)
                for hp in range(HP):
                    for odd in range(2):
                        rows = slice(64 * odd, 64 * odd + 64)
                        for w in range(4):
                            mm = nc.tensor.matmul(
                                pair[1][WIN * w:WIN * w + WIN, odd, hp * DH:hp * DH + DH],
                                PT[rows, hp, WIN * w:WIN * w + WIN],
                                VP[rows, w, hp * DH:hp * DH + DH], start=True, stop=True)
                mm.then_inc(s["pv_done"], 1)

            def attention_turned(t):
                if not t.live:
                    return
                wait(pe, "on_ready", t)
                wait(pe, "sqq_ready", t, 2)
                wait(pe, "rawq_ready", t, 2)
                turn(t, pair[2], lambda hp: On[:, hp, :, :].rearrange("p a d -> p (a d)"), "ot_done")

            def project(t):
                if not t.live:
                    return
                if t.first:
                    pe.wait_ge(s["wo_in"], 16 * t.l + 16)
                wait(pe, "ot_ready", t)
                for hp in range(HP):
                    mm = nc.tensor.matmul(b3[:, 0:128], Wo[:, hp, :], OT[:, hp, :], start=hp == 0, stop=hp == HP - 1)
                mm.then_inc(s["proj_done"], 1)

            def mean(t):
                if not t.live:
                    return
                wait(pe, "xs2_ready", t, per=2)
                wait(pe, "h_ready", t, -1, HCH)
                nc.tensor.matmul(b6[:, 0:128], mean_w[:], xs2[:], start=True, stop=True).then_inc(s["mean_done"], 1)

            def variance(t):
                if not t.live:
                    return
                wait(pe, "xsq_ready", t)
                wait(pe, "x_ready", t, -1)
                nc.tensor.matmul(b0[:, 0:128], mean_w[:], xsq[:], start=True, stop=True).then_inc(s["var_done"], 1)

            def hidden(t, side, ps, done):
                for c in range(HCH):
                    at = HID * side + 128 * c
                    mm = nc.tensor.matmul(ps[0:HROWS[c], 128 * c:128 * c + 128], W1[:, at:at + HROWS[c]], xn[:],
                                          start=True, stop=True)
                mm.then_inc(s[done], 1)

            def hidden_a(t):
                if not t.live:
                    return
                if t.first:
                    pe.wait_ge(s["w1_in"], 16 * t.l + 16)
                wait(pe, "xn_ready", t)
                wait(pe, "vp2_ready", t, 2)
                hidden(t, 0, b6, "upa_done")

            def hidden_gate(t):
                if not t.live:
                    return
                wait(pe, "vp1_ready", t, 1)
                hidden(t, 1, b7, "upg_done")

            def down(t):
                if not t.live:
                    return
                if t.first:
                    pe.wait_ge(s["w2_in"], 16 * t.l + 16)
                wait(pe, "h_ready", t, 0, HCH)
                wait(pe, "sm_ready", t, 2)
                for c in range(HCH):
                    mm = nc.tensor.matmul(b0[:, 0:128], W2[0:HROWS[c], c, :], H[0:HROWS[c], c, :],
                                          start=c == 0, stop=c == HCH - 1)
                mm.then_inc(s["down_done"], 1)

            def slot(tile):
                values(tile(1), 2)
                variance(tile(3))
                keys(tile(0))
                attend(tile(2))
                queries_turned(tile(1))
                queries(tile(0))
                scores(tile(1))
                attention_turned(tile(2))
                values(tile(1), 0)
                hidden_a(tile(3))
                hidden_gate(tile(3))
                project(tile(2))
                values(tile(1), 1)
                values(tile(1), 3)
                down(tile(3))
                keys_turned(tile(0))
                mean(tile(2))
                probabilities_turned(tile(1))

            run(pe, slot)

        @block.scalar
        def _(act):
            act.wait_ge(s["memset_done"], 5)

            def take(t, half, ps, qk):
                if not t.live:
                    return
                wait(act, f"qk{qk}_done", t)
                wait(act, f"ss{qk}_ready", t, -1)
                nc.scalar.activation(sq[:, half, :], flat_pair(ps), ACT.Square).then_inc(s[f"sq{qk}_ready"], 1)
                wait(act, f"rc{qk}_ready", t, -1)
                wait(act, f"rs{qk}_ready", t, -1)
                nc.scalar.activation(raw[:, INNER * half:INNER * half + INNER], flat_pair(ps), ACT.Copy)\
                    .then_inc(s[f"raw{qk}_ready"], 1)

            def lengths(t):
                if not t.live:
                    return
                wait(act, "ssk_ready", t)
                wait(act, "ssq_ready", t)
                wait(act, "norm_ready", t, -1)
                nc.scalar.activation(length[:], ss[:], ACT.Sqrt).then_inc(s["len_ready"], 1)

            def take_queries_turned(t):
                if not t.live:
                    return
                wait(act, "tq_done", t)
                wait(act, "s_done", t, -1)
                nc.scalar.activation(QT[:].rearrange("p h t -> p (h t)"), flat_pair(pair[0]), ACT.Copy).then_inc(s["qt_ready"], 1)

            def take_keys_turned(t):
                if not t.live:
                    return
                wait(act, "tk_done", t)
                wait(act, "s_done", t, -1)
                at = WIN + 128 * t.par
                nc.scalar.activation(KT[:, :, at:at + 128], pair[2][:].rearrange("p a (h t) -> p (a h) t", t=128), ACT.Copy)\
                    .then_inc(s["kt_ready"], 1)

            def exponentials(t):
                if not t.live:
                    return
                wait(act, "sc_ready", t)
                wait(act, "pt_done", t, -1)
                wait(act, "den_ready", t, -1)
                for odd in range(2):
                    ins = nc.scalar.activation(P[:, :, odd, :], sc[:, odd, :, :], ACT.Exp, scale=8.0)
                ins.then_inc(s["p_ready"], 1)

            def take_values(t, w):
                if not t.live:
                    return
                wait(act, f"v{w}_done", t)
                if w == 2:
                    wait(act, "pv_done", t, -1)
                nc.scalar.activation(VP[:, w, :], v_bank[w], ACT.Copy).then_inc(s[f"vp{w}_ready"], 1)

            def take_probabilities_turned(t):
                if not t.live:
                    return
                wait(act, "pt_done", t)
                wait(act, "pv_done", t, -1)
                nc.scalar.activation(PT[:].rearrange("p h t -> p (h t)"), flat_pair(pair[1]), ACT.Copy).then_inc(s["pt_ready"], 1)

            def take_attention_turned(t):
                if not t.live:
                    return
                wait(act, "ot_done", t)
                wait(act, "proj_done", t, -1)
                nc.scalar.activation(OT[:].rearrange("p h t -> p (h t)"), flat_pair(pair[2]), ACT.Copy).then_inc(s["ot_ready"], 1)

            def deviation(t):
                if not t.live:
                    return
                wait(act, "var_done", t)
                wait(act, "rstd_ready", t, -1)
                nc.scalar.activation(std[:], b0[:, 0:128], ACT.Sqrt, bias=eps[:, 0:1]).then_inc(s["std_ready"], 1)

            def gate(t):
                if not t.live:
                    return
                if t.first:
                    act.wait_ge(s["vecs_in"], 16 * t.l + 16)
                wait(act, "upg_done", t)
                wait(act, "h_ready", t, -1, HCH)
                for c in range(HCH):
                    r = HROWS[c]
                    nc.scalar.activation(G[0:r, c, :], b7[0:r, 128 * c:128 * c + 128], ACT.Gelu,
                                         bias=vecs[0:r, 5 + c:6 + c]).then_inc(s["g_ready"], 1)

            def slot(tile):
                take_probabilities_turned(tile(2))
                deviation(tile(3))
                take(tile(0), 1, k_pair, "k")
                take_values(tile(1), 2)
                take_queries_turned(tile(1))
                take(tile(0), 0, q_pair, "q")
                take_attention_turned(tile(2))
                lengths(tile(0))
                gate(tile(3))
                take_values(tile(1), 0)
                exponentials(tile(1))
                take_values(tile(1), 1)
                take_values(tile(1), 3)
                take_keys_turned(tile(0))

            run(act, slot)

        @block.gpsimd
        def _(pool):
            nc.gpsimd.memset(eps[:], 1e-5).then_inc(s["memset_done"], 1)
            nc.gpsimd.memset(mean_w[:], 1.0 / 128).then_inc(s["memset_done"], 1)
            nc.gpsimd.memset(KT[:, :, 0:WIN], 0.0).then_inc(s["memset_done"], 1)
            nc.gpsimd.memset(X[:, :, 0:PAD], 0.0).then_inc(s["memset_done"], 1)
            nc.gpsimd.memset(XM[:, :, 0:PAD], 0.0).then_inc(s["memset_done"], 1)
            pool.wait_ge(s["memset_done"], 5)

            def two_halves(t, target, source, shift_of, ready):
                for half in range(2):
                    if half:
                        wait(pool, ready, t, per=2, part=1)
                    pool.sem_inc(s["gate_pool"], 1)
                    rows = slice(64 * half, 64 * half + 64)
                    nc.gpsimd.tensor_copy(target[rows], columns(source, t, shift_of, half)[rows]).then_inc(s[ready], 1)

            def shifted_input(t):
                if not t.live:
                    return
                if not (isinstance(t.l, int) and t.l == 0):
                    wait(pool, "x_ready", t, -32)
                wait(pool, "v3_done", t, -2)
                if isinstance(t.k, int) and t.k == 1:
                    wait(pool, "rsk_ready", t, -1)
                elif isinstance(t.k, int) and t.k == 2:
                    wait(pool, "sc_ready", t, -2)
                else:
                    wait(pool, "xs2_ready", t, -3, 2)
                two_halves(t, xs[:, t.par, :], X, WIN, "xs_ready")

            def after_shifted_input(newest):
                wait(pool, "xs_ready", newest, per=2)

            def squares(t, newest):
                if not t.live:
                    return
                after_shifted_input(newest)
                wait(pool, "xc_ready", t)
                wait(pool, "var_done", t, -1)
                nc.gpsimd.tensor_tensor(xsq[:], xc[:], xc[:], ALU.mult).then_inc(s["xsq_ready"], 1)

            def sine_part(t, half, qk, newest):
                if not t.live:
                    return
                if half == 0:
                    after_shifted_input(newest)
                wait(pool, f"raw{qk}_ready", t)
                if t.first:
                    pool.wait_ge(s[f"tables_{qk}"], 4 * t.l + 4)
                wait(pool, f"add{qk}_ready", t, -1, 2)
                nc.gpsimd.tensor_tensor(by_head(rs, half), by_head(raw, half),
                                        rot[:, t.par, half, 1, :].unsqueeze(1).to_broadcast([128, HEADS, DH]), ALU.mult)\
                    .then_inc(s[f"rs{qk}_ready"], 1)

            def centred_scores(t):
                if not t.live:
                    return
                wait(pool, "mx_ready", t)
                wait(pool, "p_ready", t, -1)
                nc.gpsimd.tensor_tensor(sc[:].rearrange("p a h n -> p (a h) n"), sm[:].rearrange("p a h n -> p (a h) n"),
                                        mx[:].unsqueeze(2).to_broadcast([128, HEADS, DH]), ALU.subtract)\
                    .then_inc(s["sc_ready"], 1)

            def shifted_middle(t):
                if not t.live:
                    return
                wait(pool, "xm_ready", t)
                wait(pool, "xc_ready", t, -1)
                if isinstance(t.k, int) and t.k == TILES - 1:
                    wait(pool, "xsq_ready", t, -1)
                else:
                    wait(pool, "sc_ready", t, 1)
                two_halves(t, xs2, XM, 0, "xs2_ready")

            def slot(tile):
                shifted_input(tile(0))
                squares(tile(3), tile(0))
                sine_part(tile(1), 0, "q", tile(0))
                sine_part(tile(0), 1, "k", tile(0))
                centred_scores(tile(1))
                shifted_middle(tile(2))

            run(pool, slot)

        @block.vector
        def _(dve):
            dve.wait_ge(s["consts_in"], 48)
            dve.wait_ge(s["memset_done"], 5)

            def tables(t, half, qk):
                dve.wait_ge(s["qks_in"], 16 * t.l + 16)
                wait(dve, f"rs{qk}_ready", t, -1)
                for par in range(2):
                    for cs in range(2):
                        nc.vector.tensor_tensor(rot[:, par, half, cs, :], rot_const[:, par, half, cs, :],
                                                qkscale[:, half, :], ALU.mult).then_inc(s[f"tables_{qk}"], 1)
                dve.wait_ge(s[f"tables_{qk}"], 4 * t.l + 4)

            def cosine_part(t, half, qk):
                if not t.live:
                    return
                if t.first:
                    tables(t, half, qk)
                wait(dve, f"raw{qk}_ready", t)
                wait(dve, f"t{qk}_done", t, -1)
                nc.vector.tensor_tensor(by_head(rc, half), by_head(raw, half),
                                        rot[:, t.par, half, 0, :].unsqueeze(1).to_broadcast([128, HEADS, DH]), ALU.mult)\
                    .then_inc(s[f"rc{qk}_ready"], 1)

            def add_sine_part(t, half, qk):
                if not t.live:
                    return
                wait(dve, f"rc{qk}_ready", t)
                wait(dve, f"rs{qk}_ready", t)
                halves = lambda flat: flat[:, INNER * half:INNER * half + INNER].rearrange("p (h a d) -> p h a d", a=2, d=DH // 2)
                for a in range(2):
                    nc.vector.tensor_tensor(halves(rc)[:, :, a, :], halves(rc)[:, :, a, :], halves(rs)[:, :, 1 - a, :], ALU.add)\
                        .then_inc(s[f"add{qk}_ready"], 1)

            def unit_length(t, half, qk):
                if not t.live:
                    return
                wait(dve, "inv_ready", t)
                wait(dve, f"add{qk}_ready", t, 0, 2)
                nc.vector.tensor_tensor(by_head(rc, half), by_head(rc, half),
                                        inv[:, half, :].unsqueeze(2).to_broadcast([128, HEADS, DH]), ALU.mult)\
                    .then_inc(s[f"fin{qk}_ready"], 1)

            def squared_lengths(t, half, qk):
                if not t.live:
                    return
                wait(dve, f"sq{qk}_ready", t)
                nc.vector.tensor_reduce(ss[:, half, :], sq[:, half, :].rearrange("p (h d) -> p h d", d=DH), AX_X, ALU.add)\
                    .then_inc(s[f"ss{qk}_ready"], 1)

            def inverse_lengths(t):
                if not t.live:
                    return
                wait(dve, "len_ready", t)
                nc.vector.tensor_scalar(norm[:], length[:], 1e-12, None, ALU.max).then_inc(s["norm_ready"], 1)
                wait(dve, "norm_ready", t)
                nc.vector.reciprocal(inv[:], norm[:]).then_inc(s["inv_ready"], 1)

            def mask_scores(t):
                if not t.live:
                    return
                wait(dve, "s_done", t)
                wait(dve, "sc_ready", t, -1)
                nc.vector.tensor_tensor(sm[:].rearrange("p a h n -> p (a h) n"), pair[0][:].rearrange("p a (h n) -> p (a h) n", n=DH),
                                        mask[:, t.par, :].unsqueeze(1).to_broadcast([128, HEADS, DH]), ALU.add)\
                    .then_inc(s["sm_ready"], 1)

            def row_maxima(t):
                if not t.live:
                    return
                wait(dve, "sm_ready", t)
                nc.vector.tensor_reduce(mx[:], sm[:].rearrange("p a h n -> p (a h) n"), AX_X, ALU.max).then_inc(s["mx_ready"], 1)

            def denominators(t):
                if not t.live:
                    return
                wait(dve, "p_ready", t)
                nc.vector.tensor_reduce(den[:], P[:].rearrange("p h a d -> p (h a) d"), AX_X, ALU.add).then_inc(s["den_ready"], 1)
                wait(dve, "den_ready", t)
                nc.vector.reciprocal(rden[:], den[:]).then_inc(s["rden_ready"], 1)

            def normalised_attention(t):
                if not t.live:
                    return
                wait(dve, "pv_done", t)
                wait(dve, "rden_ready", t)
                wait(dve, "ot_done", t, -1)
                nc.vector.tensor_tensor(On[:].rearrange("p h a d -> p a h d"), pair[1][:].rearrange("p a (h d) -> p a h d", d=DH),
                                        rden[:].rearrange("p (h a) -> p a h", a=2).unsqueeze(3).to_broadcast([128, 2, HP, DH]),
                                        ALU.mult).then_inc(s["on_ready"], 1)

            def add_attention(t):
                if not t.live:
                    return
                wait(dve, "proj_done", t)
                nc.vector.tensor_tensor(columns(XM, t), columns(X, t), b3[:, 0:128], ALU.add).then_inc(s["xm_ready"], 1)

            def centred(t):
                if not t.live:
                    return
                wait(dve, "mean_done", t)
                wait(dve, "xh_ready", t, -1)
                nc.vector.tensor_tensor(xc[:], xs2[:], b6[:, 0:128], ALU.subtract).then_inc(s["xc_ready"], 1)

            def layernorm(t):
                if not t.live:
                    return
                wait(dve, "std_ready", t)
                nc.vector.reciprocal(rstd[:], std[:]).then_inc(s["rstd_ready"], 1)
                wait(dve, "rstd_ready", t)
                nc.vector.tensor_tensor(xh[:], xc[:], rstd[:], ALU.mult).then_inc(s["xh_ready"], 1)
                wait(dve, "xh_ready", t)
                if t.first:
                    dve.wait_ge(s["vecs_in"], 16 * t.l + 16)
                wait(dve, "upg_done", t, -1)
                nc.vector.tensor_scalar(xn[:], xh[:], vecs[:, 0:1], vecs[:, 1:2], ALU.mult, ALU.add).then_inc(s["xn_ready"], 1)

            def gated(t):
                if not t.live:
                    return
                wait(dve, "upa_done", t)
                wait(dve, "down_done", t, -1)
                for c in range(HCH):
                    r = HROWS[c]
                    wait(dve, "g_ready", t, 0, HCH, c + 1)
                    nc.vector.scalar_tensor_tensor(H[0:r, c, :], b6[0:r, 128 * c:128 * c + 128], vecs[0:r, 2 + c:3 + c],
                                                   G[0:r, c, :], ALU.add, ALU.mult).then_inc(s["h_ready"], 1)

            def add_feed_forward(t):
                if not t.live:
                    return
                wait(dve, "down_done", t)
                wait(dve, "xm_ready", t)
                nc.vector.scalar_tensor_tensor(columns(X, t), b0[:, 0:128], vecs[:, 8:9], columns(XM, t), ALU.add, ALU.add)\
                    .then_inc(s["x_ready"], 1)

            def slot(tile):
                cosine_part(tile(1), 0, "q")
                add_sine_part(tile(1), 0, "q")
                unit_length(tile(1), 0, "q")
                layernorm(tile(3))
                cosine_part(tile(0), 1, "k")
                normalised_attention(tile(2))
                squared_lengths(tile(0), 1, "k")
                squared_lengths(tile(0), 0, "q")
                add_sine_part(tile(0), 1, "k")
                mask_scores(tile(1))
                inverse_lengths(tile(0))
                row_maxima(tile(1))
                gated(tile(3))
                add_attention(tile(2))
                unit_length(tile(0), 1, "k")
                add_feed_forward(tile(3))
                centred(tile(2))
                denominators(tile(1))

            run(dve, slot)


def constants():
    half = np.arange(0, DH, 2, dtype=np.float32)
    inv_freq = (np.float32(1.0) / np.float32(10000.0) ** (half / np.float32(DH))).astype(np.float32)
    t = np.arange(T, dtype=np.float32)
    freqs = t[:, None] * inv_freq[None, :]
    freqs = np.concatenate([freqs, freqs], -1)
    base = (half + np.float32(0.4 * DH)) / np.float32(1.4 * DH)
    power = (t - T // 2) / np.float32(WIN // 2)
    scale = base[None, :] ** power[:, None]
    scale = np.concatenate([scale, scale], -1).astype(np.float32)
    cos, sin = np.cos(freqs), np.sin(freqs)
    sign = np.where(np.arange(DH) < DH // 2, 1.0, -1.0).astype(np.float32)
    rotary = np.zeros((128, 2, 2, 2, DH), np.float32)
    for par in range(2):
        rows = slice(128 * par, 128 * par + 128)
        for half_, s in ((0, scale), (1, np.float32(1.0) / scale)):
            rotary[:, par, half_, 0] = cos[rows] * s[rows]
            rotary[:, par, half_, 1] = sin[rows] * sign * s[rows]
    query = np.arange(128)[:, None] % WIN
    slot = np.arange(2 * WIN)[None, :]
    seen = (slot >= query) & (slot <= query + WIN)
    first = seen & ((np.arange(128)[:, None] >= WIN) | (slot >= WIN))
    mask = np.where(np.stack([first, seen], 1), 0.0, -1e30).astype(np.float32)
    return {"ident": np.eye(128, dtype=np.float32), "rotary": rotary, "window_mask": mask}


def layouts_d(i):
    a = lambda n: np.asarray(i["L1_ffn_" + n])
    out = {"Wqkv": a("Wqkv").reshape(LAYERS, D, 3, INNER)}
    out["Wv"] = np.ascontiguousarray(a("Wqkv").reshape(LAYERS, D, 3, HP, 2, DH)[:, :, 2].transpose(0, 1, 3, 2, 4)
                                     ).reshape(LAYERS, D, 2, HEAD_COLS)
    out["qk_scale"] = np.stack([a("q_scale"), a("k_scale")], 1)
    out["Wo"] = a("Wo")
    out["W1"] = a("W1")
    w2 = np.zeros((LAYERS, HCH * 128, D), np.float32)
    w2[:, :HID] = a("W2")
    out["W2"] = np.ascontiguousarray(w2.reshape(LAYERS, HCH, 128, D).transpose(0, 2, 1, 3))
    b1 = np.zeros((LAYERS, 2, HCH * 128), np.float32)
    b1[:, :, :HID] = a("b1").reshape(LAYERS, 2, HID)
    cols = [a("ln_g"), a("ln_b")] + [b1[:, s, 128 * c:128 * c + 128] for s in range(2) for c in range(HCH)] + [a("b2")]
    out["vecs"] = np.stack(cols, 2)
    return out


def build(nc, dram, out):
    with ExitStack() as ctx:
        X = ctx.enter_context(nc.sbuf_tensor("X", [128, SEQS, STRIDE], F32))
        s_in = ctx.enter_context(nc.semaphore("x_in"))
        s_out = ctx.enter_context(nc.semaphore("x_out"))
        with nc.Block() as block:
            @block.sync
            def _(sp):
                sp.dma_start(X[:, :, PAD:], dram["x"].rearrange("d (b t) -> d b t", t=T)).then_inc(s_in, 16)
                sp.wait_ge(s_in, 16)
        causal_attention(nc, dram, X)
        fast_feedforward_block(nc, dram, X)
        X0 = ctx.enter_context(nc.sbuf_tensor("X0", [128, SEQS * T], F32))
        gated_scan(nc, dram, X, X0)
        with ExitStack() as inner:
            XM = inner.enter_context(nc.sbuf_tensor("XM", [128, SEQS, STRIDE], F32))
            local_attention_layers(nc, dram, X, XM)
        add_and_norm(nc, X, X0, None, "o")
        with nc.Block() as block:
            @block.sync
            def _(sp):
                sp.dma_start(out.rearrange("d (b t) -> d b t", t=T), X[:, :, PAD:]).then_inc(s_out, 16)
                sp.wait_ge(s_out, 16)


def kernel(**inputs):
    import concourse.bacc as _bacc
    from concourse.bass_utils import run_bass_kernel_spmd as _run

    nc = _bacc.Bacc("TRN2", target_bir_lowering=False, num_devices=1)
    arrays = {"x": np.asarray(inputs["L0_attn_x"]).reshape(SEQS * T, D).T}
    for part in (constants(), constants_a(), constants_b(), layouts_a(inputs), layouts_b(inputs), layouts_c(inputs),
                 layouts_d(inputs)):
        arrays.update(part)
    dram = {}
    for name, a in arrays.items():
        arrays[name] = a = np.ascontiguousarray(a)
        dram[name] = nc.dram_tensor(name + "_dram", a.shape, mybir.dt.from_np(a.dtype), kind="ExternalInput").ap()
    out = nc.dram_tensor("out_dram", (D, SEQS * T), F32, kind="ExternalOutput").ap()
    build(nc, dram, out)
    r = _run(nc, [{name + "_dram": a for name, a in arrays.items()}], core_ids=[0])
    return np.ascontiguousarray(r.results[0]["out_dram"].T).reshape(SEQS, T, D)
```

```python
from contextlib import ExitStack

import numpy as np

import concourse.bass as bass
from concourse import mybir

F32 = mybir.dt.float32
BF16 = mybir.dt.bfloat16
F32R = mybir.dt.float32r
U32 = mybir.dt.uint32
ALU = mybir.AluOpType
ACT = mybir.ActivationFunctionType
AX_X = mybir.AxisListType.X

SEQS = 16
T = 256
D = 128
PAD = 34
STRIDE = PAD + T


def clear_semaphores(nc, semaphores):
    with nc.Block() as block:
        @block.gpsimd
        def _(pool):
            for semaphore in semaphores.values():
                pool.sem_clear(semaphore)

A_HEADS = 16
A_DH = D // A_HEADS
A_G = 4
A_GP = 8
A_SCORE_JOBS = 12
Q_PIECES = (1, 1, 2, 2, 1, 3)
K_PIECES = (1, 2, 1, 2, 3, 1)
A_ROWS = A_DH * len(Q_PIECES)
A_AUG = A_ROWS + 3
NEG = -1e30


def causal_attention(nc, dram, X):
    with ExitStack() as ctx:
        def sb(name, shape, dt=F32):
            return ctx.enter_context(nc.sbuf_tensor("a_" + name, shape, dt))

        Wqk = sb("Wqk", [128, 2, A_GP, 128])
        Wv = sb("Wv", [128, 128])
        Wp = sb("Wp", [128, A_G, 128])
        qk_bias = sb("qk_bias", [128, 2, A_GP])
        later = sb("later", [128, 2, 2])
        late_bias = sb("late_bias", [128, 2, A_GP])
        v_bias = sb("v_bias", [128, 128])
        p_bias = sb("p_bias", [128, 1])
        neg_ident = sb("neg_ident", [128, 128], BF16)
        ident_b = sb("ident_b", [128, 128], BF16)
        mask_q = sb("mask_q", [128, 256], BF16)
        mask_k = sb("mask_k", [128, 256], BF16)
        mean_w = sb("mean_w", [128, 128])
        ones = sb("ones", [128, 32])
        eps = sb("eps", [128, 1])
        xf = sb("xf", [128, 2, T])
        first = sb("first", [128, 2, 512], BF16)
        rest = sb("rest", [128, 2, 512])
        second = sb("second", [128, 2, 512], BF16)
        qs = sb("qs", [128, 2, A_GP, T], BF16)
        ks = sb("ks", [128, 2, A_GP, T], BF16)
        V = sb("V", [128, 2, 2, A_HEADS, 32])
        mx = sb("mx", [128, 2, A_HEADS])
        mx_rest = sb("mx_rest", [128, 2, 2, A_HEADS])
        M = sb("M", [128, 2, A_GP, 2, 64], BF16)
        PTa = sb("PTa", [128, 2, 4, A_G, T])
        PTb = sb("PTb", [128, 2, 4, A_G, 128])
        rsum = sb("rsum", [128, 512])
        Y = sb("Y", [128, A_G, T])
        r = sb("r", [128, T])
        xc = sb("xc", [128, T])
        xsq = sb("xsq", [128, T])
        std = sb("std", [128, T])
        rstd = sb("rstd", [128, T])
        banks = [ctx.enter_context(nc.psum_tensor(f"a_bank{i}", [128, 512], F32)) for i in range(8)]

        names = """w_in memset_done bias_done xf_ready qk_done first_ready rest_ready second_ready split_ready v_done v_ready
            s_done max_ready piece_ready mt_done q_aug st_done pt_ready pv_done rsum_ready y_ready out_done r_ready
            mean_done xc_ready xsq_ready var_done std_ready rstd_ready x_ready gate""".split()
        s = {n: ctx.enter_context(nc.semaphore("a_" + n)) for n in names}
        ctx.callback(clear_semaphores, nc, s)

        def wait(eng, name, seq, per=1, part=None):
            if isinstance(seq, int) and not 0 <= seq < SEQS:
                return
            eng.wait_ge(s[name], seq * per + (per if part is None else part))

        block = ctx.enter_context(nc.Block())
        n_loads = 11
        jobs = A_SCORE_JOBS

        def live(seq):
            return not isinstance(seq, int) or 0 <= seq < SEQS

        def run(eng, slot):
            for k in range(4):
                slot(k, k % 2)
            with eng.Fori(2, SEQS // 2) as half:
                slot(half * 2, 0)
                slot(half * 2 + 1, 1)
            slot(SEQS, 0)
            slot(SEQS + 1, 1)
            slot(SEQS + 2, 0)

        QK_AFTER = {1: 3, 3: 4, 5: 5, 7: 6, 9: 7}
        V_AFTER = {0: (0,), 2: (1,), 4: (2, 3), 8: (4,), 10: (5, 6), 11: (7,)}

        @block.sync
        def _(sp):
            for dst, name in ((Wqk, "A_Wqk"), (Wv, "A_Wv"), (Wp, "A_Wp"), (qk_bias, "A_qk_bias"), (later, "A_later"),
                              (p_bias, "A_p_bias"), (neg_ident, "neg_ident")):
                sp.dma_start(dst[:], dram[name]).then_inc(s["w_in"], 16)
            sp.dma_start(v_bias[:], dram["A_v_bias"].partition_broadcast(128)).then_inc(s["w_in"], 16)
            for dst, name in ((ident_b, "ident_b"), (mask_q, "mask_q"), (mask_k, "mask_k")):
                sp.dma_start(dst[:], dram[name]).then_inc(s["w_in"], 16)

        @block.tensor
        def _(pe):
            pe.wait_ge(s["w_in"], 16 * n_loads)
            pe.wait_ge(s["memset_done"], 5)

            def project(k, par, job):
                if not live(k):
                    return
                if job == 0:
                    wait(pe, "xf_ready", k)
                    wait(pe, "v_ready", k - 1)
                if job == 1:
                    wait(pe, "rest_ready", k - 1, 16)
                if job >= 2:
                    wait(pe, "rest_ready", k, 16, 2 * job - 2)
                for g in range(2):
                    mm = nc.tensor.matmul(banks[4 + job % 2][:, 256 * g:256 * g + 256],
                                          Wqk[:, job // 4, 2 * (job % 4) + g, :], xf[:, par, :], start=True, stop=True)
                mm.then_inc(s["qk_done"], 1)

            def values(k, par):
                if not live(k):
                    return
                wait(pe, "rest_ready", k, 16, 14)
                for t in range(2):
                    mm = nc.tensor.matmul(banks[4][:, 128 * t:128 * t + 128], xf[:, par, 128 * t:128 * t + 128], Wv[:],
                                          start=True, stop=True)
                mm.then_inc(s["v_done"], 1)

            def score_bank(bank, mask, left, right, rows, i, j, left_late, right_late, par, done):
                gs = range(4) if j == 0 else range(2 * j - 2, 2 * j)
                width = 512 // len(gs)
                nc.tensor.matmul(bank[:], ident_b[:], mask.unsqueeze(1).to_broadcast([128, len(gs), width]),
                                 start=True, stop=False, skip_group_check=True)
                at = slice(64 * (i % 2), 64 * (i % 2) + rows)
                for n, g in enumerate(gs):
                    mm = nc.tensor.matmul(bank[:, width * n:width * n + width], left[at, par, 2 * g + i // 2, left_late],
                                          right[at, par, 2 * g + i // 2, right_late], start=False, stop=n == len(gs) - 1,
                                          skip_group_check=True)
                mm.then_inc(s[done], 1)

            def scores(k, par, job):
                if not live(k):
                    return
                i, j = divmod(job, 3)
                if job == 0:
                    wait(pe, "split_ready", k, 8)
                if job >= 4:
                    wait(pe, "max_ready", k, jobs, job - 3)
                else:
                    wait(pe, "pt_ready", k - 1, jobs, job + 9)
                if j == 0:
                    score_bank(banks[job % 4], mask_q[:, 128:256], qs, ks, A_ROWS, i, j, slice(0, 128), slice(0, 128), par, "s_done")
                else:
                    score_bank(banks[job % 4], mask_q[:], qs, ks, A_ROWS, i, j, slice(128, 256), slice(0, 256), par, "s_done")

            def scores_turned(p, was, job):
                if not live(p):
                    return
                i, j = divmod(job, 3)
                if job == 0:
                    wait(pe, "q_aug", p, 4)
                if job < 4:
                    wait(pe, "max_ready", p, jobs)
                else:
                    wait(pe, "pt_ready", p, jobs, job - 3)
                if j == 0:
                    score_bank(banks[job % 4], mask_k[:, 0:128], ks, qs, A_AUG, i, j, slice(128, 256), slice(128, 256), was, "st_done")
                else:
                    score_bank(banks[job % 4], mask_k[:], ks, qs, A_AUG, i, j, slice(0, 128), slice(0, 256), was, "st_done")

            def attend(t, par, quarter):
                if not live(t):
                    return
                gp, what, g = quarter // 4, quarter // 2 % 2, quarter % 2
                if quarter == 0:
                    wait(pe, "pt_ready", t, jobs)
                    wait(pe, "std_ready", t - 1)
                    wait(pe, "v_ready", t)
                if quarter == 2:
                    wait(pe, "xc_ready", t - 1)
                if quarter == 4:
                    wait(pe, "y_ready", t, 2, 1)
                bank, at, G = banks[6 + what], 256 * g, 2 * gp + g
                for tile in range(2):
                    for i in range(4):
                        w = ones[:] if what else V[:, par, tile, 4 * G + i, :]
                        rhs = PTa[:, par, i, G, :] if tile == 0 else PTb[:, par, i, G, :]
                        mm = nc.tensor.matmul(bank[32 * i:32 * i + 32, at + 128 * tile:at + 256], w, rhs,
                                              start=tile == 0, stop=tile == 1, skip_group_check=True)
                mm.then_inc(s["pv_done"], 1)

            def maxima_turned(p):
                if not live(p):
                    return
                wait(pe, "piece_ready", p, 5)
                for t in range(2):
                    for half in range(2):
                        for g in range(4):
                            mm = nc.tensor.matmul(banks[2 * t + half][:, 128 * g:128 * g + 128],
                                                  M[:, t, 4 * half + g, :, :].rearrange("p e c -> p (e c)"), neg_ident[:],
                                                  start=True, stop=True)
                        mm.then_inc(s["mt_done"], 1)

            def output(t):
                if not live(t):
                    return
                wait(pe, "y_ready", t, 2)
                for g in range(A_G):
                    mm = nc.tensor.matmul(banks[6][:, 0:T], Wp[:, g, :], Y[:, g, :], start=g == 0, stop=g == A_G - 1)
                mm.then_inc(s["out_done"], 1)

            def mean(t):
                if not live(t):
                    return
                wait(pe, "r_ready", t)
                nc.tensor.matmul(banks[7][:, 0:T], mean_w[:], r[:], start=True, stop=True).then_inc(s["mean_done"], 1)

            def variance(t):
                if not live(t):
                    return
                wait(pe, "xsq_ready", t)
                nc.tensor.matmul(banks[6][:, 0:T], mean_w[:], xsq[:], start=True, stop=True).then_inc(s["var_done"], 1)

            def slot(k, par):
                p, t, u, was = k - 1, k - 2, k - 3, 1 - par
                project(k, par, 0)
                project(k, par, 1)
                maxima_turned(p)
                variance(u)
                project(k, par, 2)
                for job in range(jobs):
                    scores_turned(p, was, job)
                    if job in QK_AFTER:
                        project(k, par, QK_AFTER[job])
                    for quarter in V_AFTER.get(job, ()):
                        attend(t, par, quarter)
                values(k, par)
                for job in range(jobs):
                    scores(k, par, job)
                    if job == 6:
                        output(t)
                    if job == 9:
                        mean(t)

            run(pe, slot)

        @block.scalar
        def _(act):
            act.wait_ge(s["bias_done"], 1)
            act.wait_ge(s["memset_done"], 5)

            def first_piece(k, job):
                if not live(k):
                    return
                wait(act, "qk_done", k, 8, job + 1)
                half = job // 4
                for g in range(2):
                    G = 2 * (job % 4) + g
                    nc.scalar.activation(first[:, job % 2, 256 * g:256 * g + 256], banks[4 + job % 2][:, 256 * g:256 * g + 256],
                                         ACT.Identity, bias=late_bias[:, half, G:G + 1], scale=later[:, half, 0:1])\
                        .then_inc(s["first_ready"], 1)

            def second_piece(k, job):
                if not live(k):
                    return
                wait(act, "rest_ready", k, 16, 2 * job + 2)
                if job >= 2:
                    wait(act, "split_ready", k, 8, job - 1)
                else:
                    wait(act, "split_ready", k - 1, 8, job + 7)
                nc.scalar.activation(second[:, job % 2, :], rest[:, job % 2, :], ACT.Copy, scale=later[:, job // 4, 1:2])\
                    .then_inc(s["second_ready"], 1)

            def exponentials(p, was, job):
                if not live(p):
                    return
                i, j = divmod(job, 3)
                wait(act, "st_done", p, jobs, job + 1)
                if job == 0:
                    wait(act, "pv_done", p - 2, 8)
                dst = PTb[:, was, i, :, :] if j == 0 else PTa[:, was, i, 2 * (j - 1):2 * j, :]
                nc.scalar.activation(dst.rearrange("p g t -> p (g t)"), banks[job % 4][:], ACT.Exp,
                                     scale=float(A_DH) ** -0.5).then_inc(s["pt_ready"], 1)

            def deviation(t):
                if not live(t):
                    return
                wait(act, "var_done", t)
                wait(act, "rstd_ready", t - 1)
                nc.scalar.activation(std[:], banks[6][:, 0:T], ACT.Sqrt, bias=eps[:, 0:1]).then_inc(s["std_ready"], 1)

            def slot(k, par):
                p, u = k - 1, k - 3
                first_piece(k, 0)
                first_piece(k, 1)
                deviation(u)
                second_piece(k, 0)
                first_piece(k, 2)
                for job in range(jobs):
                    exponentials(p, 1 - par, job)
                    if job in QK_AFTER:
                        second_piece(k, QK_AFTER[job] - 2)
                        first_piece(k, QK_AFTER[job])
                second_piece(k, 6)
                second_piece(k, 7)

            run(act, slot)

        @block.gpsimd
        def _(pool):
            nc.gpsimd.memset(eps[:], 1e-5).then_inc(s["memset_done"], 1)
            nc.gpsimd.memset(mean_w[:], 1.0 / 128).then_inc(s["memset_done"], 1)
            nc.gpsimd.memset(ones[:], 1.0).then_inc(s["memset_done"], 1)
            nc.gpsimd.memset(V[:], 0.0).then_inc(s["memset_done"], 1)
            nc.gpsimd.memset(M[:], 0.0).then_inc(s["memset_done"], 1)

            def third_piece(k, par, job):
                if not live(k):
                    return
                wait(pool, "second_ready", k, 8, job + 1)
                if job == 0:
                    wait(pool, "st_done", k - 2, jobs)
                dst = (qs, ks)[job // 4][:, par, 2 * (job % 4):2 * (job % 4) + 2, :]
                nc.gpsimd.tensor_tensor(dst.rearrange("p g t -> p (g t)"), rest[:, job % 2, :], second[:, job % 2, :], ALU.add)\
                    .then_inc(s["split_ready"], 1)

            def squares(t):
                if not live(t):
                    return
                wait(pool, "xc_ready", t)
                wait(pool, "var_done", t - 1)
                nc.gpsimd.tensor_tensor(xsq[:], xc[:], xc[:], ALU.mult).then_inc(s["xsq_ready"], 1)

            def slot(k, par):
                if live(k):
                    wait(pool, "qk_done", k - 2, 8)
                    wait(pool, "v_done", k - 2)
                    pool.sem_inc(s["gate"], 1)
                    nc.gpsimd.tensor_copy(xf[:, par, :], X[:, k, PAD:]).then_inc(s["xf_ready"], 1)
                squares(k - 3)
                for job in range(8):
                    third_piece(k, par, job)

            run(pool, slot)

        @block.vector
        def _(dve):
            dve.wait_ge(s["w_in"], 16 * n_loads)
            dve.wait_ge(s["memset_done"], 5)
            nc.vector.tensor_tensor(late_bias[:], qk_bias[:], later[:, :, 0:1].to_broadcast([128, 2, A_GP]), ALU.mult)\
                .then_inc(s["bias_done"], 1)

            def rest_of(k, job):
                if not live(k):
                    return
                wait(dve, "first_ready", k, 16, 2 * job + 2)
                if job >= 2:
                    wait(dve, "split_ready", k, 8, job - 1)
                else:
                    wait(dve, "split_ready", k - 1, 8, job + 7)
                for g in range(2):
                    G = 2 * (job % 4) + g
                    cols = slice(256 * g, 256 * g + 256)
                    nc.vector.scalar_tensor_tensor(rest[:, job % 2, cols], banks[4 + job % 2][:, cols],
                                                   qk_bias[:, job // 4, G:G + 1], first[:, job % 2, cols], ALU.add, ALU.add)\
                        .then_inc(s["rest_ready"], 1)

            def values(k, par):
                if not live(k):
                    return
                wait(dve, "v_done", k)
                wait(dve, "pv_done", k - 2, 8)
                nc.vector.tensor_tensor(V[:, par, :, :, 0:A_DH], banks[4][:, 0:256].rearrange("p (t h d) -> p t h d", t=2, d=A_DH),
                                        v_bias[:].rearrange("p (h d) -> p h d", d=A_DH).unsqueeze(1).to_broadcast([128, 2, A_HEADS, A_DH]),
                                        ALU.add).then_inc(s["v_ready"], 1)

            def row_maxima(k, job):
                if not live(k):
                    return
                i, j = divmod(job, 3)
                wait(dve, "s_done", k, jobs, job + 1)
                if job == 0:
                    wait(dve, "piece_ready", k - 1, 5)
                heads = mx[:].rearrange("p t (g i) -> p t g i", i=4)
                if j == 0:
                    dst, src = heads[:, 0, :, i], banks[job % 4][:].rearrange("p (g t) -> p g t", g=4)
                else:
                    dst = heads[:, 1, 2 * (j - 1):2 * j, i]
                    src = banks[job % 4][:].rearrange("p (g t) -> p g t", g=2)
                nc.vector.tensor_reduce(dst, src, AX_X, ALU.max).then_inc(s["max_ready"], 1)

            def pieces_of_maxima(k):
                if not live(k):
                    return
                piece = lambda c: M[:].rearrange("p t g e c -> p t (g e) c")[:, :, :, A_ROWS + c]
                wait(dve, "max_ready", k, jobs)
                wait(dve, "mt_done", k - 1, 4)
                nc.vector.tensor_copy(piece(0), mx[:]).then_inc(s["piece_ready"], 1)
                wait(dve, "piece_ready", k, 5, 1)
                nc.vector.tensor_tensor(mx_rest[:, 0], mx[:], piece(0), ALU.subtract).then_inc(s["piece_ready"], 1)
                wait(dve, "piece_ready", k, 5, 2)
                nc.vector.tensor_copy(piece(1), mx_rest[:, 0]).then_inc(s["piece_ready"], 1)
                wait(dve, "piece_ready", k, 5, 3)
                nc.vector.tensor_tensor(mx_rest[:, 1], mx_rest[:, 0], piece(1), ALU.subtract).then_inc(s["piece_ready"], 1)
                wait(dve, "piece_ready", k, 5, 4)
                nc.vector.tensor_copy(piece(2), mx_rest[:, 1]).then_inc(s["piece_ready"], 1)

            def normalised(p, gp):
                if not live(p):
                    return
                wait(dve, "pv_done", p, 8, 4 * gp + 4)
                if gp == 1:
                    wait(dve, "y_ready", p, 2, 1)
                else:
                    wait(dve, "y_ready", p - 1, 2)
                    wait(dve, "out_done", p - 1)
                nc.vector.reciprocal(rsum[:], banks[7][:]).then_inc(s["rsum_ready"], 1)
                wait(dve, "rsum_ready", p, 2, gp + 1)
                nc.vector.tensor_tensor(Y[:, 2 * gp:2 * gp + 2, :].rearrange("p g t -> p (g t)"), banks[6][:], rsum[:], ALU.mult)\
                    .then_inc(s["y_ready"], 1)

            def take_maxima_off(p, was):
                if not live(p):
                    return
                wait(dve, "s_done", p, jobs)
                for t in range(2):
                    for half in range(2):
                        wait(dve, "mt_done", p, 4, 2 * t + half + 1)
                        part = qs[:, was, 4 * half:4 * half + 4, 128 * t:128 * t + 128]
                        nc.vector.tensor_tensor(part, part, banks[2 * t + half][:].rearrange("p (g t) -> p g t", g=4), ALU.add)\
                            .then_inc(s["q_aug"], 1)

            def residual(t):
                if not live(t):
                    return
                wait(dve, "out_done", t)
                wait(dve, "mean_done", t - 1)
                nc.vector.scalar_tensor_tensor(r[:], banks[6][:, 0:T], p_bias[:, 0:1], X[:, t, PAD:], ALU.add, ALU.add)\
                    .then_inc(s["r_ready"], 1)

            def centred(t):
                if not live(t):
                    return
                wait(dve, "mean_done", t)
                wait(dve, "r_ready", t)
                nc.vector.tensor_tensor(xc[:], r[:], banks[7][:, 0:T], ALU.subtract).then_inc(s["xc_ready"], 1)

            def layernorm(t):
                if not live(t):
                    return
                wait(dve, "std_ready", t)
                nc.vector.reciprocal(rstd[:], std[:]).then_inc(s["rstd_ready"], 1)
                wait(dve, "rstd_ready", t)
                nc.vector.tensor_tensor(X[:, t, PAD:], xc[:], rstd[:], ALU.mult).then_inc(s["x_ready"], 1)
                wait(dve, "x_ready", t)

            def slot(k, par):
                p, t, u = k - 1, k - 2, k - 3
                rest_of(k, 0)
                rest_of(k, 1)
                take_maxima_off(p, 1 - par)
                rest_of(k, 2)
                layernorm(u)
                rest_of(k, 3)
                rest_of(k, 4)
                normalised(t, 0)
                rest_of(k, 5)
                rest_of(k, 6)
                rest_of(k, 7)
                values(k, par)
                for job in range(jobs):
                    row_maxima(k, job)
                    if job == 2:
                        normalised(t, 1)
                    if job == 8:
                        residual(t)
                    if job == 11:
                        centred(t)
                pieces_of_maxima(k)

            run(dve, slot)


def layouts_a(i):
    n = len(Q_PIECES)
    w = np.asarray(i["L0_attn_W_qkv"]).reshape(D, 3, A_GP, 2, 1, A_DH)
    b = np.asarray(i["L0_attn_b_qkv"]).reshape(3, A_GP, 2, 1, A_DH)
    wqk = np.zeros((D, 2, A_GP, 2, 8, A_DH), np.float32)
    wqk[..., :n, :] = w[:, 0:2]
    bias = np.zeros((2, A_GP, 2, 8, A_DH), np.float32)
    bias[..., :n, :] = b[0:2]
    bias = bias.reshape(2, A_GP, 2, 64)
    bias[1, :, :, A_ROWS:A_AUG] = 1.0
    out = {"A_Wqk": wqk.reshape(D, 2, A_GP, 128), "A_qk_bias": bias.reshape(2, A_GP, 128).transpose(2, 0, 1)}
    out["A_Wv"] = w[:, 2].reshape(D, D)
    out["A_v_bias"] = b[2].reshape(D)
    wp = np.zeros((4, 32, A_G, D), np.float32)
    wp[:, :A_DH] = np.asarray(i["L0_attn_W_proj"]).reshape(A_G, 4, A_DH, D).transpose(1, 2, 0, 3)
    out["A_Wp"] = wp.reshape(128, A_G, D)
    out["A_p_bias"] = np.asarray(i["L0_attn_b_proj"]).reshape(D, 1)
    return out


def constants_a():
    late = np.triu(np.ones((128, 128), bool), 1)
    q = np.zeros((128, 256), np.float32)
    q[:, 128:][late] = NEG
    k = np.zeros((128, 256), np.float32)
    k[:, :128][late.T] = NEG
    later = np.zeros((2, 8, A_DH, 2, 2), np.float32)
    for qk, pieces in enumerate((Q_PIECES, K_PIECES)):
        for block, piece in enumerate(pieces):
            later[:, block, :, qk, 0] = -1.0 if piece >= 2 else 0.0
            later[:, block, :, qk, 1] = -1.0 if piece == 3 else 0.0
    b = lambda a: a.astype(mybir.dt.np(BF16))
    eye = np.eye(128, dtype=np.float32)
    return {"A_later": later.reshape(128, 2, 2), "neg_ident": b(-eye), "ident_b": b(eye), "mask_q": b(q), "mask_k": b(k)}


DEPTH = 8
LEAVES = 2 ** DEPTH
LW = 16
CH = LEAVES * LW // 128
NG = 8
GT = SEQS * T // NG
RING = 4


def standardise(nc, dram, X, XN):
    with ExitStack() as ctx:
        def sb(name, shape, dt=F32):
            return ctx.enter_context(nc.sbuf_tensor("n_" + name, shape, dt))

        mean_w = sb("mean_w", [128, 128])
        var_w = sb("var_w", [128, 128])
        eps = sb("eps", [128, 1])
        xc = sb("xc", [128, 2, T])
        xsq = sb("xsq", [128, 2, T])
        sd = sb("sd", [128, 2, T])
        root = sb("root", [128, 2, T])
        inv = sb("inv", [128, 2, T])
        ps = ctx.enter_context(nc.psum_tensor("n_ps", [128, 4, 512], F32))
        names = "memset_done mean_done xc_ready xsq_ready var_done sd_ready root_ready inv_ready xn_ready gate".split()
        s = {n: ctx.enter_context(nc.semaphore("n_" + n)) for n in names}
        ctx.callback(clear_semaphores, nc, s)

        def seq_wait(eng, name, seq):
            eng.wait_ge(s[name], seq + 1)

        block = ctx.enter_context(nc.Block())

        def run(eng, slot):
            slot(0, 0, False)
            slot(1, 1, False)
            with eng.Fori(1, SEQS // 2) as half:
                slot(half * 2, 0, True)
                slot(half * 2 + 1, 1, True)

        @block.tensor
        def _(pe):
            pe.wait_ge(s["memset_done"], 3)

            def slot(k, par, again):
                if again:
                    seq_wait(pe, "xc_ready", k - 2)
                nc.tensor.matmul(ps[:, par, 0:T], mean_w[:], X[:, k, PAD:], start=True, stop=True).then_inc(s["mean_done"], 1)
                seq_wait(pe, "xsq_ready", k)
                if again:
                    seq_wait(pe, "sd_ready", k - 2)
                nc.tensor.matmul(ps[:, 2 + par, 0:T], var_w[:], xsq[:, par, :], start=True, stop=True).then_inc(s["var_done"], 1)

            run(pe, slot)

        @block.scalar
        def _(act):
            act.wait_ge(s["memset_done"], 3)

            def slot(k, par, again):
                seq_wait(act, "var_done", k)
                nc.scalar.activation(sd[:, par, :], ps[:, 2 + par, 0:T], ACT.Sqrt).then_inc(s["sd_ready"], 1)
                seq_wait(act, "sd_ready", k)
                if again:
                    seq_wait(act, "inv_ready", k - 2)
                nc.scalar.activation(root[:, par, :], sd[:, par, :], ACT.Sqrt, bias=eps[:, 0:1]).then_inc(s["root_ready"], 1)

            run(act, slot)

        @block.gpsimd
        def _(pool):
            nc.gpsimd.memset(eps[:], 1e-5).then_inc(s["memset_done"], 1)
            nc.gpsimd.memset(mean_w[:], 1.0 / D).then_inc(s["memset_done"], 1)
            nc.gpsimd.memset(var_w[:], 1.0 / (D - 1)).then_inc(s["memset_done"], 1)

            def slot(k, par, again):
                seq_wait(pool, "xc_ready", k)
                nc.gpsimd.tensor_tensor(xsq[:, par, :], xc[:, par, :], xc[:, par, :], ALU.mult).then_inc(s["xsq_ready"], 1)

            run(pool, slot)

        @block.vector
        def _(dve):
            def slot(k, par, again):
                seq_wait(dve, "mean_done", k)
                if again:
                    seq_wait(dve, "xn_ready", k - 2)
                nc.vector.tensor_tensor(xc[:, par, :], X[:, k, PAD:], ps[:, par, 0:T], ALU.subtract).then_inc(s["xc_ready"], 1)
                seq_wait(dve, "root_ready", k)
                nc.vector.reciprocal(inv[:, par, :], root[:, par, :]).then_inc(s["inv_ready"], 1)
                seq_wait(dve, "inv_ready", k)
                nc.vector.tensor_tensor(XN[:, bass.ds(k * T, T)], xc[:, par, :], inv[:, par, :], ALU.mult).then_inc(s["xn_ready"], 1)

            run(dve, slot)


def fast_feedforwards(nc, dram, modules, act_func):
    with ExitStack() as ctx:
        n_mod = len(modules)
        tag = modules[0][0]

        def sb(name, shape, dt=F32):
            return ctx.enter_context(nc.sbuf_tensor(f"{tag}_{name}", shape, dt))

        nbuf = 2 if n_mod > 1 else 1
        nodes = sb("nodes", [128, nbuf, LEAVES])
        node_b = sb("node_b", [128, nbuf, 2])
        W1 = sb("W1", [128, nbuf, CH * 128])
        b1 = sb("b1", [128, nbuf, CH])
        W2 = sb("W2", [128, nbuf, CH, 128])
        b2 = sb("b2", [128, nbuf, 2, 128])
        paths = sb("paths", [128, 2, LEAVES], BF16)
        rights = sb("rights", [128, 2])
        leaf_no = sb("leaf_no", [128, 2, 128])
        chunk_leaf = sb("chunk_leaf", [128, CH])
        bits = sb("bits", [128, 2, GT], BF16)
        onehot = sb("onehot", [128, 2, 2, GT])
        routed = sb("routed", [128, 2, GT])
        hid = sb("hid", [128, RING, GT])
        hm = sb("hm", [128, RING, GT])
        pp = ctx.enter_context(nc.psum_tensor(f"{tag}_ps_prep", [128, 2, 512], F32))
        ph = ctx.enter_context(nc.psum_tensor(f"{tag}_ps_hid", [128, RING, 512], F32))
        po = ctx.enter_context(nc.psum_tensor(f"{tag}_ps_out", [128, 2, 512], F32))
        names = """consts_in w_in0 w_in1 bits_done bits_ready match_done onehot_ready routed_done routed_ready
            hid_done hid_ready hm_ready second_done out_done out_ready gate_act""".split()
        s = {n: ctx.enter_context(nc.semaphore(f"{tag}_{n}")) for n in names}
        ctx.callback(clear_semaphores, nc, s)

        def group_wait(eng, name, group, per=1, more=None):
            eng.wait_ge(s[name], group * per + (per if more is None else more))

        block = ctx.enter_context(nc.Block())

        def run(eng, slot):
            for m in range(n_mod):
                if m == 0:
                    slot(0, 0, 0, 0, True, False, False)
                    slot(0, 1, 1, 1, True, True, False)
                else:
                    slot(m, m * NG, 0, 0, True, True, True)
                    slot(m, m * NG + 1, 1, 1, True, True, True)
                with eng.Fori(1, NG // 2) as half:
                    slot(m, half * 2 + m * NG, half * 2, 0, True, True, True)
                    slot(m, half * 2 + (m * NG + 1), half * 2 + 1, 1, True, True, True)
            slot(n_mod, n_mod * NG, 0, 0, False, True, True)

        @block.sync
        def _(sp):
            for dst, name in ((paths, "paths"), (rights, "rights"), (leaf_no, "leaf_no"), (chunk_leaf, "chunk_leaf")):
                sp.dma_start(dst[:], dram[name]).then_inc(s["consts_in"], 16)
            for m, (name, _, _) in enumerate(modules):
                buf = m % nbuf
                if m >= nbuf:
                    sp.wait_ge(s["out_done"], NG * (m - nbuf + 1))
                for dst, part in ((nodes, "nw"), (node_b, "nb"), (W1, "w1"), (b1, "b1"), (W2, "w2"), (b2, "b2")):
                    sp.dma_start(dst[:, buf], dram[f"{name}_{part}"]).then_inc(s[f"w_in{buf}"], 16)

        @block.tensor
        def _(pe):
            pe.wait_ge(s["consts_in"], 64)

            def slot(m, n, g, par, cur, prev, pprev):
                q = n - 1
                buf = m % nbuf
                prep = []
                if cur:
                    src = modules[m][1]
                    cols = bass.ds(g * GT, GT)

                    def route_bits(j):
                        if isinstance(n, int) and n % NG == 0 and j == 0:
                            pe.wait_ge(s[f"w_in{buf}"], 96 * (m // nbuf + 1))
                        if prev:
                            group_wait(pe, "routed_ready", q)
                            group_wait(pe, "onehot_ready", q, 2)
                        nc.tensor.matmul(pp[:, j, :], nodes[:, buf, 128 * j:128 * j + 128], src[:, cols], start=True, stop=True)\
                            .then_inc(s["bits_done"], 1)

                    def match(j):
                        group_wait(pe, "bits_ready", n, 2)
                        for half in range(2):
                            mm = nc.tensor.matmul(pp[:, j, :], paths[:, half, 128 * j:128 * j + 128], bits[:, half, :],
                                                  start=half == 0, stop=half == 1)
                        mm.then_inc(s["match_done"], 1)

                    def leaf_number():
                        group_wait(pe, "onehot_ready", n, 2)
                        for half in range(2):
                            mm = nc.tensor.matmul(pp[:, 0, :], leaf_no[:, half, :], onehot[:, par, half, :],
                                                  start=half == 0, stop=half == 1)
                        mm.then_inc(s["routed_done"], 1)

                    prep = [(2, lambda: route_bits(0)), (3, lambda: route_bits(1)), (8, lambda: match(0)),
                            (9, lambda: match(1)), (14, leaf_number)]
                if prev:
                    first = isinstance(n, int) and n % NG == 0
                    qm = m - 1 if first else m
                    qbuf, qpar = qm % nbuf, 1 - par
                    qcols = bass.ds(((NG - 1) if first else g - 1) * GT, GT)
                    qsrc = modules[qm][1]

                    def hidden(c):
                        if c >= RING:
                            group_wait(pe, "hid_ready", q, CH, c - RING + 1)
                        elif pprev:
                            group_wait(pe, "hid_ready", n - 2, CH, CH - RING + c + 1)
                        nc.tensor.matmul(ph[:, c % RING, :], W1[:, qbuf, 128 * c:128 * c + 128], qsrc[:, qcols],
                                         start=True, stop=True).then_inc(s["hid_done"], 1)

                    def second(c):
                        group_wait(pe, "hm_ready", q, CH, c + 1)
                        mm = nc.tensor.matmul(po[:, qpar, :], W2[:, qbuf, c, :], hm[:, c % RING, :], start=False, stop=c == CH - 1)
                        mm.then_inc(s["out_done"] if c == CH - 1 else s["second_done"], 1)

                    if pprev:
                        group_wait(pe, "out_ready", n - 2)
                    for half in range(2):
                        nc.tensor.matmul(po[:, qpar, :], b2[:, qbuf, half, :], onehot[:, qpar, half, :], start=half == 0, stop=False)
                    for c in range(CH + 2):
                        for at, step in prep:
                            if at == c:
                                step()
                        if c < CH:
                            hidden(c)
                        if c >= 2:
                            second(c - 2)
                else:
                    for _, step in prep:
                        step()

            run(pe, slot)

        @block.scalar
        def _(act):
            def slot(m, n, g, par, cur, prev, pprev):
                q = n - 1
                if prev:
                    first = isinstance(n, int) and n % NG == 0
                    qm = m - 1 if first else m
                    qbuf, qpar = qm % nbuf, 1 - par
                    dst = modules[qm][2]
                    qcols = bass.ds(((NG - 1) if first else g - 1) * GT, GT)
                    for c in range(CH):
                        if cur and c == 15:
                            leaf_number(n, par)
                        group_wait(act, "hid_done", q, CH, c + 1)
                        if c >= RING:
                            group_wait(act, "hm_ready", q, CH, c - RING + 1)
                        nc.scalar.activation(hid[:, c % RING, :], ph[:, c % RING, :], act_func, bias=b1[:, qbuf, c:c + 1])\
                            .then_inc(s["hid_ready"], 1)
                    group_wait(act, "out_done", q)
                    act.sem_inc(s["gate_act"], 1)
                    nc.scalar.activation(dst[:, qcols], po[:, qpar, :], ACT.Copy).then_inc(s["out_ready"], 1)
                else:
                    leaf_number(n, par)

            def leaf_number(n, par):
                group_wait(act, "routed_done", n)
                nc.scalar.activation(routed[:, par, :], pp[:, 0, :], ACT.Copy).then_inc(s["routed_ready"], 1)

            run(act, slot)

        @block.vector
        def _(dve):
            dve.wait_ge(s["consts_in"], 64)

            def route_bits(m, n, j, prev):
                group_wait(dve, "bits_done", n, 2, j + 1)
                if prev and j == 0:
                    group_wait(dve, "match_done", n - 1, 2)
                nc.vector.tensor_scalar(bits[:, j, :], pp[:, j, :], node_b[:, m % nbuf, j:j + 1], 0.0, ALU.add, ALU.is_gt)\
                    .then_inc(s["bits_ready"], 1)

            def match(n, par, j, pprev):
                group_wait(dve, "match_done", n, 2, j + 1)
                if pprev and j == 0:
                    group_wait(dve, "out_done", n - 2)
                nc.vector.tensor_scalar(onehot[:, par, j, :], pp[:, j, :], rights[:, j:j + 1], None, ALU.is_equal)\
                    .then_inc(s["onehot_ready"], 1)

            def slot(m, n, g, par, cur, prev, pprev):
                q = n - 1
                if prev:
                    qpar = 1 - par
                    for c in range(CH):
                        if cur and c in (3, 4):
                            route_bits(m, n, c - 3, prev)
                        if cur and c in (9, 10):
                            match(n, par, c - 9, pprev)
                        group_wait(dve, "hid_ready", q, CH, c + 1)
                        if c == 0:
                            group_wait(dve, "routed_ready", q)
                        if c >= RING:
                            group_wait(dve, "second_done", q, CH - 1, c - RING + 1)
                        elif pprev:
                            group_wait(dve, "out_done", n - 2)
                        nc.vector.scalar_tensor_tensor(hm[:, c % RING, :], routed[:, qpar, :], chunk_leaf[:, c:c + 1],
                                                       hid[:, c % RING, :], ALU.is_equal, ALU.mult).then_inc(s["hm_ready"], 1)
                else:
                    for j in range(2):
                        route_bits(m, n, j, prev)
                    for j in range(2):
                        match(n, par, j, pprev)

            run(dve, slot)


def leaf_attention(nc, dram, XN, Q, K, V):
    with ExitStack() as ctx:
        def sb(name, shape, dt=F32):
            return ctx.enter_context(nc.sbuf_tensor("t_" + name, shape, dt))

        ident = sb("ident", [128, 128])
        qf = sb("qf", [128, 2, T])
        vf = sb("vf", [128, 2, T])
        Vt = sb("Vt", [128, 2, T])
        mx = sb("mx", [128, 2])
        nm = sb("nm", [128, 2])
        P = sb("P", [128, 2, T])
        den = sb("den", [128, 2])
        rden = sb("rden", [128, 2])
        Pn = sb("Pn", [128, 2, T])
        PT = sb("PT", [128, 2, T])
        ps_s = ctx.enter_context(nc.psum_tensor("t_s", [128, 512], F32))
        ps_v = ctx.enter_context(nc.psum_tensor("t_v", [128, 512], F32))
        ps_t = ctx.enter_context(nc.psum_tensor("t_t", [128, 512], F32))
        ps_o = ctx.enter_context(nc.psum_tensor("t_o", [128, 512], F32))
        names = """ident_in qf_ready vf_ready s_done mx_ready nm_ready p_ready rden_ready pn_ready pt_done pt_ready
            vt_done vt_ready o_done y_ready gate""".split()
        s = {n: ctx.enter_context(nc.semaphore("t_" + n)) for n in names}
        ctx.callback(clear_semaphores, nc, s)

        def seq_wait(eng, name, seq, per=1, more=None):
            eng.wait_ge(s[name], seq * per + (per if more is None else more))

        scale = float(D) ** -0.5
        block = ctx.enter_context(nc.Block())

        def run(eng, slot):
            slot(0, 0, True, False, False)
            slot(1, 1, True, True, False)
            with eng.Fori(1, SEQS // 2) as half:
                slot(half * 2, 0, True, True, True)
                slot(half * 2 + 1, 1, True, True, True)
            slot(SEQS, 0, False, True, True)

        @block.sync
        def _(sp):
            sp.dma_start(ident[:], dram["ident"]).then_inc(s["ident_in"], 16)

        @block.gpsimd
        def _(pool):
            def slot(k, par, cur, prev, pprev):
                if cur:
                    if pprev:
                        seq_wait(pool, "s_done", k - 2)
                        seq_wait(pool, "vt_done", k - 2)
                        pool.sem_inc(s["gate"], 1)
                    nc.gpsimd.tensor_copy(qf[:, par, :], Q[:, bass.ds(k * T, T)]).then_inc(s["qf_ready"], 1)
                    nc.gpsimd.tensor_copy(vf[:, par, :], V[:, bass.ds(k * T, T)]).then_inc(s["vf_ready"], 1)

            run(pool, slot)

        @block.tensor
        def _(pe):
            pe.wait_ge(s["ident_in"], 16)

            def slot(k, par, cur, prev, pprev):
                p = k - 1
                if cur:
                    seq_wait(pe, "qf_ready", k)
                    if prev:
                        seq_wait(pe, "p_ready", p, 2)
                        seq_wait(pe, "mx_ready", p)
                    for t in range(2):
                        mm = nc.tensor.matmul(ps_s[:, T * t:T * t + T], qf[:, par, 128 * t:128 * t + 128], K[:, bass.ds(k * T, T)],
                                              start=True, stop=True)
                    mm.then_inc(s["s_done"], 1)
                    seq_wait(pe, "vf_ready", k)
                    if prev:
                        seq_wait(pe, "vt_ready", p)
                    for t in range(2):
                        mm = nc.tensor.transpose(ps_v[:, 128 * t:128 * t + 128], vf[:, par, 128 * t:128 * t + 128], ident[:])
                    mm.then_inc(s["vt_done"], 1)
                if prev:
                    seq_wait(pe, "pn_ready", p, 2)
                    if pprev:
                        seq_wait(pe, "pt_ready", k - 2)
                    for tq in range(2):
                        for tk in range(2):
                            mm = nc.tensor.transpose(ps_t[:, T * tk + 128 * tq:T * tk + 128 * tq + 128],
                                                     Pn[:, tq, 128 * tk:128 * tk + 128], ident[:])
                    mm.then_inc(s["pt_done"], 1)
                    seq_wait(pe, "pt_ready", p)
                    seq_wait(pe, "vt_ready", p)
                    if pprev:
                        seq_wait(pe, "y_ready", k - 2)
                    for t in range(2):
                        mm = nc.tensor.matmul(ps_o[:, 0:T], Vt[:, 1 - par, 128 * t:128 * t + 128], PT[:, t, :],
                                              start=t == 0, stop=t == 1)
                    mm.then_inc(s["o_done"], 1)

            run(pe, slot)

        @block.scalar
        def _(act):
            def slot(k, par, cur, prev, pprev):
                p = k - 1
                if cur:
                    seq_wait(act, "nm_ready", k)
                    if prev:
                        seq_wait(act, "pn_ready", p, 2)
                    for t in range(2):
                        nc.scalar.activation(P[:, t, :], ps_s[:, T * t:T * t + T], ACT.Exp, bias=nm[:, t:t + 1], scale=scale,
                                             accum_out=den[:, t:t + 1]).then_inc(s["p_ready"], 1)
                    seq_wait(act, "vt_done", k)
                    if pprev:
                        seq_wait(act, "o_done", k - 2)
                    nc.scalar.activation(Vt[:, par, :], ps_v[:, 0:T], ACT.Copy).then_inc(s["vt_ready"], 1)
                if prev:
                    seq_wait(act, "pt_done", p)
                    if pprev:
                        seq_wait(act, "o_done", k - 2)
                    nc.scalar.activation(PT[:].rearrange("p a t -> p (a t)"), ps_t[:], ACT.Copy).then_inc(s["pt_ready"], 1)

            run(act, slot)

        @block.vector
        def _(dve):
            def slot(k, par, cur, prev, pprev):
                p = k - 1
                if prev:
                    seq_wait(dve, "p_ready", p, 2)
                    nc.vector.reciprocal(rden[:], den[:]).then_inc(s["rden_ready"], 1)
                    seq_wait(dve, "rden_ready", p)
                    if pprev:
                        seq_wait(dve, "pt_done", k - 2)
                    for t in range(2):
                        nc.vector.tensor_scalar(Pn[:, t, :], P[:, t, :], rden[:, t:t + 1], None, ALU.mult).then_inc(s["pn_ready"], 1)
                if cur:
                    seq_wait(dve, "s_done", k)
                    nc.vector.tensor_reduce(mx[:], ps_s[:].rearrange("p (t k) -> p t k", t=2), AX_X, ALU.max).then_inc(s["mx_ready"], 1)
                    seq_wait(dve, "mx_ready", k)
                    nc.vector.tensor_scalar(nm[:], mx[:], -scale, None, ALU.mult).then_inc(s["nm_ready"], 1)
                if prev:
                    seq_wait(dve, "o_done", p)
                    part = XN[:, bass.ds(p * T, T)]
                    nc.vector.tensor_tensor(part, part, ps_o[:, 0:T], ALU.add).then_inc(s["y_ready"], 1)

            run(dve, slot)


def add_and_norm(nc, X, Y, Z, tag):
    with ExitStack() as ctx:
        def sb(name, shape, dt=F32):
            return ctx.enter_context(nc.sbuf_tensor(f"{tag}_{name}", shape, dt))

        mean_w = sb("mean_w", [128, 128])
        eps = sb("eps", [128, 1])
        yz = sb("yz", [128, 2, T])
        r = sb("r", [128, 2, T])
        xc = sb("xc", [128, 2, T])
        xsq = sb("xsq", [128, 2, T])
        std = sb("std", [128, 2, T])
        rstd = sb("rstd", [128, 2, T])
        ps = ctx.enter_context(nc.psum_tensor(f"{tag}_ps", [128, 4, 512], F32))
        names = "memset_done yz_ready r_ready mean_done xc_ready xsq_ready var_done std_ready rstd_ready x_ready".split()
        s = {n: ctx.enter_context(nc.semaphore(f"{tag}_{n}")) for n in names}
        ctx.callback(clear_semaphores, nc, s)

        def seq_wait(eng, name, seq):
            eng.wait_ge(s[name], seq + 1)

        block = ctx.enter_context(nc.Block())

        def run(eng, slot):
            slot(0, 0, False)
            slot(1, 1, False)
            with eng.Fori(1, SEQS // 2) as half:
                slot(half * 2, 0, True)
                slot(half * 2 + 1, 1, True)

        @block.tensor
        def _(pe):
            pe.wait_ge(s["memset_done"], 2)

            def slot(k, par, again):
                seq_wait(pe, "r_ready", k)
                if again:
                    seq_wait(pe, "xc_ready", k - 2)
                nc.tensor.matmul(ps[:, par, 0:T], mean_w[:], r[:, par, :], start=True, stop=True).then_inc(s["mean_done"], 1)
                seq_wait(pe, "xsq_ready", k)
                if again:
                    seq_wait(pe, "std_ready", k - 2)
                nc.tensor.matmul(ps[:, 2 + par, 0:T], mean_w[:], xsq[:, par, :], start=True, stop=True).then_inc(s["var_done"], 1)

            run(pe, slot)

        @block.scalar
        def _(act):
            act.wait_ge(s["memset_done"], 2)

            def slot(k, par, again):
                seq_wait(act, "var_done", k)
                if again:
                    seq_wait(act, "rstd_ready", k - 2)
                nc.scalar.activation(std[:, par, :], ps[:, 2 + par, 0:T], ACT.Sqrt, bias=eps[:, 0:1]).then_inc(s["std_ready"], 1)

            run(act, slot)

        @block.gpsimd
        def _(pool):
            nc.gpsimd.memset(eps[:], 1e-5).then_inc(s["memset_done"], 1)
            nc.gpsimd.memset(mean_w[:], 1.0 / D).then_inc(s["memset_done"], 1)

            def slot(k, par, again):
                seq_wait(pool, "xc_ready", k)
                if again:
                    seq_wait(pool, "var_done", k - 2)
                nc.gpsimd.tensor_tensor(xsq[:, par, :], xc[:, par, :], xc[:, par, :], ALU.mult).then_inc(s["xsq_ready"], 1)

            run(pool, slot)

        @block.vector
        def _(dve):
            def slot(k, par, again):
                cols = bass.ds(k * T, T)
                if again:
                    seq_wait(dve, "r_ready", k - 2)
                if Z is not None:
                    nc.vector.tensor_tensor(yz[:, par, :], Y[:, cols], Z[:, cols], ALU.add).then_inc(s["yz_ready"], 1)
                    seq_wait(dve, "yz_ready", k)
                if again:
                    seq_wait(dve, "mean_done", k - 2)
                nc.vector.tensor_tensor(r[:, par, :], X[:, k, PAD:], yz[:, par, :] if Z is not None else Y[:, cols], ALU.add)\
                    .then_inc(s["r_ready"], 1)
                seq_wait(dve, "mean_done", k)
                seq_wait(dve, "r_ready", k)
                if again:
                    seq_wait(dve, "x_ready", k - 2)
                nc.vector.tensor_tensor(xc[:, par, :], r[:, par, :], ps[:, par, 0:T], ALU.subtract).then_inc(s["xc_ready"], 1)
                seq_wait(dve, "std_ready", k)
                nc.vector.reciprocal(rstd[:, par, :], std[:, par, :]).then_inc(s["rstd_ready"], 1)
                seq_wait(dve, "rstd_ready", k)
                nc.vector.tensor_tensor(X[:, k, PAD:], xc[:, par, :], rstd[:, par, :], ALU.mult).then_inc(s["x_ready"], 1)

            run(dve, slot)


def fast_feedforward_block(nc, dram, X):
    with ExitStack() as ctx:
        def flat(name):
            return ctx.enter_context(nc.sbuf_tensor(name, [128, SEQS * T], F32))

        XN, Q, K, V = flat("b_XN"), flat("b_Q"), flat("b_K"), flat("b_V")
        standardise(nc, dram, X, XN)
        fast_feedforwards(nc, dram, [("q", XN, Q), ("k", XN, K), ("v", XN, V)], ACT.Relu)
        leaf_attention(nc, dram, XN, Q, K, V)
        fast_feedforwards(nc, dram, [("f", XN, Q)], ACT.Gelu)
        add_and_norm(nc, X, XN, Q, "l")


def layouts_b(i):
    out = {}
    for m in "qkvf":
        a = lambda n: np.asarray(i[f"L0_ffn_{m}_{n}"])
        nw = np.zeros((LEAVES, D), np.float32)
        nw[:LEAVES - 1] = a("nw")
        nb = np.zeros(LEAVES, np.float32)
        nb[:LEAVES - 1] = a("nb")
        out[m + "_nw"] = nw.T
        out[m + "_nb"] = nb.reshape(2, 128).T
        out[m + "_w1"] = a("w1").transpose(1, 0, 2).reshape(D, LEAVES * LW)
        out[m + "_b1"] = a("b1").reshape(CH, 128).T
        out[m + "_w2"] = a("w2").reshape(CH, 128, D).transpose(1, 0, 2)
        out[m + "_b2"] = a("b2").reshape(2, 128, D).transpose(1, 0, 2)
    return out


def constants_b():
    paths = np.zeros((LEAVES, LEAVES), np.float32)
    for leaf in range(LEAVES):
        node = 0
        for level in range(DEPTH):
            right = (leaf >> (DEPTH - 1 - level)) & 1
            paths[node, leaf] = 1.0 if right else -1.0
            node = 2 * node + 1 + right
    rights = (paths > 0).sum(0).astype(np.float32)
    number = np.arange(LEAVES, dtype=np.float32).reshape(2, 128)
    return {"paths": paths.reshape(2, 128, LEAVES).transpose(1, 0, 2).astype(mybir.dt.np(BF16)),
            "rights": rights.reshape(2, 128).T,
            "leaf_no": np.repeat(number.T[:, :, None], 128, 2),
            "chunk_leaf": (8 * np.arange(CH)[None, :] + np.arange(128)[:, None] // LW).astype(np.float32),
            "ident": np.eye(128, dtype=np.float32)}




def gated_scan(nc, dram, X, X0):
    with ExitStack() as ctx:
        def sb(name, shape, dt=F32):
            return ctx.enter_context(nc.sbuf_tensor("c_" + name, shape, dt))

        W = sb("W", [128, 3, 128])
        bias = sb("bias", [128, 3])
        mean_w = sb("mean_w", [128, 128])
        eps = sb("eps", [128, 1])
        gate = sb("gate", [128, 3, T])
        u = sb("u", [128, T])
        a = sb("a", [128, T])
        h = sb("h", [128, T])
        r = sb("r", [128, 2, T])
        xc = sb("xc", [128, T])
        xsq = sb("xsq", [128, T])
        std = sb("std", [128, T])
        rstd = sb("rstd", [128, T])
        ps = ctx.enter_context(nc.psum_tensor("c_gates", [128, 3, 512], F32))
        ps_mean = ctx.enter_context(nc.psum_tensor("c_mean", [128, 512], F32))
        ps_var = ctx.enter_context(nc.psum_tensor("c_var", [128, 512], F32))
        names = """w_in memset_done gates_done gate_ready u_ready a_ready h_ready r_ready mean_done xc_ready
            xsq_ready var_done std_ready rstd_ready x_ready copied gate""".split()
        s = {n: ctx.enter_context(nc.semaphore("c_" + n)) for n in names}
        ctx.callback(clear_semaphores, nc, s)

        def seq_wait(eng, name, seq, per=1, more=None):
            eng.wait_ge(s[name], seq * per + (per if more is None else more))

        block = ctx.enter_context(nc.Block())

        def run(eng, slot):
            slot(0, 0, True, False, False)
            slot(1, 1, True, True, False)
            with eng.Fori(1, SEQS // 2) as half:
                slot(half * 2, 0, True, True, True)
                slot(half * 2 + 1, 1, True, True, True)
            slot(SEQS, 0, False, True, True)

        @block.sync
        def _(sp):
            sp.dma_start(W[:], dram["C_W"]).then_inc(s["w_in"], 16)
            sp.dma_start(bias[:], dram["C_bias"]).then_inc(s["w_in"], 16)

        @block.tensor
        def _(pe):
            pe.wait_ge(s["w_in"], 32)
            pe.wait_ge(s["memset_done"], 2)

            def slot(k, par, cur, prev, pprev):
                p = k - 1
                if cur:
                    if prev:
                        seq_wait(pe, "gate_ready", p, 3)
                    for n in range(3):
                        nc.tensor.matmul(ps[:, n, 0:T], W[:, n, :], X[:, k, PAD:], start=True, stop=True)\
                            .then_inc(s["gates_done"], 1)
                if prev:
                    seq_wait(pe, "r_ready", p)
                    if pprev:
                        seq_wait(pe, "xc_ready", k - 2)
                    nc.tensor.matmul(ps_mean[:, 0:T], mean_w[:], r[:, 1 - par, :], start=True, stop=True).then_inc(s["mean_done"], 1)
                    seq_wait(pe, "xsq_ready", p)
                    if pprev:
                        seq_wait(pe, "std_ready", k - 2)
                    nc.tensor.matmul(ps_var[:, 0:T], mean_w[:], xsq[:], start=True, stop=True).then_inc(s["var_done"], 1)

            run(pe, slot)

        @block.scalar
        def _(act):
            act.wait_ge(s["memset_done"], 2)
            act.wait_ge(s["w_in"], 32)

            def slot(k, par, cur, prev, pprev):
                p = k - 1
                if cur:
                    if prev:
                        seq_wait(act, "a_ready", p)
                        seq_wait(act, "u_ready", p)
                    for n in range(3):
                        seq_wait(act, "gates_done", k, 3, n + 1)
                        nc.scalar.activation(gate[:, n, :], ps[:, n, 0:T], (ACT.Sigmoid, ACT.Tanh, ACT.Sigmoid)[n],
                                             bias=bias[:, n:n + 1]).then_inc(s["gate_ready"], 1)
                if prev:
                    seq_wait(act, "var_done", p)
                    if pprev:
                        seq_wait(act, "rstd_ready", k - 2)
                    nc.scalar.activation(std[:], ps_var[:, 0:T], ACT.Sqrt, bias=eps[:, 0:1]).then_inc(s["std_ready"], 1)

            run(act, slot)

        @block.gpsimd
        def _(pool):
            nc.gpsimd.memset(eps[:], 1e-5).then_inc(s["memset_done"], 1)
            nc.gpsimd.memset(mean_w[:], 1.0 / 128).then_inc(s["memset_done"], 1)

            def slot(k, par, cur, prev, pprev):
                p = k - 1
                if prev:
                    seq_wait(pool, "xc_ready", p)
                    if pprev:
                        seq_wait(pool, "var_done", k - 2)
                    nc.gpsimd.tensor_tensor(xsq[:], xc[:], xc[:], ALU.mult).then_inc(s["xsq_ready"], 1)
                    seq_wait(pool, "x_ready", p)
                    seq_wait(pool, "r_ready", p)
                    pool.sem_inc(s["gate"], 1)
                    nc.gpsimd.tensor_copy(X[:, p, PAD:], X0[:, bass.ds(p * T, T)]).then_inc(s["copied"], 1)

            run(pool, slot)

        @block.vector
        def _(dve):
            def slot(k, par, cur, prev, pprev):
                p = k - 1
                if prev:
                    seq_wait(dve, "mean_done", p)
                    if pprev:
                        seq_wait(dve, "x_ready", k - 2)
                    nc.vector.tensor_tensor(xc[:], r[:, 1 - par, :], ps_mean[:, 0:T], ALU.subtract).then_inc(s["xc_ready"], 1)
                if cur:
                    seq_wait(dve, "gate_ready", k, 3)
                    if prev:
                        seq_wait(dve, "h_ready", p)
                    nc.vector.tensor_tensor(u[:], gate[:, 0, :], gate[:, 1, :], ALU.mult).then_inc(s["u_ready"], 1)
                    nc.vector.tensor_scalar(a[:], gate[:, 2, :], 0.998, 0.001, ALU.mult, ALU.add).then_inc(s["a_ready"], 1)
                    seq_wait(dve, "u_ready", k)
                    seq_wait(dve, "a_ready", k)
                    if prev:
                        seq_wait(dve, "r_ready", p)
                    nc.vector.tensor_tensor_scan(h[:], a[:], u[:], 0.0, ALU.mult, ALU.add).then_inc(s["h_ready"], 1)
                    seq_wait(dve, "h_ready", k)
                    if pprev:
                        seq_wait(dve, "mean_done", k - 2)
                    nc.vector.tensor_tensor(r[:, par, :], X[:, k, PAD:], h[:], ALU.add).then_inc(s["r_ready"], 1)
                if prev:
                    seq_wait(dve, "std_ready", p)
                    nc.vector.reciprocal(rstd[:], std[:]).then_inc(s["rstd_ready"], 1)
                    seq_wait(dve, "rstd_ready", p)
                    nc.vector.tensor_tensor(X0[:, bass.ds(p * T, T)], xc[:], rstd[:], ALU.mult).then_inc(s["x_ready"], 1)

            run(dve, slot)


def layouts_c(i):
    return {"C_W": np.stack([np.asarray(i["L1_attn_W" + n]).T for n in "gvd"], 1),
            "C_bias": np.stack([np.asarray(i["L1_attn_b" + n]) for n in "gvd"], 1)}


LAYERS = 6
TILES = LAYERS * SEQS * 2
HEADS = 16
DH = 64
WIN = 32
INNER = HEADS * DH
HP = HEADS // 2
HID = 341
HCH = 3
HROWS = [128, 128, HID - 256]
HEAD_COLS = HP * DH


def local_attention_layers(nc, dram, X, XM):
    with ExitStack() as ctx:
        def sb(name, shape, dt=F32):
            return ctx.enter_context(nc.sbuf_tensor(name, shape, dt))

        Wqk_high = sb("d_Wqk_high", [128, 2 * INNER], F32R)
        Wqk_low = sb("d_Wqk_low", [128, 2 * INNER], F32R)        
        Wv = sb("d_Wv", [128, 2, HEAD_COLS])
        W_whole = sb("d_W_whole", [128, 2, 512])
        W_cut = sb("d_W_cut", [128, 512])
        Wo = sb("d_Wo", [128, HP, 128])
        W1 = sb("d_W1", [128, 2 * HID])
        W2 = sb("d_W2", [128, HCH, 128])
        vecs = sb("d_vecs", [128, 9])
        qkscale = sb("d_qkscale", [128, 2, DH])
        rot_const = sb("d_rot_const", [128, 2, 2, 2, DH])
        rot = sb("d_rot", [128, 2, 2, 2, DH])
        mask = sb("d_mask", [128, 2, DH])
        ident = sb("d_ident", [128, 128])
        mean_w = sb("d_mean_w", [128, 128])
        eps = sb("d_eps", [128, 1])
        preload = sb("d_preload", [128, 2])
        xs = sb("d_xs", [128, 2, WIN + 128])
        xs_cut = sb("d_xs_cut", [128, 128])
        xs_high = sb("d_xs_high", [128, 128], F32R)
        xs_low = sb("d_xs_low", [128, 128], F32R)
        raw = sb("d_raw", [128, 2 * INNER])
        sq = sb("d_sq", [128, 2, INNER])
        rs = sb("d_rs", [128, 2 * INNER])
        rc = sb("d_rc", [128, 2 * INNER])
        ss = sb("d_ss", [128, 2, HEADS])
        length = sb("d_length", [128, 2, HEADS])
        norm = sb("d_norm", [128, 2, HEADS])
        inv = sb("d_inv", [128, 2, HEADS])
        QT = sb("d_QT", [128, HP, 128])
        KT = sb("d_KT", [128, HP, WIN + 256])
        sm = sb("d_sm", [128, 2, HP, DH])
        sc = sb("d_sc", [128, 2, HP, DH])
        mx = sb("d_mx", [128, HEADS])
        P = sb("d_P", [128, HP, 2, DH])
        den = sb("d_den", [128, HEADS])
        rden = sb("d_rden", [128, HEADS])
        PT = sb("d_PT", [128, HP, 128])
        VP = sb("d_VP", [128, 4, HEAD_COLS])
        On = sb("d_On", [128, HP, 2, DH])
        OT = sb("d_OT", [128, HP, 128])
        xs2 = sb("d_xs2", [128, 128])
        xc = sb("d_xc", [128, 128])
        xsq = sb("d_xsq", [128, 128])
        std = sb("d_std", [128, 128])
        rstd = sb("d_rstd", [128, 128])
        xh = sb("d_xh", [128, 128])
        xn = sb("d_xn", [128, 128])
        G = sb("d_G", [128, HCH, 128])
        H = sb("d_H", [128, HCH, 128])
        pair = [ctx.enter_context(nc.psum_tensor(f"d_pair{i}", [128, 2, 512], F32)) for i in range(3)]
        b6 = ctx.enter_context(nc.psum_tensor("d_b6", [128, 512], F32))
        b7 = ctx.enter_context(nc.psum_tensor("d_b7", [128, 512], F32))
        b0, b1, b2, b3 = pair[0][:, 0, :], pair[0][:, 1, :], pair[1][:, 0, :], pair[1][:, 1, :]
        q_pair = k_pair = pair[2]
        v_bank = (b2, b7[:], b6[:], b1)

        names = """w_in0 w_in1 wv_in wo_in w1_in w2_in vecs_in qks_in consts_in memset_done tables_q tables_k
            w_cut w_high w_split xs_cut xs_high xs_split
            xs_ready qkq_done qkk_done sqq_ready rawq_ready sqk_ready rawk_ready ssq_ready ssk_ready
            len_ready norm_ready inv_ready rsq_ready rsk_ready rcq_ready rck_ready addq_ready addk_ready
            finq_ready fink_ready tq_done tk_done qt_ready kt_ready s_done sm_ready mx_ready sc_ready
            p_ready den_ready rden_ready v0_done v1_done v2_done v3_done vp0_ready vp1_ready vp2_ready
            vp3_ready pt_done pt_ready pv_done on_ready ot_done ot_ready proj_done xm_ready xs2_ready
            mean_done xc_ready xsq_ready var_done std_ready rstd_ready xh_ready xn_ready upa_done
            upg_done g_ready h_ready down_done x_ready sqrt_loaded gelu_loaded gate_pe gate_pool gate_sp""".split()
        s = {n: ctx.enter_context(nc.semaphore("d_" + n)) for n in names}
        ctx.callback(clear_semaphores, nc, s)

        def wait(eng, name, t, ahead=0, per=1, part=None):
            tile = t.k + ahead
            if isinstance(tile, int) and not 0 <= tile < TILES:
                return
            eng.wait_ge(s[name], tile * per + (per if part is None else part))

        class Tile:

            def __init__(self, l, b, par, behind):
                shift = (par - behind) // 2
                self.k = l * 32 + b * 2 + par - behind
                self.par = (par - behind) % 2
                self.b, self.l = (b + shift if shift else b), l
                if isinstance(self.b, int) and self.b < 0:
                    self.b, self.l = self.b + SEQS, l - 1
                self.live = not isinstance(self.k, int) or 0 <= self.k < TILES
                self.first = isinstance(self.b, int) and self.b == 0 and self.par == 0

        def run(eng, slot):
            def sequence(l, b):
                for par in range(2):
                    slot(lambda behind: Tile(l, b, par, behind))

            def layer(l):
                sequence(l, 0)
                sequence(l, 1)
                sequence(l, 2)
                with eng.Fori(3, SEQS) as b:
                    sequence(l, b)

            layer(0)
            with eng.Fori(1, LAYERS) as l:
                layer(l)
            sequence(LAYERS, 0)
            sequence(LAYERS, 1)

        def columns(stream, t, ahead=0, shift=0):
            lo = PAD + 128 * t.par - ahead - shift
            return stream[:, t.b, lo:lo + 128 + ahead]

        def by_head(flat, half):
            return flat[:, INNER * half:INNER * half + INNER].rearrange("p (h d) -> p h d", d=DH)

        def flat_pair(ps):
            return ps[:].rearrange("p a n -> p (a n)")

        W_CHUNKS = ((1, 0), (1, 512), (0, 0), (0, 512))
        w_dram = dram["Wqkv"]
        block = ctx.enter_context(nc.Block())

        @block.sync
        def _(sp):
            sp.dma_start(ident[:], dram["ident"]).then_inc(s["consts_in"], 16)
            sp.dma_start(rot_const[:], dram["rotary"]).then_inc(s["consts_in"], 16)
            sp.dma_start(mask[:], dram["window_mask"]).then_inc(s["consts_in"], 16)

            def load(l, again):
                def layer(ap):
                    return ap[bass.ds(l, 1)]
                if again:
                    sp.wait_ge(s["tables_q"], 4 * l)
                    sp.wait_ge(s["tables_k"], 4 * l)
                sp.dma_start(qkscale[:], layer(dram["qk_scale"]).rearrange("o a d -> (o a d)").partition_broadcast(128)
                             .rearrange("p (a d) -> p a d", a=2)).then_inc(s["qks_in"], 16)
                for c, (half, first) in enumerate(W_CHUNKS):
                    if c >= 2 or again:
                        sp.wait_ge(s["w_split"], 4 * l + c - 1)
                        sp.sem_inc(s["gate_sp"], 1)
                    sp.dma_start(W_whole[:, c % 2, :], layer(w_dram)[:, :, half, first:first + 512].rearrange("o p n -> p (o n)"))\
                        .then_inc(s[f"w_in{c % 2}"], 16)
                if again:
                    sp.wait_ge(s["v3_done"], 32 * l)
                for odd in range(2):
                    sp.dma_start(Wv[:, odd, :], layer(dram["Wv"])[:, :, odd, :].rearrange("o p n -> p (o n)")).then_inc(s["wv_in"], 16)
                if again:
                    sp.wait_ge(s["proj_done"], 32 * l)
                sp.dma_start(Wo[:], layer(dram["Wo"]).rearrange("o (h p) n -> p (o h) n", p=128)).then_inc(s["wo_in"], 16)
                if again:
                    sp.wait_ge(s["down_done"], 32 * l)
                    sp.wait_ge(s["x_ready"], 32 * l)
                sp.dma_start(vecs[:], layer(dram["vecs"]).rearrange("o p n -> p (o n)")).then_inc(s["vecs_in"], 16)
                sp.dma_start(W1[:], layer(dram["W1"]).rearrange("o p n -> p (o n)")).then_inc(s["w1_in"], 16)
                sp.dma_start(W2[:], layer(dram["W2"]).rearrange("o p c n -> p (o c) n")).then_inc(s["w2_in"], 16)

            load(0, False)
            with sp.Fori(1, LAYERS) as l:
                load(l, True)

        @block.tensor
        def _(pe):
            pe.wait_ge(s["consts_in"], 48)
            pe.wait_ge(s["memset_done"], 5)

            def qk_half(t, half, ps, done, parts=(0, 1)):
                for j in parts:
                    c = INNER * half + 512 * j
                    for n, (x_part, w_part) in enumerate(((xs_high, Wqk_high), (xs_high, Wqk_low), (xs_low, Wqk_high))):
                        mm = nc.tensor.matmul(ps[:, j, :], x_part[:], w_part[:, c:c + 512], start=n == 0, stop=n == 2)
                if j == 1:
                    mm.then_inc(s[done], 1)

            def keys(t, part):
                if not t.live:
                    return
                if part == 1:
                    return qk_half(t, 1, k_pair, "qkk_done", (1,))
                if t.first:
                    pe.wait_ge(s["w_split"], 4 * t.l + 2)
                wait(pe, "xs_split", t)
                wait(pe, "kt_ready", t, -1)
                qk_half(t, 1, k_pair, "qkk_done", (0,))

            def queries(t):
                if not t.live:
                    return
                if t.first:
                    pe.wait_ge(s["w_split"], 4 * t.l + 4)
                wait(pe, "sqk_ready", t)
                wait(pe, "rawk_ready", t)
                qk_half(t, 0, q_pair, "qkq_done")

            def turn(t, ps, source, done):
                for hp in range(HP):
                    mm = nc.tensor.transpose(ps[:, hp // 4, (hp % 4) * 128:(hp % 4) * 128 + 128], source(hp), ident[:])
                mm.then_inc(s[done], 1)

            def queries_turned(t):
                if not t.live:
                    return
                wait(pe, "finq_ready", t)
                wait(pe, "std_ready", t, -2)
                wait(pe, "vp3_ready", t, -1)
                turn(t, pair[0], lambda hp: rc[:, hp * 128:hp * 128 + 128], "tq_done")

            def keys_turned(t):
                if not t.live:
                    return
                wait(pe, "fink_ready", t)
                wait(pe, "ot_ready", t, -2)
                turn(t, pair[2], lambda hp: rc[:, INNER + hp * 128:INNER + hp * 128 + 128], "tk_done")

            def scores(t, part):
                if not t.live:
                    return
                if part == 0:
                    wait(pe, "kt_ready", t)
                    wait(pe, "qt_ready", t)
                    pe.sem_inc(s["gate_pe"], 1)
                at = 128 * t.par
                for hp in range(HP // 2 * part, HP // 2 * (part + 1)):
                    for odd in range(2):
                        rows = slice(64 * odd, 64 * odd + 64)
                        for w in range(4):
                            mm = nc.tensor.matmul(
                                pair[0][WIN * w:WIN * w + WIN, odd, hp * DH:hp * DH + DH],
                                QT[rows, hp, WIN * w:WIN * w + WIN],
                                KT[rows, hp, at + WIN * w:at + WIN * w + 2 * WIN], start=True, stop=True)
                if part == 1:
                    mm.then_inc(s["s_done"], 1)

            def values(t, w):
                if not t.live:
                    return
                if t.first and w == 2:
                    pe.wait_ge(s["wv_in"], 32 * t.l + 32)
                if w == 0:
                    wait(pe, "on_ready", t, -1)
                if w == 1:
                    wait(pe, "g_ready", t, -2, HCH)
                if w == 2:
                    wait(pe, "xc_ready", t, -2)
                    wait(pe, "xs_ready", t, per=2)
                if w == 3:
                    wait(pe, "sm_ready", t)
                for odd in range(2):
                    mm = nc.tensor.matmul(v_bank[w][64 * odd:64 * odd + 64, :],
                                          xs[:, t.par, WIN * w:WIN * w + 2 * WIN], Wv[:, odd, :], start=True, stop=True)
                mm.then_inc(s[f"v{w}_done"], 1)

            def probabilities_turned(t):
                if not t.live:
                    return
                wait(pe, "p_ready", t)
                wait(pe, "vp0_ready", t)
                wait(pe, "xm_ready", t, -1)
                turn(t, pair[1], lambda hp: P[:, hp, :, :].rearrange("p a d -> p (a d)"), "pt_done")

            def attend(t, part):
                if not t.live:
                    return
                if part == 0:
                    wait(pe, "vp3_ready", t)
                    wait(pe, "pt_ready", t)
                    pe.sem_inc(s["gate_pe"], 1)
                for hp in range(HP // 2 * part, HP // 2 * (part + 1)):
                    for odd in range(2):
                        rows = slice(64 * odd, 64 * odd + 64)
                        for w in range(4):
                            mm = nc.tensor.matmul(
                                pair[1][WIN * w:WIN * w + WIN, odd, hp * DH:hp * DH + DH],
                                PT[rows, hp, WIN * w:WIN * w + WIN],
                                VP[rows, w, hp * DH:hp * DH + DH], start=True, stop=True)
                if part == 1:
                    mm.then_inc(s["pv_done"], 1)

            def attention_turned(t):
                if not t.live:
                    return
                wait(pe, "on_ready", t)
                wait(pe, "sqq_ready", t, 2)
                wait(pe, "rawq_ready", t, 2)
                turn(t, pair[2], lambda hp: On[:, hp, :, :].rearrange("p a d -> p (a d)"), "ot_done")

            def project(t):
                if not t.live:
                    return
                if t.first:
                    pe.wait_ge(s["wo_in"], 16 * t.l + 16)
                wait(pe, "ot_ready", t)
                for hp in range(HP):
                    mm = nc.tensor.matmul(b3[:, 0:128], Wo[:, hp, :], OT[:, hp, :], start=hp == 0, stop=hp == HP - 1)
                mm.then_inc(s["proj_done"], 1)

            def mean(t):
                if not t.live:
                    return
                wait(pe, "xs2_ready", t, per=2)
                wait(pe, "h_ready", t, -1, HCH)
                nc.tensor.matmul(b6[:, 0:128], mean_w[:], xs2[:], start=True, stop=True).then_inc(s["mean_done"], 1)

            def variance(t):
                if not t.live:
                    return
                wait(pe, "xsq_ready", t)
                wait(pe, "x_ready", t, -1)
                nc.tensor.matmul(b0[:, 0:128], mean_w[:], xsq[:], start=True, stop=True).then_inc(s["var_done"], 1)

            def hidden(t, side, ps, done):
                for c in range(HCH):
                    at = HID * side + 128 * c
                    mm = nc.tensor.matmul(ps[0:HROWS[c], 128 * c:128 * c + 128], W1[:, at:at + HROWS[c]], xn[:],
                                          start=True, stop=True)
                mm.then_inc(s[done], 1)

            def hidden_a(t):
                if not t.live:
                    return
                if t.first:
                    pe.wait_ge(s["w1_in"], 16 * t.l + 16)
                wait(pe, "xn_ready", t)
                wait(pe, "vp2_ready", t, 2)
                hidden(t, 0, b6, "upa_done")

            def hidden_gate(t):
                if not t.live:
                    return
                wait(pe, "vp1_ready", t, 1)
                hidden(t, 1, b7, "upg_done")

            def down(t):
                if not t.live:
                    return
                if t.first:
                    pe.wait_ge(s["w2_in"], 16 * t.l + 16)
                wait(pe, "h_ready", t, 0, HCH)
                wait(pe, "sm_ready", t, 2)
                for c in range(HCH):
                    mm = nc.tensor.matmul(b0[:, 0:128], W2[0:HROWS[c], c, :], H[0:HROWS[c], c, :],
                                          start=c == 0, stop=c == HCH - 1)
                mm.then_inc(s["down_done"], 1)

            def slot(tile):
                values(tile(2), 2)
                variance(tile(4))
                keys(tile(1), 0)
                attend(tile(3), 0)
                keys(tile(1), 1)
                attend(tile(3), 1)
                queries_turned(tile(2))
                queries(tile(1))
                scores(tile(2), 0)
                values(tile(2), 0)
                scores(tile(2), 1)
                attention_turned(tile(3))
                hidden_a(tile(4))
                hidden_gate(tile(4))
                project(tile(3))
                values(tile(2), 1)
                values(tile(2), 3)
                down(tile(4))
                keys_turned(tile(1))
                mean(tile(3))
                probabilities_turned(tile(2))

            run(pe, slot)

        @block.scalar
        def _(act):
            act.wait_ge(s["memset_done"], 5)

            def take(t, half, ps, qk):
                if not t.live:
                    return
                wait(act, f"qk{qk}_done", t)
                wait(act, f"ss{qk}_ready", t, -1)
                nc.scalar.activation(sq[:, half, :], flat_pair(ps), ACT.Square).then_inc(s[f"sq{qk}_ready"], 1)
                wait(act, f"rc{qk}_ready", t, -1)
                wait(act, f"rs{qk}_ready", t, -1)
                nc.scalar.activation(raw[:, INNER * half:INNER * half + INNER], flat_pair(ps), ACT.Copy)\
                    .then_inc(s[f"raw{qk}_ready"], 1)

            def lengths(t):
                if not t.live:
                    return
                wait(act, "ssk_ready", t)
                wait(act, "ssq_ready", t)
                wait(act, "norm_ready", t, -1)
                nc.scalar.activation(length[:], ss[:], ACT.Sqrt).then_inc(s["len_ready"], 1)

            def take_queries_turned(t):
                if not t.live:
                    return
                wait(act, "tq_done", t)
                wait(act, "s_done", t, -1)
                nc.scalar.activation(QT[:].rearrange("p h t -> p (h t)"), flat_pair(pair[0]), ACT.Copy).then_inc(s["qt_ready"], 1)

            def take_keys_turned(t):
                if not t.live:
                    return
                wait(act, "tk_done", t)
                wait(act, "s_done", t, -1)
                at = WIN + 128 * t.par
                nc.scalar.activation(KT[:, :, at:at + 128], pair[2][:].rearrange("p a (h t) -> p (a h) t", t=128), ACT.Copy)\
                    .then_inc(s["kt_ready"], 1)

            def exponentials(t):
                if not t.live:
                    return
                wait(act, "sc_ready", t)
                wait(act, "pt_done", t, -1)
                wait(act, "den_ready", t, -1)
                for odd in range(2):
                    ins = nc.scalar.activation(P[:, :, odd, :], sc[:, odd, :, :], ACT.Exp, scale=8.0)
                ins.then_inc(s["p_ready"], 1)

            def take_values(t, w):
                if not t.live:
                    return
                wait(act, f"v{w}_done", t)
                if w == 2:
                    wait(act, "pv_done", t, -1)
                nc.scalar.activation(VP[:, w, :], v_bank[w], ACT.Copy).then_inc(s[f"vp{w}_ready"], 1)

            def take_probabilities_turned(t):
                if not t.live:
                    return
                wait(act, "pt_done", t)
                wait(act, "pv_done", t, -1)
                nc.scalar.activation(PT[:].rearrange("p h t -> p (h t)"), flat_pair(pair[1]), ACT.Copy).then_inc(s["pt_ready"], 1)

            def take_attention_turned(t):
                if not t.live:
                    return
                wait(act, "ot_done", t)
                wait(act, "proj_done", t, -1)
                nc.scalar.activation(OT[:].rearrange("p h t -> p (h t)"), flat_pair(pair[2]), ACT.Copy).then_inc(s["ot_ready"], 1)

            def deviation(t):
                if not t.live:
                    return
                nc.scalar.activation(preload[:, 0:1], eps[:], ACT.Sqrt).then_inc(s["sqrt_loaded"], 1)
                wait(act, "var_done", t)
                wait(act, "rstd_ready", t, -1)
                nc.scalar.activation(std[:], b0[:, 0:128], ACT.Sqrt, bias=eps[:, 0:1]).then_inc(s["std_ready"], 1)

            def gate(t):
                if not t.live:
                    return
                if t.first:
                    act.wait_ge(s["vecs_in"], 16 * t.l + 16)
                nc.scalar.activation(preload[:, 1:2], eps[:], ACT.Gelu).then_inc(s["gelu_loaded"], 1)
                wait(act, "upg_done", t)
                wait(act, "h_ready", t, -1, HCH)
                for c in range(HCH):
                    r = HROWS[c]
                    nc.scalar.activation(G[0:r, c, :], b7[0:r, 128 * c:128 * c + 128], ACT.Gelu,
                                         bias=vecs[0:r, 5 + c:6 + c]).then_inc(s["g_ready"], 1)

            def slot(tile):
                take_probabilities_turned(tile(3))
                deviation(tile(4))
                take(tile(1), 1, k_pair, "k")
                take_values(tile(2), 2)
                take_queries_turned(tile(2))
                take(tile(1), 0, q_pair, "q")
                take_attention_turned(tile(3))
                lengths(tile(1))
                gate(tile(4))
                take_values(tile(2), 0)
                exponentials(tile(2))
                take_values(tile(2), 1)
                take_values(tile(2), 3)
                take_keys_turned(tile(1))

            run(act, slot)

        @block.gpsimd
        def _(pool):
            nc.gpsimd.memset(eps[:], 1e-5).then_inc(s["memset_done"], 1)
            nc.gpsimd.memset(mean_w[:], 1.0 / 128).then_inc(s["memset_done"], 1)
            nc.gpsimd.memset(KT[:, :, 0:WIN], 0.0).then_inc(s["memset_done"], 1)
            nc.gpsimd.memset(X[:, :, 0:PAD], 0.0).then_inc(s["memset_done"], 1)
            nc.gpsimd.memset(XM[:, :, 0:PAD], 0.0).then_inc(s["memset_done"], 1)
            pool.wait_ge(s["memset_done"], 5)

            def two_halves(t, target, source, shift_of, ready):
                for half in range(2):
                    if half:
                        wait(pool, ready, t, per=2, part=1)
                    pool.sem_inc(s["gate_pool"], 1)
                    rows = slice(64 * half, 64 * half + 64)
                    nc.gpsimd.tensor_copy(target[rows], columns(source, t, shift_of, half)[rows]).then_inc(s[ready], 1)

            def shifted_input(t):
                if not t.live:
                    return
                if not (isinstance(t.l, int) and t.l == 0):
                    wait(pool, "x_ready", t, -32)
                wait(pool, "v3_done", t, -2)
                if isinstance(t.k, int) and t.k == 1:
                    wait(pool, "rsq_ready", t, -1)
                elif isinstance(t.k, int) and t.k == 2:
                    wait(pool, "sc_ready", t, -2)
                else:
                    wait(pool, "xs2_ready", t, -3, 2)
                two_halves(t, xs[:, t.par, :], X, WIN, "xs_ready")

            def squares(t):
                if not t.live:
                    return
                wait(pool, "xs_ready", t, 3, 2)
                wait(pool, "xc_ready", t)
                wait(pool, "var_done", t, -1)
                nc.gpsimd.tensor_tensor(xsq[:], xc[:], xc[:], ALU.mult).then_inc(s["xsq_ready"], 1)

            def sine_part(t, half, qk):
                if not t.live:
                    return
                wait(pool, f"raw{qk}_ready", t)
                if t.first:
                    pool.wait_ge(s[f"tables_{qk}"], 4 * t.l + 4)
                wait(pool, f"add{qk}_ready", t, -1, 2)
                nc.gpsimd.tensor_tensor(by_head(rs, half), by_head(raw, half),
                                        rot[:, t.par, half, 1, :].unsqueeze(1).to_broadcast([128, HEADS, DH]), ALU.mult)\
                    .then_inc(s[f"rs{qk}_ready"], 1)

            def centred_scores(t):
                if not t.live:
                    return
                wait(pool, "mx_ready", t)
                wait(pool, "p_ready", t, -1)
                nc.gpsimd.tensor_tensor(sc[:].rearrange("p a h n -> p (a h) n"), sm[:].rearrange("p a h n -> p (a h) n"),
                                        mx[:].unsqueeze(2).to_broadcast([128, HEADS, DH]), ALU.subtract)\
                    .then_inc(s["sc_ready"], 1)

            def shifted_middle(t):
                if not t.live:
                    return
                wait(pool, "xm_ready", t)
                wait(pool, "xc_ready", t, -1)
                if isinstance(t.k, int) and t.k == TILES - 1:
                    wait(pool, "xsq_ready", t, -1)
                else:
                    wait(pool, "sc_ready", t, 1)
                two_halves(t, xs2, XM, 0, "xs2_ready")

            def slot(tile):
                squares(tile(4))
                sine_part(tile(1), 1, "k")
                sine_part(tile(1), 0, "q")
                centred_scores(tile(2))
                shifted_middle(tile(3))
                shifted_input(tile(0))

            run(pool, slot)

        @block.vector
        def _(dve):
            dve.wait_ge(s["consts_in"], 48)
            dve.wait_ge(s["memset_done"], 5)

            def tables(t, half, qk):
                dve.wait_ge(s["qks_in"], 16 * t.l + 16)
                wait(dve, f"rs{qk}_ready", t, -1)
                for par in range(2):
                    for cs in range(2):
                        nc.vector.tensor_tensor(rot[:, par, half, cs, :], rot_const[:, par, half, cs, :],
                                                qkscale[:, half, :], ALU.mult).then_inc(s[f"tables_{qk}"], 1)
                dve.wait_ge(s[f"tables_{qk}"], 4 * t.l + 4)

            def cut(target, source):
                return nc.vector.tensor_scalar(target.bitcast(U32), source.bitcast(U32), 0xFFFFF000, None, ALU.bitwise_and)

            def split_weights(t, chunks):
                if not (t.live and t.first):
                    return
                wait(dve, "qkq_done", t, -1)
                for c in chunks:
                    half, first = W_CHUNKS[c]
                    cols = slice(INNER * half + first, INNER * half + first + 512)
                    dve.wait_ge(s[f"w_in{c % 2}"], 32 * t.l + 16 * (c // 2) + 16)
                    if c or not isinstance(t.l, int):
                        dve.wait_ge(s["w_split"], 4 * t.l + c)
                    cut(W_cut[:], W_whole[:, c % 2, :]).then_inc(s["w_cut"], 1)
                    dve.wait_ge(s["w_cut"], 4 * t.l + c + 1)
                    nc.vector.tensor_copy(Wqk_high[:, cols], W_cut[:]).then_inc(s["w_high"], 1)
                    nc.vector.tensor_tensor(Wqk_low[:, cols], W_whole[:, c % 2, :], W_cut[:], ALU.subtract)\
                        .then_inc(s["w_split"], 1)

            def split_input(t):
                if not t.live:
                    return
                wait(dve, "xs_ready", t, per=2)
                wait(dve, "qkq_done", t, -1)
                cut(xs_cut[:], xs[:, t.par, WIN:]).then_inc(s["xs_cut"], 1)
                wait(dve, "xs_cut", t)
                nc.vector.tensor_copy(xs_high[:], xs_cut[:]).then_inc(s["xs_high"], 1)
                nc.vector.tensor_tensor(xs_low[:], xs[:, t.par, WIN:], xs_cut[:], ALU.subtract).then_inc(s["xs_split"], 1)

            def cosine_part(t, half, qk):
                if not t.live:
                    return
                wait(dve, f"raw{qk}_ready", t)
                wait(dve, f"t{qk}_done", t, -1)
                nc.vector.tensor_tensor(by_head(rc, half), by_head(raw, half),
                                        rot[:, t.par, half, 0, :].unsqueeze(1).to_broadcast([128, HEADS, DH]), ALU.mult)\
                    .then_inc(s[f"rc{qk}_ready"], 1)

            def add_sine_part(t, half, qk):
                if not t.live:
                    return
                wait(dve, f"rc{qk}_ready", t)
                wait(dve, f"rs{qk}_ready", t)
                halves = lambda flat: flat[:, INNER * half:INNER * half + INNER].rearrange("p (h a d) -> p h a d", a=2, d=DH // 2)
                for a in range(2):
                    nc.vector.tensor_tensor(halves(rc)[:, :, a, :], halves(rc)[:, :, a, :], halves(rs)[:, :, 1 - a, :], ALU.add)\
                        .then_inc(s[f"add{qk}_ready"], 1)

            def unit_length(t, half, qk):
                if not t.live:
                    return
                wait(dve, "inv_ready", t)
                wait(dve, f"add{qk}_ready", t, 0, 2)
                nc.vector.tensor_tensor(by_head(rc, half), by_head(rc, half),
                                        inv[:, half, :].unsqueeze(2).to_broadcast([128, HEADS, DH]), ALU.mult)\
                    .then_inc(s[f"fin{qk}_ready"], 1)

            def squared_lengths(t, half, qk):
                if not t.live:
                    return
                wait(dve, f"sq{qk}_ready", t)
                nc.vector.tensor_reduce(ss[:, half, :], sq[:, half, :].rearrange("p (h d) -> p h d", d=DH), AX_X, ALU.add)\
                    .then_inc(s[f"ss{qk}_ready"], 1)

            def inverse_lengths(t):
                if not t.live:
                    return
                wait(dve, "len_ready", t)
                nc.vector.tensor_scalar(norm[:], length[:], 1e-12, None, ALU.max).then_inc(s["norm_ready"], 1)
                wait(dve, "norm_ready", t)
                nc.vector.reciprocal(inv[:], norm[:]).then_inc(s["inv_ready"], 1)

            def mask_scores(t):
                if not t.live:
                    return
                wait(dve, "s_done", t)
                wait(dve, "sc_ready", t, -1)
                nc.vector.tensor_tensor(sm[:].rearrange("p a h n -> p (a h) n"), pair[0][:].rearrange("p a (h n) -> p (a h) n", n=DH),
                                        mask[:, t.par, :].unsqueeze(1).to_broadcast([128, HEADS, DH]), ALU.add)\
                    .then_inc(s["sm_ready"], 1)

            def row_maxima(t):
                if not t.live:
                    return
                wait(dve, "sm_ready", t)
                nc.vector.tensor_reduce(mx[:], sm[:].rearrange("p a h n -> p (a h) n"), AX_X, ALU.max).then_inc(s["mx_ready"], 1)

            def denominators(t):
                if not t.live:
                    return
                wait(dve, "p_ready", t)
                nc.vector.tensor_reduce(den[:], P[:].rearrange("p h a d -> p (h a) d"), AX_X, ALU.add).then_inc(s["den_ready"], 1)
                wait(dve, "den_ready", t)
                nc.vector.reciprocal(rden[:], den[:]).then_inc(s["rden_ready"], 1)

            def normalised_attention(t):
                if not t.live:
                    return
                wait(dve, "pv_done", t)
                wait(dve, "rden_ready", t)
                wait(dve, "ot_done", t, -1)
                nc.vector.tensor_tensor(On[:].rearrange("p h a d -> p a h d"), pair[1][:].rearrange("p a (h d) -> p a h d", d=DH),
                                        rden[:].rearrange("p (h a) -> p a h", a=2).unsqueeze(3).to_broadcast([128, 2, HP, DH]),
                                        ALU.mult).then_inc(s["on_ready"], 1)

            def add_attention(t):
                if not t.live:
                    return
                wait(dve, "proj_done", t)
                nc.vector.tensor_tensor(columns(XM, t), columns(X, t), b3[:, 0:128], ALU.add).then_inc(s["xm_ready"], 1)

            def centred(t):
                if not t.live:
                    return
                wait(dve, "mean_done", t)
                wait(dve, "xh_ready", t, -1)
                nc.vector.tensor_tensor(xc[:], xs2[:], b6[:, 0:128], ALU.subtract).then_inc(s["xc_ready"], 1)

            def layernorm(t):
                if not t.live:
                    return
                wait(dve, "std_ready", t)
                nc.vector.reciprocal(rstd[:], std[:]).then_inc(s["rstd_ready"], 1)
                wait(dve, "rstd_ready", t)
                nc.vector.tensor_tensor(xh[:], xc[:], rstd[:], ALU.mult).then_inc(s["xh_ready"], 1)
                wait(dve, "xh_ready", t)
                if t.first:
                    dve.wait_ge(s["vecs_in"], 16 * t.l + 16)
                wait(dve, "upg_done", t, -1)
                nc.vector.tensor_scalar(xn[:], xh[:], vecs[:, 0:1], vecs[:, 1:2], ALU.mult, ALU.add).then_inc(s["xn_ready"], 1)

            def gated(t):
                if not t.live:
                    return
                wait(dve, "upa_done", t)
                wait(dve, "down_done", t, -1)
                for c in range(HCH):
                    r = HROWS[c]
                    wait(dve, "g_ready", t, 0, HCH, c + 1)
                    nc.vector.scalar_tensor_tensor(H[0:r, c, :], b6[0:r, 128 * c:128 * c + 128], vecs[0:r, 2 + c:3 + c],
                                                   G[0:r, c, :], ALU.add, ALU.mult).then_inc(s["h_ready"], 1)

            def add_feed_forward(t):
                if not t.live:
                    return
                wait(dve, "down_done", t)
                wait(dve, "xm_ready", t)
                nc.vector.scalar_tensor_tensor(columns(X, t), b0[:, 0:128], vecs[:, 8:9], columns(XM, t), ALU.add, ALU.add)\
                    .then_inc(s["x_ready"], 1)

            def slot(tile):
                unit_length(tile(2), 0, "q")
                layernorm(tile(4))
                if tile(1).live and tile(1).first:
                    tables(tile(1), 0, "q")
                    tables(tile(1), 1, "k")
                cosine_part(tile(1), 1, "k")
                normalised_attention(tile(3))
                squared_lengths(tile(1), 1, "k")
                squared_lengths(tile(1), 0, "q")
                add_sine_part(tile(1), 1, "k")
                mask_scores(tile(2))
                inverse_lengths(tile(1))
                row_maxima(tile(2))
                gated(tile(4))
                split_weights(tile(0), (0, 1))
                add_attention(tile(3))
                unit_length(tile(1), 1, "k")
                cosine_part(tile(1), 0, "q")
                add_feed_forward(tile(4))
                centred(tile(3))
                add_sine_part(tile(1), 0, "q")
                split_input(tile(0))
                denominators(tile(2))
                split_weights(tile(0), (2, 3))

            run(dve, slot)


def constants():
    half = np.arange(0, DH, 2, dtype=np.float32)
    inv_freq = (np.float32(1.0) / np.float32(10000.0) ** (half / np.float32(DH))).astype(np.float32)
    t = np.arange(T, dtype=np.float32)
    freqs = t[:, None] * inv_freq[None, :]
    freqs = np.concatenate([freqs, freqs], -1)
    base = (half + np.float32(0.4 * DH)) / np.float32(1.4 * DH)
    power = (t - T // 2) / np.float32(WIN // 2)
    scale = base[None, :] ** power[:, None]
    scale = np.concatenate([scale, scale], -1).astype(np.float32)
    cos, sin = np.cos(freqs), np.sin(freqs)
    sign = np.where(np.arange(DH) < DH // 2, 1.0, -1.0).astype(np.float32)
    rotary = np.zeros((128, 2, 2, 2, DH), np.float32)
    for par in range(2):
        rows = slice(128 * par, 128 * par + 128)
        for half_, s in ((0, scale), (1, np.float32(1.0) / scale)):
            rotary[:, par, half_, 0] = cos[rows] * s[rows]
            rotary[:, par, half_, 1] = sin[rows] * sign * s[rows]
    query = np.arange(128)[:, None] % WIN
    slot = np.arange(2 * WIN)[None, :]
    seen = (slot >= query) & (slot <= query + WIN)
    first = seen & ((np.arange(128)[:, None] >= WIN) | (slot >= WIN))
    mask = np.where(np.stack([first, seen], 1), 0.0, -1e30).astype(np.float32)
    return {"ident": np.eye(128, dtype=np.float32), "rotary": rotary, "window_mask": mask}


def layouts_d(i):
    a = lambda n: np.asarray(i["L1_ffn_" + n])
    out = {"Wqkv": a("Wqkv").reshape(LAYERS, D, 3, INNER)}
    out["Wv"] = np.ascontiguousarray(a("Wqkv").reshape(LAYERS, D, 3, HP, 2, DH)[:, :, 2].transpose(0, 1, 3, 2, 4)
                                     ).reshape(LAYERS, D, 2, HEAD_COLS)
    out["qk_scale"] = np.stack([a("q_scale"), a("k_scale")], 1)
    out["Wo"] = a("Wo")
    out["W1"] = a("W1")
    w2 = np.zeros((LAYERS, HCH * 128, D), np.float32)
    w2[:, :HID] = a("W2")
    out["W2"] = np.ascontiguousarray(w2.reshape(LAYERS, HCH, 128, D).transpose(0, 2, 1, 3))
    b1 = np.zeros((LAYERS, 2, HCH * 128), np.float32)
    b1[:, :, :HID] = a("b1").reshape(LAYERS, 2, HID)
    cols = [a("ln_g"), a("ln_b")] + [b1[:, s, 128 * c:128 * c + 128] for s in range(2) for c in range(HCH)] + [a("b2")]
    out["vecs"] = np.stack(cols, 2)
    return out


def build(nc, dram, out):
    with ExitStack() as ctx:
        X = ctx.enter_context(nc.sbuf_tensor("X", [128, SEQS, STRIDE], F32))
        s_in = ctx.enter_context(nc.semaphore("x_in"))
        s_out = ctx.enter_context(nc.semaphore("x_out"))
        with nc.Block() as block:
            @block.sync
            def _(sp):
                sp.dma_start(X[:, :, PAD:], dram["x"].rearrange("d (b t) -> d b t", t=T)).then_inc(s_in, 16)
                sp.wait_ge(s_in, 16)
        causal_attention(nc, dram, X)
        fast_feedforward_block(nc, dram, X)
        X0 = ctx.enter_context(nc.sbuf_tensor("X0", [128, SEQS * T], F32))
        gated_scan(nc, dram, X, X0)
        with ExitStack() as inner:
            XM = inner.enter_context(nc.sbuf_tensor("XM", [128, SEQS, STRIDE], F32))
            local_attention_layers(nc, dram, X, XM)
        add_and_norm(nc, X, X0, None, "o")
        with nc.Block() as block:
            @block.sync
            def _(sp):
                sp.dma_start(out.rearrange("d (b t) -> d b t", t=T), X[:, :, PAD:]).then_inc(s_out, 16)
                sp.wait_ge(s_out, 16)


def kernel(**inputs):
    import concourse.bacc as _bacc
    from concourse.bass_utils import run_bass_kernel_spmd as _run

    nc = _bacc.Bacc("TRN2", target_bir_lowering=False, num_devices=1)
    arrays = {"x": np.asarray(inputs["L0_attn_x"]).reshape(SEQS * T, D).T}
    for part in (constants(), constants_a(), constants_b(), layouts_a(inputs), layouts_b(inputs), layouts_c(inputs),
                 layouts_d(inputs)):
        arrays.update(part)
    dram = {}
    for name, a in arrays.items():
        arrays[name] = a = np.ascontiguousarray(a)
        dram[name] = nc.dram_tensor(name + "_dram", a.shape, mybir.dt.from_np(a.dtype), kind="ExternalInput").ap()
    out = nc.dram_tensor("out_dram", (D, SEQS * T), F32, kind="ExternalOutput").ap()
    build(nc, dram, out)
    r = _run(nc, [{name + "_dram": a for name, a in arrays.items()}], core_ids=[0])
    return np.ascontiguousarray(r.results[0]["out_dram"].T).reshape(SEQS, T, D)
```
